# Optimizing a Trainium2 kernel written in Bass

```python
import numpy as np
import jax
import jax.numpy as jnp

def _softmax(x, axis=-1):
    return jax.nn.softmax(x, axis=axis)

def _gelu(x):
    return jax.nn.gelu(x, approximate=True)

def _silu(x):
    return jax.nn.silu(x)

def _sigmoid(x):
    return jax.nn.sigmoid(x)

def _layernorm(x, axis=-1, eps=1e-05):
    m = jnp.mean(x, axis=axis, keepdims=True)
    v = jnp.var(x, axis=axis, keepdims=True)
    return (x - m) / jnp.sqrt(v + eps)

def _scatter_add(tgt, idx, src, axis=0):
    return tgt.at[idx].add(src)

def _segment_sum(src, seg, n):
    return jax.ops.segment_sum(src, seg, n)
kernel_name = 'mk_xattn_ffn_d1_seqx_r2_aa3513'

def setup_inputs(seed: int=0):
    np.random.seed(seed)
    _w = jnp.asarray

    def _rec_inputs():
        import jax
        import jax.numpy as jnp
        _rk = jax.random.key(seed)
        x = -0.0002928 + 1 * jax.random.normal(jax.random.fold_in(_rk, 1), (8, 512, 512), jnp.float32)
        _lenS = 512 - jax.random.randint(jax.random.fold_in(_rk, 7), (8,), 0, max(1, 512 // 4) + 1, jnp.int32)
        _lenS2 = 77 - jax.random.randint(jax.random.fold_in(_rk, 8), (8,), 0, max(1, 77 // 4) + 1, jnp.int32)
        _ctx_1024P = jax.random.normal(jax.random.fold_in(_rk, 11), (8, 16, 512), jnp.float32)
        _ctx_1024c = jax.random.dirichlet(jax.random.fold_in(_rk, 511), 0.3 * jnp.ones((16,), jnp.float32), (8, 77))
        _ctx_1024t = jnp.einsum('bsk,bkd->bsd', _ctx_1024c, _ctx_1024P)
        _ctx_1024t = _ctx_1024t * jax.lax.rsqrt(jnp.mean(jnp.square(_ctx_1024t)) + 1e-12) * 0.953939
        ctx_1024 = -1.39393e-06 + 0.999914 * (_ctx_1024t + 0.3 * jax.random.normal(jax.random.fold_in(_rk, 611), (8, 77, 512), jnp.float32))
        return (x, ctx_1024)
    x, ctx_1024 = _rec_inputs()

    def _L0_xattn_setup():
        import jax, jax.numpy as jnp
        import numpy as np
        from math import sqrt
        D_MODEL = 512
        N_HEADS = 16
        DK = D_MODEL // N_HEADS
        key = jax.random.key(seed)
        ks = jax.random.split(key, 11)
        B, L, S = (2, 1024, 1024)
        inp = {'queries': jax.random.normal(ks[0], (B, L, D_MODEL), jnp.float32), 'keys': jax.random.normal(ks[1], (B, S, D_MODEL), jnp.float32), 'values': jax.random.normal(ks[2], (B, S, D_MODEL), jnp.float32), 'Wq': jax.random.normal(ks[3], (D_MODEL, D_MODEL), jnp.float32) * 0.02, 'bq': jnp.zeros((D_MODEL,), jnp.float32), 'Wk': jax.random.normal(ks[4], (D_MODEL, D_MODEL), jnp.float32) * 0.02, 'bk': jnp.zeros((D_MODEL,), jnp.float32), 'Wv': jax.random.normal(ks[5], (D_MODEL, D_MODEL), jnp.float32) * 0.02, 'bv': jnp.zeros((D_MODEL,), jnp.float32), 'Wo': jax.random.normal(ks[6], (D_MODEL, D_MODEL), jnp.float32) * 0.02, 'bo': jnp.zeros((D_MODEL,), jnp.float32)}
        return inp
    _L0_xattn_all = _L0_xattn_setup()
    _L0_xattn_in = {k: v for k, v in _L0_xattn_all.items() if k in ('Wq', 'bq', 'Wk', 'bk', 'Wv', 'bv', 'Wo', 'bo')}
    del _L0_xattn_all

    def _L0_ffn_setup():
        import jax, jax.numpy as jnp
        import numpy as np
        NH, NKV, E, K = (16, 4, 8, 2)
        CAP_FACTOR = 1.25
        LN_EPS = 1e-05

        def _layer_norm(x, w, b):
            mu = jnp.mean(x, axis=-1, keepdims=True)
            var = jnp.mean(jnp.square(x - mu), axis=-1, keepdims=True)
            return (x - mu) * jax.lax.rsqrt(var + LN_EPS) * w + b
        key = jax.random.key(seed)
        ks = jax.random.split(key, 6)
        S, B, H, F = (1024, 1, 512, 1024)
        HD = H // NH
        qkv_out = NKV * (NH // NKV + 2) * HD
        f32 = jnp.float32
        return {'hidden_states': jax.random.normal(ks[0], (S, B, H), f32), 'ln1_weight': jnp.ones((H,), f32), 'ln1_bias': jnp.zeros((H,), f32), 'ln2_weight': jnp.ones((H,), f32), 'ln2_bias': jnp.zeros((H,), f32), 'qkv_weight': jax.random.normal(ks[1], (qkv_out, H), f32) * 0.02, 'proj_weight': jax.random.normal(ks[2], (H, H), f32) * 0.02, 'router_weight': jax.random.normal(ks[3], (H, E), f32) * 0.02, 'moe_w1': jax.random.normal(ks[4], (E, H, F), f32) * 0.02, 'moe_w2': jax.random.normal(ks[5], (F and E, F, H), f32)[:E] * 0.02 if False else jax.random.normal(ks[5], (E, F, H), f32) * 0.02}
    _L0_ffn_all = _L0_ffn_setup()
    _L0_ffn_in = {k: v for k, v in _L0_ffn_all.items() if k in ('ln1_weight', 'ln1_bias', 'ln2_weight', 'ln2_bias', 'qkv_weight', 'proj_weight', 'router_weight', 'moe_w1', 'moe_w2')}
    del _L0_ffn_all
    return {'x': x, 'ctx_1024': ctx_1024, 'L0_xattn_Wq': _L0_xattn_in['Wq'], 'L0_xattn_bq': _L0_xattn_in['bq'], 'L0_xattn_Wk': _L0_xattn_in['Wk'], 'L0_xattn_bk': _L0_xattn_in['bk'], 'L0_xattn_Wv': _L0_xattn_in['Wv'], 'L0_xattn_bv': _L0_xattn_in['bv'], 'L0_xattn_Wo': _L0_xattn_in['Wo'], 'L0_xattn_bo': _L0_xattn_in['bo'], 'L0_ffn_ln1_weight': _L0_ffn_in['ln1_weight'], 'L0_ffn_ln1_bias': _L0_ffn_in['ln1_bias'], 'L0_ffn_ln2_weight': _L0_ffn_in['ln2_weight'], 'L0_ffn_ln2_bias': _L0_ffn_in['ln2_bias'], 'L0_ffn_qkv_weight': _L0_ffn_in['qkv_weight'], 'L0_ffn_proj_weight': _L0_ffn_in['proj_weight'], 'L0_ffn_router_weight': _L0_ffn_in['router_weight'], 'L0_ffn_moe_w1': _L0_ffn_in['moe_w1'], 'L0_ffn_moe_w2': _L0_ffn_in['moe_w2']}

def reference(x, ctx_1024, L0_xattn_Wq, L0_xattn_bq, L0_xattn_Wk, L0_xattn_bk, L0_xattn_Wv, L0_xattn_bv, L0_xattn_Wo, L0_xattn_bo, L0_ffn_ln1_weight, L0_ffn_ln1_bias, L0_ffn_ln2_weight, L0_ffn_ln2_bias, L0_ffn_qkv_weight, L0_ffn_proj_weight, L0_ffn_router_weight, L0_ffn_moe_w1, L0_ffn_moe_w2):
    import jax
    import jax.numpy as jnp

    def _L0_xattn_ref(queries, keys, values, Wq, bq, Wk, bk, Wv, bv, Wo, bo):
        import jax, jax.numpy as jnp
        import numpy as np
        from math import sqrt
        D_MODEL = 512
        N_HEADS = 16
        DK = D_MODEL // N_HEADS
        B, L, _ = queries.shape
        S = values.shape[1]
        H, dk = (N_HEADS, DK)
        q = (queries @ Wq + bq).reshape(B, L, H, dk)
        k = (keys @ Wk + bk).reshape(B, S, H, dk)
        v = (values @ Wv + bv).reshape(B, S, H, dk)
        scale = 1.0 / sqrt(dk)
        scores = jnp.einsum('blhd,bshd->bhls', q, k)
        causal = jnp.triu(jnp.ones((L, S), dtype=bool), k=1)
        scores = jnp.where(causal[None, None], -jnp.inf, scores)
        attn = jax.nn.softmax(scores * scale, axis=-1)
        out = jnp.einsum('bhls,bshd->blhd', attn, v).reshape(B, L, H * dk)
        out = out @ Wo + bo
        return out

    def _L0_ffn_ref(hidden_states, ln1_weight, ln1_bias, ln2_weight, ln2_bias, qkv_weight, proj_weight, router_weight, moe_w1, moe_w2):
        import jax, jax.numpy as jnp
        import numpy as np
        NH, NKV, E, K = (16, 4, 8, 2)
        CAP_FACTOR = 1.25
        LN_EPS = 1e-05

        def _layer_norm(x, w, b):
            mu = jnp.mean(x, axis=-1, keepdims=True)
            var = jnp.mean(jnp.square(x - mu), axis=-1, keepdims=True)
            return (x - mu) * jax.lax.rsqrt(var + LN_EPS) * w + b
        S, B, H = hidden_states.shape
        HD = H // NH
        q_per_kv = NH // NKV
        ln1 = _layer_norm(hidden_states, ln1_weight, ln1_bias)
        qkv = jnp.einsum('sbh,oh->sbo', ln1, qkv_weight)
        qkv = qkv.reshape(S, B, NKV, (q_per_kv + 2) * HD)
        q = qkv[..., :q_per_kv * HD].reshape(S, B, NH, HD)
        k = qkv[..., q_per_kv * HD:(q_per_kv + 1) * HD]
        v = qkv[..., (q_per_kv + 1) * HD:]
        qb = jnp.transpose(q, (1, 2, 0, 3)).reshape(B, NKV, q_per_kv, S, HD)
        kb = jnp.transpose(k, (1, 2, 0, 3))
        vb = jnp.transpose(v, (1, 2, 0, 3))
        scale = 1.0 / np.sqrt(HD).astype(np.float32)
        scores = jnp.einsum('bgqsd,bgtd->bgqst', qb, kb) * scale
        causal = jnp.tril(jnp.ones((S, S), bool))
        scores = jnp.where(causal, scores, jnp.finfo(scores.dtype).min)
        attn = jax.nn.softmax(scores, axis=-1)
        ao = jnp.einsum('bgqst,bgtd->bgqsd', attn, vb)
        ao = ao.reshape(B, NH, S, HD)
        ao = jnp.transpose(ao, (2, 0, 1, 3)).reshape(S, B, H)
        proj = jnp.einsum('sbh,oh->sbo', ao, proj_weight)
        h1 = hidden_states + proj
        ln2 = _layer_norm(h1, ln2_weight, ln2_bias)
        x = ln2.reshape(-1, H)
        N = x.shape[0]
        logits = x @ router_weight
        probs = jax.nn.softmax(logits, axis=-1)
        top_p, top_i = jax.lax.top_k(probs, K)
        top_p = top_p / jnp.sum(top_p, axis=-1, keepdims=True)
        exp_idx = top_i.reshape(-1)
        exp_p = top_p.reshape(-1)
        order = jnp.argsort(exp_idx, stable=True)
        sorted_exp = exp_idx[order]
        counts = jnp.bincount(exp_idx, length=E)
        offsets = jnp.concatenate([jnp.zeros((1,), counts.dtype), jnp.cumsum(counts)[:-1]])
        within = jnp.arange(N * K) - offsets[sorted_exp]
        cap = int(np.ceil(N * K / E * CAP_FACTOR))
        T = E * cap
        valid = within < cap
        dst = jnp.where(valid, sorted_exp * cap + within, T)
        padded_tokens = jnp.zeros((T, H), x.dtype).at[dst].set(x[order // K], mode='drop')
        padded_probs = jnp.zeros((T,), exp_p.dtype).at[dst].set(exp_p[order], mode='drop')
        padded_tid = jnp.zeros((T,), jnp.int32).at[dst].set((order // K).astype(jnp.int32), mode='drop')
        xt = padded_tokens.reshape(E, cap, H)
        fc1 = jax.nn.gelu(jnp.einsum('ech,ehf->ecf', xt, moe_w1))
        fc2 = jnp.einsum('ecf,efh->ech', fc1, moe_w2).reshape(T, H)
        weighted = fc2 * padded_probs[:, None]
        moe_out = jnp.zeros((N, H), hidden_states.dtype).at[padded_tid].add(weighted)
        return h1 + moe_out.reshape(S, B, H)
    x = x + _L0_xattn_ref(_layernorm(x, axis=-1), ctx_1024, ctx_1024, L0_xattn_Wq, L0_xattn_bq, L0_xattn_Wk, L0_xattn_bk, L0_xattn_Wv, L0_xattn_bv, L0_xattn_Wo, L0_xattn_bo)
    x = x + _L0_ffn_ref(_layernorm(x, axis=-1), L0_ffn_ln1_weight, L0_ffn_ln1_bias, L0_ffn_ln2_weight, L0_ffn_ln2_bias, L0_ffn_qkv_weight, L0_ffn_proj_weight, L0_ffn_router_weight, L0_ffn_moe_w1, L0_ffn_moe_w2)
    return x

_drawn_inputs = setup_inputs


def setup_inputs(seed=0):
    import zlib

    import numpy as np

    out = dict(_drawn_inputs(seed))
    spreads = {'L0_xattn_bq': (0.0, 0.8),
     'L0_xattn_bk': (0.0, 0.8),
     'L0_xattn_bv': (0.0, 0.1),
     'L0_xattn_bo': (0.0, 0.1),
     'L0_ffn_ln1_weight': (1.0, 0.6),
     'L0_ffn_ln1_bias': (0.0, 0.575),
     'L0_ffn_ln2_weight': (1.0, 0.546),
     'L0_ffn_ln2_bias': (0.0, 0.329)}
    factors = {'L0_xattn_Wq': 6.078, 'L0_xattn_Wk': 5.997}
    for name, (base, spread) in spreads.items():
        noise = np.random.default_rng([zlib.crc32(name.encode()), seed]).standard_normal(out[name].shape)
        drawn = base * np.exp(spread * noise) if base else spread * noise
        out[name] = jnp.asarray(drawn.astype(out[name].dtype))
    for name, factor in factors.items():
        out[name] = (out[name] * factor).astype(out[name].dtype)
    return out
```

```python
from contextlib import ExitStack

import concourse.bass as bass
from concourse import mybir

F32 = mybir.dt.float32
F32R = mybir.dt.float32r
I32 = mybir.dt.int32
ALU = mybir.AluOpType
ACT = mybir.ActivationFunctionType
X = mybir.AxisListType.X

P = 128
S = 8
L = 512
D = 512
KT = D // P
H = 16
DH = D // H
SK = 77
NKV = 4
HQ = H // NKV
QKV = D + 2 * NKV * DH
NC = L // P
NT = S * NC
N = S * L
E = 8
F = 1024
FT = F // P
CAP = 1280
BPE = CAP // P
NBLK = E * BPE
GB = 2
GPE = BPE // GB
NG = E * GPE
EPS = 1e-5
SCALE = float(DH) ** -0.5
MASKED = -1e30
HUGE = -3e38


class At:

    def __init__(self, c, off, period=8):
        self.c, self.off, self.period = c, off, period
        self.s = off % period
        self.chunk = c + off // period

    def count(self, k, i=0):
        if isinstance(self.c, int):
            return k * (self.period * self.c + self.off) + i
        return self.c * (k * self.period) + (k * self.off + i)

    def turns(self, ring, k=16, i=0):
        return (self.c * (k * (self.period // ring))) + (k * (self.off // ring) + i)

    def within(self, n):
        return not isinstance(self.c, int) or 0 <= self.period * self.c + self.off < n


def need(engine, sem, value):
    if not isinstance(value, int) or value > 0:
        engine.wait_ge(sem, value)


def need_apart(engine, *waits):
    waits = [(sem, v if isinstance(v, int) else engine.to_reg(v)) for sem, v in waits]
    if not all(isinstance(v, int) for _, v in waits):
        engine.wait_ge(waits[0][0], 1)
    for sem, v in waits:
        need(engine, sem, v)


def bc(ap, axis, shape):
    return ap.unsqueeze(axis).to_broadcast(shape)


def build(nc, a, out):
    x2d = a["x"].rearrange("b l d -> (b l) d")
    out2d = out.rearrange("b l d -> (b l) d")
    z2d = nc.dram_tensor("normed_tokens", [N, D], F32, kind="Internal").ap()

    whole = ExitStack()
    with whole:
        def sem(name):
            return whole.enter_context(nc.semaphore(name))

        def keeper(stack):
            def sb(name, shape, dt=F32):
                return stack.enter_context(nc.sbuf_tensor(name, shape, dt))
            return sb

        sb = keeper(whole)
        ident = sb("ident", [P, P])
        logits = sb("logits", [P, NT, E])
        ln2w = sb("ln2w", [P, KT])
        ln2b = sb("ln2b", [P, KT])
        main = ExitStack()
        with main:
            build_main(nc, a, x2d, out2d, z2d, ident, logits, ln2w, ln2b, keeper(main), sem)
        tables = {
            "rows": sb("rows", [P, NBLK], I32),
                "shares": sb("shares", [P, NBLK]),
        }
        routing = ExitStack()
        with routing:
            build_routing(nc, logits, tables, keeper(routing), sem)
        experts = ExitStack()
        with experts:
            build_experts(nc, a, out2d, z2d, ident, ln2w, ln2b, tables, keeper(experts), sem)



JOBS = ([("z2t", 8, 0), ("xt", 1, 0), ("ot", 4, 0), ("zt", 5, 0), ("at", 7, 0), ("q", 2, 0), ("q", 2, 1)]
        + [("pt", 3, i) for i in range(4)]
        + [("lg", 8, 0), ("wo", 4, 0), ("qkv", 5, 0), ("qkv", 5, 1), ("pj", 7, 0), ("pv", 3, 0), ("pv", 3, 1)])
RING = 4


def job_places():
    places, order = {}, []
    for s in range(8):
        for job in JOBS:
            if job[0] == "q" and s % 2:
                continue
            places[s, job[0], job[2]] = len(order)
            order.append((s, job))
    assert len(order) % RING == 0
    return places, order


def build_main(nc, a, x2d, out2d, z2d, ident, logits, ln2w, ln2b, sb, sem):
    wq = [sb("wq_hi", [P, KT, D], F32R), sb("wq_lo", [P, KT, D], F32R)]
    wo = [sb("wo_hi", [P, KT, D], F32R), sb("wo_lo", [P, KT, D], F32R)]
    wqkv = [sb("wqkv_hi", [P, KT, QKV], F32R), sb("wqkv_lo", [P, KT, QKV], F32R)]
    wpj = [sb("wpj_hi", [P, KT, D], F32R), sb("wpj_lo", [P, KT, D], F32R)]
    wr = sb("wr", [P, KT, E])
    kT = sb("kT", [P, KT, S * SK])
    va = sb("va", [SK, S, H, DH + 1])
    bq = sb("bq", [P, KT])
    bk = sb("bk", [P, KT])
    ln1w = sb("ln1w", [P, KT])
    ln1b = sb("ln1b", [P, KT])
    bo = sb("bo", [P, D])
    mask = sb("mask", [P, NC, SK])
    expo = sb("expo", [P, 1])

    with ExitStack() as st:
        def tmp(name, shape, dt=F32):
            return st.enter_context(nc.sbuf_tensor(name, shape, dt))

        rq = tmp("rq", [P, KT, D])
        ro = tmp("ro", [P, KT, D])
        rqkv = tmp("rqkv", [P, 6, D])
        rpj = tmp("rpj", [P, KT, D])
        rk = tmp("rk", [P, KT, D])
        rv = tmp("rv", [P, KT, D])
        cx = tmp("cx", [SK, S, D])
        cT = tmp("cT", [P, KT, S * SK])
        bv = tmp("bv", [SK, D])
        ps = st.enter_context(nc.psum_tensor("setup_ps", [P, 8, 512], F32))
        ctx_in, wk_in, wv_in, qkv_in, pj_in, wq_in, wo_in, small_in = (
            sem(n) for n in ("ctx_in", "wk_in", "wv_in", "qkv_in", "pj_in", "wq_in", "wo_in", "small_in"))
        made, mm_done, hi_done, evac = (sem(n) for n in ("consts_made", "setup_mm", "setup_hi", "setup_evac"))
        split_hi = sem("setup_split_hi")

        jobs = ([("ctx", b, 0) for b in range(S)] + [("k", m, h) for m in range(KT) for h in range(2)]
                + [("v", b, 0) for b in range(S)] + [("qkv", k, h) for k in range(KT) for h in range(2)]
                + [("pj", k, 0) for k in range(KT)])
        HC = S * SK // 2
        SMALL = 9
        block = st.enter_context(nc.Block())

        @block.sync
        def _(sp):
            sp.dma_start(cx[:, :, :], a["ctx_1024"].rearrange("b s d -> s b d")).then_inc(ctx_in, 16)
            sp.dma_start(rk[:, :, :], a["L0_xattn_Wk"].rearrange("(k p) n -> p k n", p=P)).then_inc(wk_in, 16)
            sp.dma_start(rv[:, :, :], a["L0_xattn_Wv"].rearrange("(k p) n -> p k n", p=P)).then_inc(wv_in, 16)
            by_group = a["L0_ffn_qkv_weight"].rearrange("(g r) h -> r g h", g=NKV)
            sp.dma_start(rqkv[:, 0:4, :], by_group[0:P, :, :]).then_inc(qkv_in, 16)
            for g in range(NKV):
                rows = slice(g * DH, (g + 1) * DH)
                sp.dma_start(rqkv[rows, 4, :], by_group[P:P + DH, g, :]).then_inc(qkv_in, 16)
                sp.dma_start(rqkv[rows, 5, :], by_group[P + DH:P + 2 * DH, g, :]).then_inc(qkv_in, 16)
            sp.dma_start(rpj[:, :, :], a["L0_ffn_proj_weight"].rearrange("(m p) h -> p m h", p=P)).then_inc(pj_in, 16)
            sp.dma_start(rq[:, :, :], a["L0_xattn_Wq"].rearrange("(k p) n -> p k n", p=P)).then_inc(wq_in, 16)
            sp.dma_start(ro[:, :, :], a["L0_xattn_Wo"].rearrange("(k p) n -> p k n", p=P)).then_inc(wo_in, 16)

        @block.gpsimd
        def _(pool):
            pool.memset(ident[:, :], 0.0).then_inc(made, 1)
            pool.memset(mask[:, :, :], 0.0).then_inc(made, 1)
            pool.memset(expo[:, :], -0.5).then_inc(made, 1)
            pool.memset(va[:, :, :, DH:DH + 1], 1.0).then_inc(made, 1)
            pool.wait_ge(made, 4)
            pool.affine_select(out=ident[:, :], in_=ident[:, :], compare_op=ALU.not_equal, fill=1.0, base=0,
                               pattern=[[-1, P]], channel_multiplier=1).then_inc(made, 1)
            pool.affine_select(out=mask[:, 0, :], in_=mask[:, 0, :], compare_op=ALU.is_ge, fill=MASKED, base=0,
                               pattern=[[-1, SK]], channel_multiplier=1).then_inc(made, 1)

        @block.scalar
        def _(act):
            with nc.allow_non_contiguous_dma(reason="512 words of a bias as columns"):
                for dst, name in ((bq, "L0_xattn_bq"), (bk, "L0_xattn_bk"), (ln1w, "L0_ffn_ln1_weight"),
                                  (ln1b, "L0_ffn_ln1_bias"), (ln2w, "L0_ffn_ln2_weight"),
                                  (ln2b, "L0_ffn_ln2_bias")):
                    act.dma_start(dst[:, :], a[name].rearrange("(k p) -> p k", p=P)).then_inc(small_in, 16)
            act.dma_start(bv[:, :], a["L0_xattn_bv"].partition_broadcast(SK)).then_inc(small_in, 16)
            act.dma_start(bo[:, :], a["L0_xattn_bo"].partition_broadcast(P)).then_inc(small_in, 16)
            act.dma_start(wr[:, :, :], a["L0_ffn_router_weight"].rearrange("(k p) e -> p k e", p=P))\
               .then_inc(small_in, 16)
            act.wait_ge(wq_in, 16)
            act.activation(wq[0][:, :, :], rq[:, :, :], ACT.Copy).then_inc(split_hi, 1)
            act.wait_ge(wo_in, 16)
            act.activation(wo[0][:, :, :], ro[:, :, :], ACT.Copy).then_inc(split_hi, 1)
            for n, (kind, i, h) in enumerate(jobs):
                if kind in ("qkv", "pj"):
                    act.wait_ge(mm_done, n + 1)
                    w, c0, c1 = (wpj, 0, D) if kind == "pj" else (wqkv, 512 * h, 512 if h == 0 else QKV)
                    act.activation(w[0][:, i, c0:c1], ps[:, n % 8, 0:c1 - c0], ACT.Copy).then_inc(hi_done, 1)

        @block.vector
        def _(dve):
            dve.wait_ge(small_in, 16 * SMALL)
            halves = 0
            for n, (kind, i, h) in enumerate(jobs):
                dve.wait_ge(mm_done, n + 1)
                if kind == "ctx":
                    dve.tensor_copy(cT[:, :, i * SK:(i + 1) * SK],
                                    ps[:, n % 8, 0:KT * SK].rearrange("p (k s) -> p k s", k=KT)).then_inc(evac, 1)
                elif kind == "k":
                    dve.tensor_scalar(kT[:, i, h * HC:(h + 1) * HC], ps[:, n % 8, 0:HC], bk[:, i:i + 1], None,
                                      ALU.add).then_inc(evac, 1)
                elif kind == "v":
                    dve.tensor_tensor(va[:, i, :, 0:DH], ps[0:SK, n % 8, :].rearrange("p (h d) -> p h d", h=H),
                                      bv[:, :].rearrange("p (h d) -> p h d", h=H), ALU.add).then_inc(evac, 1)
                else:
                    halves += 1
                    dve.wait_ge(hi_done, halves)
                    w, c0, c1 = (wpj, 0, D) if kind == "pj" else (wqkv, 512 * h, 512 if h == 0 else QKV)
                    dve.tensor_tensor(w[1][:, i, c0:c1], ps[:, n % 8, 0:c1 - c0],
                                      w[0][:, i, c0:c1].bitcast(F32), ALU.subtract).then_inc(evac, 1)
            dve.wait_ge(split_hi, 2)
            dve.tensor_tensor(wq[1][:, :, :], rq[:, :, :], wq[0][:, :, :].bitcast(F32), ALU.subtract)
            dve.tensor_tensor(wo[1][:, :, :], ro[:, :, :], wo[0][:, :, :].bitcast(F32), ALU.subtract)

        @block.tensor
        def _(pe):
            pe.wait_ge(made, 6)
            for n, (kind, i, h) in enumerate(jobs):
                need(pe, evac, n - 7)
                bank = ps[:, n % 8, :]
                if kind == "ctx":
                    if n == 0:
                        pe.wait_ge(ctx_in, 16)
                    for k in range(KT):
                        last = pe.transpose(bank[:, k * SK:(k + 1) * SK], cx[:, i, k * P:(k + 1) * P],
                                            ident[0:SK, 0:SK])
                elif kind == "k":
                    pe.wait_ge(wk_in, 16)
                    pe.wait_ge(evac, S)
                    for k in range(KT):
                        last = pe.matmul(bank[:, 0:HC], rk[:, k, i * P:(i + 1) * P],
                                         cT[:, k, h * HC:(h + 1) * HC], start=k == 0, stop=k == KT - 1)
                elif kind == "v":
                    pe.wait_ge(wv_in, 16)
                    for k in range(KT):
                        last = pe.matmul(bank[0:SK, :], cT[:, k, i * SK:(i + 1) * SK], rv[:, k, :],
                                         start=k == 0, stop=k == KT - 1)
                else:
                    if kind == "qkv":
                        pe.wait_ge(qkv_in, 16 * 9)
                        raw, m0, m1 = rqkv, 4 * h, 4 if h == 0 else 6
                    else:
                        pe.wait_ge(pj_in, 16)
                        raw, m0, m1 = rpj, 0, KT
                    for m in range(m0, m1):
                        last = pe.transpose(bank[:, (m - m0) * P:(m - m0 + 1) * P],
                                            raw[:, m, i * P:(i + 1) * P], ident[:, :])
                last.then_inc(mm_done, 1)

    xa = sb("xa", [P, 2, D])
    xc = sb("xc", [P, 2, D])
    xn = sb("xn", [P, D])
    xT = [sb("xT_hi", [P, KT, 2 * P], F32R), sb("xT_lo", [P, KT, 2 * P], F32R)]
    qT = sb("qT", [P, KT, 2 * P])
    pr = sb("pr", [P, 4, 4, SK])
    pT = sb("pT", [SK, 4, 4, P])
    ot = sb("ot", [P, D])
    oT = [sb("oT_hi", [P, KT, P], F32R), sb("oT_lo", [P, KT, P], F32R)]
    x2 = sb("x2", [P, 8, D])
    z = sb("z", [P, D])
    y = sb("y", [P, KT, P])
    zT = [sb("zT_hi", [P, KT, P], F32R), sb("zT_lo", [P, KT, P], F32R)]
    qb = sb("qb", [P, 2, D])
    kc = sb("kc", [P, S, NKV * DH])
    vc = sb("vc", [P, S, NKV * DH])
    prod = sb("prod", [P, 2, S * P])
    sc = sb("sc", [P, H, S])
    pa = sb("pa", [P, H, S])
    att_small = sb("att_small", [P, 3, H])
    ao = sb("ao", [P, D])
    aT = [sb("aT_hi", [P, KT, P], F32R), sb("aT_lo", [P, KT, P], F32R)]
    h1 = sb("h1", [P, D])
    z2 = sb("z2", [P, D])
    base = sb("base", [P, D])
    y2 = sb("y2", [P, KT, P])
    bnx, bnc, bnf = sb("bnx", [P, 6]), sb("bnc", [P, 6]), sb("bnf", [P, 6])
    mvx, mvc, mvf = sb("mvx", [P, 2, 2]), sb("mvc", [P, 8, 2]), sb("mvf", [P, 2, 2])
    rx, rc, rcc, rf = sb("rx", [P, 2]), sb("rc", [P, 8]), sb("rcc", [P, 2]), sb("rf", [P, 2])
    wx, wc, wf = sb("wx", [P, 1]), sb("wc", [P, 4]), sb("wf", [P, 1])
    mx, nm = sb("mx", [P, H]), sb("nm", [P, H])
    rec = sb("rec", [P, 2, 8])

    main_psum = ExitStack()
    with main_psum:
        psS = main_psum.enter_context(nc.psum_tensor("score_ps", [P, 4, 512], F32))
        psR = main_psum.enter_context(nc.psum_tensor("ring_ps", [P, RING, 512], F32))

        xa_in = [sem(f"xa_in{i}") for i in range(2)]
        xc_in = [sem(f"xc_in{i}") for i in range(2)]
        z2_out = sem("z2_out")
        base_out = sem("base_out")
        names = ("stat_x chain_x rstd_x normed_x xt_mm xt_hi xt_lo q_mm q_evac s_mm masked mx_done nm_done exp_done "
                 "pt_mm pt_act pt_dve pv_mm rec_done o_done ot_mm ot_hi ot_lo wo_mm bias_x x2_done chain_c stat_c "
                 "pool_c rstd_c z_done zt_mm y_done z_hi z_lo qkv_mm qkv_evac prods reduced sm_chain sm_sub sm_exp "
                 "sm_p at_mm at_hi at_lo pj_mm h0_done h1_done chain_f stat_f pool_f rstd_f base_done z2_done "
                 "z2t_mm y2_done lg_mm lg_evac pool_x").split()
        s = {n: sem(n) for n in names}
        places, order = job_places()

        read_out = {
            ("z2t", 0): ("y2_done", 4, 4), ("xt", 0): ("xt_lo", 1, 1), ("ot", 0): ("ot_lo", 1, 1),
            ("zt", 0): ("y_done", 4, 4), ("at", 0): ("at_lo", 1, 1),
            ("pt", 0): ("pt_act", 2, 1), ("pt", 1): ("pt_act", 2, 2),
            ("pt", 2): ("pt_dve", 2, 1), ("pt", 3): ("pt_dve", 2, 2),
            ("lg", 0): ("lg_evac", 1, 1), ("wo", 0): ("x2_done", 1, 1),
            ("qkv", 0): ("qkv_evac", 2, 1), ("qkv", 1): ("qkv_evac", 2, 2), ("pj", 0): ("h1_done", 1, 1),
            ("pv", 0): ("o_done", 2, 1), ("pv", 1): ("o_done", 2, 2),
        }

        def bank(step, kind, i=0):
            return psR[:, places[step, kind, i] % RING, :]

        def bank_free(pe, c, step, kind, i=0):
            at = places[step, kind, i]
            while True:
                at -= RING
                back = 0 if at >= 0 else -1
                if back and isinstance(c, int) and c == 0:
                    return
                ps_, (k, lag, j) = order[at % len(order)]
                t = At(c, ps_ + 8 * back - lag)
                if t.within(NT):
                    break
            if k == "q":
                need(pe, s["q_evac"], t.count(2, 2 * j + 2))
            else:
                name, per, j = read_out[k, j]
                need(pe, s[name], t.count(per, j))

        def pipeline(engine, step):
            for i in range(8):
                step(0, i)
            with engine.Fori(1, NC) as c:
                for i in range(8):
                    step(c, i)
            for i in range(8):
                step(NC, i)

        def row0(t):
            return t.chunk * P + t.s * L

        def split_matmuls(pe, dst, lhs, rhs):
            for k in range(KT):
                for n, (l, r) in enumerate(((0, 0), (0, 1), (1, 0))):
                    last = pe.matmul(dst, lhs(l, k), rhs(r, k), start=k == 0 and n == 0,
                                     stop=k == KT - 1 and n == 2)
            return last

        block = main_psum.enter_context(nc.Block())

        @block.sync
        def _(sp):
            def step(c, i):
                t = At(c, i)
                if t.within(NT):
                    need(sp, s["normed_x"], t.count(1, -1))
                    sp.dma_start(xa[:, t.s % 2, :], x2d[bass.ds(row0(t), P), :]).then_inc(xa_in[t.s % 2], 16)
                t = At(c, i - 2)
                if t.within(NT):
                    need(sp, s["x2_done"], t.count(1, -1))
                    sp.dma_start(xc[:, t.s % 2, :], x2d[bass.ds(row0(t), P), :]).then_inc(xc_in[t.s % 2], 16)

            pipeline(sp, step)

        @block.gpsimd
        def _(pool):
            def rstd(dst, var, work, chain, count):
                pool.tensor_scalar(work, var, EPS, None, ALU.add).then_inc(chain, 1)
                need(pool, chain, count)
                return pool.tensor_tensor(dst, work, expo[:, 0:1], ALU.pow)

            def products(t, first):
                n = t.s + 1
                for g in range(first, first + 2):
                    half, grp = divmod(g, NKV)
                    b = g % 2
                    need(pool, s["reduced"], t.count(8, g - 1))
                    o = prod[:, b, 0:n * P].rearrange("p (t h d) -> p t h d", t=n, h=HQ)
                    shape = [P, n, HQ, DH]
                    if half == 0:
                        if g == 0:
                            need(pool, s["qkv_evac"], t.count(2, 2))
                        q = qb[:, t.s % 2, grp * P:(grp + 1) * P].rearrange("p (h d) -> p h d", h=HQ)
                        pool.tensor_tensor(o, bc(q, 1, shape),
                                           bc(kc[:, 0:n, grp * DH:(grp + 1) * DH], 2, shape),
                                           ALU.mult).then_inc(s["prods"], 1)
                    else:
                        if grp == 0:
                            need(pool, s["sm_p"], t.count(1, 1))
                        w = pa[:, grp * HQ:(grp + 1) * HQ, 0:n].rearrange("p h t -> p t h")
                        pool.tensor_tensor(o, bc(w, 3, shape),
                                           bc(vc[:, 0:n, grp * DH:(grp + 1) * DH], 2, shape),
                                           ALU.mult).then_inc(s["prods"], 1)

            def step(c, i):
                t = At(c, i)
                if t.within(NT):
                    need_apart(pool, (s["stat_x"], t.count(1, 1)))
                    rstd(rx[:, i % 2:i % 2 + 1], mvx[:, i % 2, 1:2], wx[:, :], s["pool_x"], t.count(1, 1))\
                        .then_inc(s["rstd_x"], 1)
                t = At(c, i - 6)
                if t.within(NT):
                    products(t, 0)
                t = At(c, i - 5)
                if t.within(NT):
                    need(pool, s["z_hi"], t.count(1, 1))
                    need(pool, s["qkv_mm"], t.count(2))
                    pool.tensor_tensor(zT[1][:, :, :], y[:, :, :], zT[0][:, :, :].bitcast(F32), ALU.subtract)\
                        .then_inc(s["z_lo"], 1)
                t = At(c, i - 6)
                if t.within(NT):
                    products(t, 2)
                t = At(c, i - 3)
                if t.within(NT):
                    pool.wait_ge(xc_in[t.s % 2], t.turns(2, 16, 16))
                    pool.tensor_tensor(xc[:, t.s % 2, :], xc[:, t.s % 2, :], bo[:, :], ALU.add)\
                        .then_inc(s["bias_x"], 1)
                t = At(c, i - 6)
                if t.within(NT):
                    products(t, 4)
                t = At(c, i - 4)
                if t.within(NT):
                    need_apart(pool, (s["stat_c"], t.count(1, 1)))
                    var, r = mvc[:, t.s, 1:2], rc[:, t.s:t.s + 1]
                    rstd(r, var, wc[:, 0:1], s["pool_c"], t.count(6, 1)).then_inc(s["pool_c"], 1)
                    need(pool, s["pool_c"], t.count(6, 2))
                    pool.tensor_tensor(wc[:, 1:2], var, r, ALU.mult).then_inc(s["pool_c"], 1)
                    need(pool, s["pool_c"], t.count(6, 3))
                    pool.tensor_tensor(wc[:, 2:3], wc[:, 1:2], r, ALU.mult).then_inc(s["pool_c"], 1)
                    need_apart(pool, (s["pool_c"], t.count(6, 4)))
                    rstd(wc[:, 3:4], wc[:, 2:3], wc[:, 0:1], s["pool_c"], t.count(6, 5)).then_inc(s["pool_c"], 1)
                    need(pool, s["pool_c"], t.count(6, 6))
                    need(pool, s["z_done"], t.count(1, -1))
                    pool.tensor_tensor(rcc[:, t.s % 2:t.s % 2 + 1], r, wc[:, 3:4], ALU.mult)\
                        .then_inc(s["rstd_c"], 1)
                t = At(c, i - 6)
                if t.within(NT):
                    products(t, 6)
                t = At(c, i - 7)
                if t.within(NT):
                    need_apart(pool, (s["stat_f"], t.count(1, 1)))
                    rstd(rf[:, t.s % 2:t.s % 2 + 1], mvf[:, t.s % 2, 1:2], wf[:, :], s["pool_f"], t.count(1, 1))\
                        .then_inc(s["rstd_f"], 1)
                    need(pool, base_out, t.count(16))
                    pool.tensor_tensor(base[:, :], x2[:, t.s, :], h1[:, :], ALU.add)\
                        .then_inc(s["base_done"], 1)

            pipeline(pool, step)

        @block.scalar
        def _(act):
            def step(c, i):
                t = At(c, i - 8)
                if t.within(NT):
                    need(act, s["base_done"], t.count(1, 1))
                    act.dma_start(out2d[bass.ds(row0(t), P), :], base[:, :]).then_inc(base_out, 16)
                    need(act, s["z2_done"], t.count(1, 1))
                    act.dma_start(z2d[bass.ds(row0(t), P), :], z2[:, :]).then_inc(z2_out, 16)
                    act.wait_ge(s["z2t_mm"], t.count(1, 1))
                    for k in range(KT):
                        act.activation(y2[:, k, :], bank(i, "z2t")[:, k * P:(k + 1) * P], ACT.Identity,
                                       bias=ln2b[:, k:k + 1], scale=ln2w[:, k:k + 1]).then_inc(s["y2_done"], 1)
                for lag, mm, hi, dst, kind, free in (
                        (1, "xt_mm", "xt_hi", xT, "xt", None), (4, "ot_mm", "ot_hi", oT, "ot", ("wo_mm", 1)),
                        (5, None, None, None, None, None), (7, "at_mm", "at_hi", aT, "at", ("pj_mm", 1))):
                    t = At(c, i - lag)
                    if not t.within(NT):
                        continue
                    if lag == 5:
                        act.wait_ge(s["zt_mm"], t.count(1, 1))
                        need(act, s["z_lo"], t.count(1))
                        for k in range(KT):
                            act.activation(y[:, k, :], bank(i, "zt")[:, k * P:(k + 1) * P], ACT.Identity,
                                           bias=ln1b[:, k:k + 1], scale=ln1w[:, k:k + 1]).then_inc(s["y_done"], 1)
                        continue
                    act.wait_ge(s[mm], t.count(1, 1))
                    if kind == "xt":
                        half = t.s % 2
                        need(act, s["q_mm"], At(c, i - 1 - half).count(1))
                        o = dst[0][:, :, half * P:(half + 1) * P]
                    else:
                        need(act, s[free[0]], t.count(free[1]))
                        o = dst[0][:, :, :]
                    act.activation(o, bank(i, kind).rearrange("p (k n) -> p k n", k=KT), ACT.Copy)\
                        .then_inc(s[hi], 1)
                if i % 2 == 0 and At(c, i - 2).within(NT):
                    t = At(c, i - 2)
                    for m in range(KT):
                        if m % 2 == 0:
                            act.wait_ge(s["q_mm"], t.count(1, m // 2 + 1))
                        need(act, s["s_mm"], t.count(1))
                        act.activation(qT[:, m, :], bank(i, "q", m // 2)[:, (m % 2) * 256:(m % 2) * 256 + 256],
                                       ACT.Identity, bias=bq[:, m:m + 1]).then_inc(s["q_evac"], 1)
                t = At(c, i - 3)
                if t.within(NT):
                    for j in range(2):
                        act.wait_ge(s["pt_mm"], t.count(4, j + 1))
                        need(act, s["pv_mm"], t.count(2))
                        act.activation(pT[:, j, :, :],
                                       bank(i, "pt", j)[0:SK, :].rearrange("p (g n) -> p g n", g=4),
                                       ACT.Copy).then_inc(s["pt_act"], 1)
                t = At(c, i - 6)
                if t.within(NT):
                    act.wait_ge(s["sm_sub"], t.count(1, 1))
                    act.activation(pa[:, :, 0:t.s + 1], sc[:, :, 0:t.s + 1], ACT.Exp, scale=SCALE)\
                        .then_inc(s["sm_exp"], 1)
                t = At(c, i - 8)
                if t.within(NT):
                    act.wait_ge(s["lg_mm"], t.count(1, 1))
                    act.activation(logits[:, bass.ds(t.s * NC + t.chunk, 1), :],
                                   bank(i, "lg")[:, 0:E].unsqueeze(1), ACT.Copy).then_inc(s["lg_evac"], 1)
                t = At(c, i - 5)
                if t.within(NT):
                    act.wait_ge(s["qkv_mm"], t.count(2, 1))
                    need(act, s["prods"], t.count(8, -12))
                    act.activation(qb[:, t.s % 2, :], bank(i, "qkv", 0), ACT.Copy).then_inc(s["qkv_evac"], 1)
                    act.wait_ge(s["qkv_mm"], t.count(2, 2))
                    if t.s == 0:
                        need(act, s["prods"], t.count(8))
                    act.activation(kc[:, t.s, :], bank(i, "qkv", 1)[:, 0:P], ACT.Copy)
                    act.activation(vc[:, t.s, :], bank(i, "qkv", 1)[:, P:2 * P], ACT.Copy)\
                        .then_inc(s["qkv_evac"], 1)
                t = At(c, i - 2)
                if t.within(NT):
                    act.wait_ge(s["nm_done"], t.count(1, 1))
                    need(act, s["pt_mm"], t.count(4))
                    for b in range(4):
                        for g in range(4):
                            e = act.activation(pr[:, b, g, :], psS[:, b, g * SK:(g + 1) * SK], ACT.Exp,
                                               bias=nm[:, 4 * b + g:4 * b + g + 1], scale=SCALE)
                        e.then_inc(s["exp_done"], 1)

            pipeline(act, step)
            act.wait_ge(base_out, 16 * NT)
            act.wait_ge(z2_out, 16 * NT)

        @block.vector
        def _(dve):
            def stats(src, bn, mv, chain, count):
                dve.bn_stats(bn[:, :], src).then_inc(chain, 1)
                need_apart(dve, (chain, count))
                return dve.bn_aggr(mv, bn[:, :])

            def low_half(c, i, lag, mm_bank, parts, hi, lo):
                t = At(c, i - lag)
                if t.within(NT):
                    dve.wait_ge(s[hi], t.count(1, 1))
                    half = slice((t.s % 2) * P, (t.s % 2) * P + P) if mm_bank == "xt" else slice(0, P)
                    dve.tensor_tensor(parts[1][:, :, half], bank(i, mm_bank).rearrange("p (k n) -> p k n", k=KT),
                                      parts[0][:, :, half].bitcast(F32), ALU.subtract).then_inc(s[lo], 1)

            def sums(t, first):
                n = t.s + 1
                for g in range(first, first + 2):
                    half, grp = divmod(g, NKV)
                    need(dve, s["prods"], t.count(8, g + 1))
                    if half == 0:
                        dve.tensor_reduce(sc[:, grp * HQ:(grp + 1) * HQ, 0:n].rearrange("p h t -> p t h"),
                                          prod[:, g % 2, 0:n * P].rearrange("p (t h d) -> p t h d", t=n, h=HQ),
                                          X, ALU.add).then_inc(s["reduced"], 1)
                    else:
                        need(dve, s["at_mm"], t.count(1))
                        dve.tensor_reduce(ao[:, grp * P:(grp + 1) * P],
                                          prod[:, g % 2, 0:n * P].rearrange("p (t f) -> p f t", t=n),
                                          X, ALU.add).then_inc(s["reduced"], 1)

            def step(c, i):
                t = At(c, i)
                if t.within(NT):
                    dve.wait_ge(xa_in[i % 2], t.turns(2, 16, 16))
                    stats(xa[:, i % 2, :], bnx, mvx[:, i % 2, :], s["chain_x"], t.count(1, 1)).then_inc(s["stat_x"], 1)
                low_half(c, i, 1, "xt", xT, "xt_hi", "xt_lo")
                low_half(c, i, 4, "ot", oT, "ot_hi", "ot_lo")
                t = At(c, i - 5)
                if t.within(NT):
                    dve.wait_ge(s["y_done"], t.count(4, 4))
                    need(dve, s["qkv_mm"], t.count(2))
                    dve.tensor_copy(zT[0][:, :, :], y[:, :, :]).then_inc(s["z_hi"], 1)
                low_half(c, i, 7, "at", aT, "at_hi", "at_lo")
                t = At(c, i - 6)
                if t.within(NT):
                    n = t.s + 1
                    sums(t, 0)
                    sums(t, 2)
                    need(dve, s["reduced"], t.count(8, 4))
                    dve.tensor_reduce(att_small[:, 0, :], sc[:, :, 0:n], X, ALU.max).then_inc(s["sm_chain"], 1)
                    dve.wait_ge(s["sm_chain"], t.count(3, 1))
                    dve.tensor_tensor(sc[:, :, 0:n], sc[:, :, 0:n], bc(att_small[:, 0, :], 2, [P, H, n]),
                                      ALU.subtract).then_inc(s["sm_sub"], 1)
                t = At(c, i - 3)
                if t.within(NT):
                    for j in range(2, 4):
                        dve.wait_ge(s["pt_mm"], t.count(4, j + 1))
                        need(dve, s["pv_mm"], t.count(2))
                        dve.tensor_copy(pT[:, j, :, :],
                                        bank(i, "pt", j)[0:SK, :].rearrange("p (g n) -> p g n", g=4))\
                           .then_inc(s["pt_dve"], 1)
                t = At(c, i - 6)
                if t.within(NT):
                    n = t.s + 1
                    dve.wait_ge(s["sm_exp"], t.count(1, 1))
                    dve.tensor_reduce(att_small[:, 1, :], pa[:, :, 0:n], X, ALU.add).then_inc(s["sm_chain"], 1)
                    dve.wait_ge(s["sm_chain"], t.count(3, 2))
                    dve.reciprocal(att_small[:, 2, :], att_small[:, 1, :]).then_inc(s["sm_chain"], 1)
                    dve.wait_ge(s["sm_chain"], t.count(3, 3))
                    dve.tensor_tensor(pa[:, :, 0:n], pa[:, :, 0:n], bc(att_small[:, 2, :], 2, [P, H, n]),
                                      ALU.mult).then_inc(s["sm_p"], 1)
                t = At(c, i - 4)
                if t.within(NT):
                    dve.wait_ge(s["wo_mm"], t.count(1, 1))
                    dve.wait_ge(s["bias_x"], t.count(1, 1))
                    need(dve, s["base_done"], t.count(1, -3))
                    dve.tensor_tensor(x2[:, t.s, :], bank(i, "wo"), xc[:, t.s % 2, :], ALU.add)\
                       .then_inc(s["x2_done"], 1)
                    dve.wait_ge(s["x2_done"], t.count(1, 1))
                    stats(x2[:, t.s, :], bnc, mvc[:, t.s, :], s["chain_c"], t.count(1, 1)).then_inc(s["stat_c"], 1)
                t = At(c, i - 6)
                if t.within(NT):
                    sums(t, 4)
                t = At(c, i - 7)
                if t.within(NT):
                    need(dve, s["base_done"], t.count(1))
                    dve.tensor_scalar(h1[:, :], x2[:, t.s, :], mvc[:, t.s, 0:1], rc[:, t.s:t.s + 1], ALU.subtract,
                                      ALU.mult).then_inc(s["h0_done"], 1)
                    dve.wait_ge(s["h0_done"], t.count(1, 1))
                    dve.wait_ge(s["pj_mm"], t.count(1, 1))
                    dve.tensor_tensor(h1[:, :], bank(i, "pj"), h1[:, :], ALU.add).then_inc(s["h1_done"], 1)
                    dve.wait_ge(s["h1_done"], t.count(1, 1))
                    stats(h1[:, :], bnf, mvf[:, t.s % 2, :], s["chain_f"], t.count(1, 1)).then_inc(s["stat_f"], 1)
                t = At(c, i - 6)
                if t.within(NT):
                    sums(t, 6)
                t = At(c, i - 3)
                if t.within(NT):
                    for j in range(2):
                        dve.wait_ge(s["pv_mm"], t.count(2, j + 1))
                        heads = bank(i, "pv", j)[:, 0:8 * (DH + 1)].rearrange("p (h d) -> p h d", h=8)
                        dve.reciprocal(rec[:, j, :], heads[:, :, DH]).then_inc(s["rec_done"], 1)
                        dve.wait_ge(s["rec_done"], t.count(2, j + 1))
                        need(dve, s["ot_mm"], t.count(1))
                        dve.tensor_tensor(ot[:, j * 256:(j + 1) * 256].rearrange("p (h d) -> p h d", h=8),
                                          heads[:, :, 0:DH], bc(rec[:, j, :], 2, [P, 8, DH]), ALU.mult)\
                           .then_inc(s["o_done"], 1)
                t = At(c, i - 4)
                if t.within(NT):
                    dve.wait_ge(s["rstd_c"], t.count(1, 1))
                    need(dve, s["zt_mm"], t.count(1))
                    dve.tensor_scalar(z[:, :], x2[:, t.s, :], mvc[:, t.s, 0:1], rcc[:, t.s % 2:t.s % 2 + 1],
                                      ALU.subtract, ALU.mult).then_inc(s["z_done"], 1)
                t = At(c, i - 7)
                if t.within(NT):
                    dve.wait_ge(s["rstd_f"], t.count(1, 1))
                    need(dve, z2_out, t.count(16))
                    need(dve, s["z2t_mm"], t.count(1))
                    dve.tensor_scalar(z2[:, :], h1[:, :], mvf[:, t.s % 2, 0:1], rf[:, t.s % 2:t.s % 2 + 1],
                                      ALU.subtract, ALU.mult).then_inc(s["z2_done"], 1)
                t = At(c, i)
                if t.within(NT):
                    dve.wait_ge(s["rstd_x"], t.count(1, 1))
                    need(dve, s["xt_mm"], t.count(1))
                    dve.tensor_scalar(xn[:, :], xa[:, i % 2, :], mvx[:, i % 2, 0:1], rx[:, i % 2:i % 2 + 1],
                                      ALU.subtract, ALU.mult).then_inc(s["normed_x"], 1)
                t = At(c, i - 2)
                if t.within(NT):
                    dve.wait_ge(s["s_mm"], t.count(1, 1))
                    scores = psS[:, :, 0:4 * SK].rearrange("p b (g k) -> p b g k", g=4)
                    if (isinstance(c, int) and c == 0) or t.off < 0:
                        m = mask[:, bass.ds(t.chunk, 1), :].unsqueeze(1).to_broadcast([P, 4, 4, SK])
                        dve.tensor_tensor(scores, scores, m, ALU.add).then_inc(s["masked"], 1)
                        dve.wait_ge(s["masked"], c * 2 + (i - 1 if isinstance(c, int) and c == 0 else 5 + i))
                    need(dve, s["exp_done"], t.count(4))
                    dve.tensor_reduce(mx[:, :].rearrange("p (b g) -> p b g", b=4), scores, X, ALU.max)\
                       .then_inc(s["mx_done"], 1)
                    dve.wait_ge(s["mx_done"], t.count(1, 1))
                    dve.tensor_scalar(nm[:, :], mx[:, :], -SCALE, None, ALU.mult).then_inc(s["nm_done"], 1)

            pipeline(dve, step)

        @block.tensor
        def _(pe):
            def transposes(c, i, lag, kind, ready, count, src, mm):
                t = At(c, i - lag)
                if t.within(NT):
                    pe.wait_ge(s[ready], t.count(*count))
                    bank_free(pe, c, i, kind)
                    for k in range(KT):
                        last = pe.transpose(bank(i, kind)[:, k * P:(k + 1) * P], src(t)[:, k * P:(k + 1) * P],
                                            ident[:, :])
                    last.then_inc(s[mm], 1)

            def step(c, i):
                transposes(c, i, 8, "z2t", "z2_done", (1, 1), lambda t: z2[:, :], "z2t_mm")
                transposes(c, i, 1, "xt", "normed_x", (1, 1), lambda t: xn[:, :], "xt_mm")
                transposes(c, i, 4, "ot", "o_done", (2, 2), lambda t: ot[:, :], "ot_mm")
                transposes(c, i, 5, "zt", "z_done", (1, 1), lambda t: z[:, :], "zt_mm")
                transposes(c, i, 7, "at", "reduced", (8, 8), lambda t: ao[:, :], "at_mm")
                if i % 2 == 0 and At(c, i - 2).within(NT):
                    t = At(c, i - 2)
                    pe.wait_ge(s["xt_lo"], t.count(1, 2))
                    for j in range(2):
                        bank_free(pe, c, i, "q", j)
                        for m in range(2):
                            cols = slice((2 * j + m) * P, (2 * j + m + 1) * P)
                            last = split_matmuls(pe, bank(i, "q", j)[:, m * 256:(m + 1) * 256],
                                                 lambda h, k: wq[h][:, k, cols], lambda h, k: xT[h][:, k, :])
                        last.then_inc(s["q_mm"], 1)
                t = At(c, i - 3)
                if t.within(NT):
                    for b in range(4):
                        pe.wait_ge(s["exp_done"], t.count(4, b + 1))
                        bank_free(pe, c, i, "pt", b)
                        for g in range(4):
                            last = pe.transpose(bank(i, "pt", b)[0:SK, g * P:(g + 1) * P], pr[:, b, g, :],
                                                ident[:, :])
                        last.then_inc(s["pt_mm"], 1)
                t = At(c, i - 8)
                if t.within(NT):
                    pe.wait_ge(s["y2_done"], t.count(4, 4))
                    bank_free(pe, c, i, "lg")
                    for k in range(KT):
                        last = pe.matmul(bank(i, "lg")[:, 0:E], y2[:, k, :], wr[:, k, :], start=k == 0,
                                         stop=k == KT - 1)
                    last.then_inc(s["lg_mm"], 1)
                t = At(c, i - 4)
                if t.within(NT):
                    pe.wait_ge(s["ot_lo"], t.count(1, 1))
                    bank_free(pe, c, i, "wo")
                    split_matmuls(pe, bank(i, "wo"), lambda h, k: oT[h][:, k, :], lambda h, k: wo[h][:, k, :])\
                        .then_inc(s["wo_mm"], 1)
                t = At(c, i - 5)
                if t.within(NT):
                    pe.wait_ge(s["z_lo"], t.count(1, 1))
                    for j, (c0, c1) in enumerate(((0, D), (D, QKV))):
                        bank_free(pe, c, i, "qkv", j)
                        split_matmuls(pe, bank(i, "qkv", j)[:, 0:c1 - c0], lambda h, k: zT[h][:, k, :],
                                      lambda h, k: wqkv[h][:, k, c0:c1]).then_inc(s["qkv_mm"], 1)
                t = At(c, i - 7)
                if t.within(NT):
                    pe.wait_ge(s["at_lo"], t.count(1, 1))
                    bank_free(pe, c, i, "pj")
                    split_matmuls(pe, bank(i, "pj"), lambda h, k: aT[h][:, k, :], lambda h, k: wpj[h][:, k, :])\
                        .then_inc(s["pj_mm"], 1)
                t = At(c, i - 3)
                if t.within(NT):
                    pe.wait_ge(s["pt_act"], t.count(2, 2))
                    pe.wait_ge(s["pt_dve"], t.count(2, 2))
                    for j in range(2):
                        bank_free(pe, c, i, "pv", j)
                        for n in range(8):
                            h = 8 * j + n
                            last = pe.matmul(bank(i, "pv", j)[:, n * (DH + 1):(n + 1) * (DH + 1)],
                                             pT[:, h % 4, h // 4, :], va[:, t.s, h, :], start=True, stop=True)
                        last.then_inc(s["pv_mm"], 1)
                t = At(c, i - 2)
                if t.within(NT):
                    pe.wait_ge(s["q_evac"], At(c, i - 2 - t.s % 2).count(2, 4))
                    for g in range(4):
                        for b in range(4):
                            if g == 0:
                                need(pe, s["exp_done"], t.count(4, b - 3))
                            rows = slice(b * DH, (b + 1) * DH)
                            last = pe.matmul(psS[:, b, g * SK:(g + 1) * SK],
                                             qT[rows, g, (t.s % 2) * P:(t.s % 2) * P + P],
                                             kT[rows, g, t.s * SK:(t.s + 1) * SK], start=True, stop=True)
                    last.then_inc(s["s_mm"], 1)

            pipeline(pe, step)



def build_routing(nc, logits, tables, sb, sem):
    ranks = sb("ranks", [P, E])
    ramp = sb("ramp", [P, P])
    number = sb("number", [P, NT])
    before = sb("before", [P, P])
    ones = sb("ones", [P, P])
    ints = sb("ints", [P, P], I32)
    ints2 = sb("ints2", [P, NT], I32)
    ints3 = sb("ints3", [P, E], I32)
    best = sb("best", [P, 2, NT])
    first = sb("first", [P, 2, NT])
    eq = sb("eq", [P, NT, E])
    hot = sb("hot", [P, 2, NT, E])
    rest = sb("rest", [P, NT, E])
    both = sb("both", [P, NT, E])
    seen = sb("seen", [P, 2, NT, E])
    place = sb("place", [P, NT, E])
    share = sb("share", [P, 2, NT])
    diff = sb("diff", [P, NT])
    ex = sb("ex", [P, NT])
    den = sb("den", [P, NT])
    within = sb("within", [P, 2, NT])
    wi = sb("wi", [P, 2, NT], I32)
    qi = sb("qi", [P, 2, NT], I32)
    ri = sb("ri", [P, 2, NT], I32)
    blk = sb("blk", [P, 2, NT])
    row = sb("row", [P, 2, NT])
    over = sb("over", [P, 2, NT])
    hot_row = sb("hot_row", [P, 4, P])
    hot_blk = sb("hot_blk", [P, 4, 2, NBLK])
    ids = sb("ids", [P, NBLK])
    idc = sb("idc", [P, NBLK])
    with ExitStack() as st:
        pp = st.enter_context(nc.psum_tensor("prefix_ps", [P, 2, 512], F32))
        pt = st.enter_context(nc.psum_tensor("table_ps", [P, 2 * NBLK], F32))
        made, chain, sm, expd, prefixed, hots, tabled = (
            sem(n) for n in ("r_made", "r_chain", "r_diff", "r_exp", "r_prefixed", "r_hots", "r_tabled"))
        counted = sem("r_counted")
        block = st.enter_context(nc.Block())

        @block.gpsimd
        def _(pool):
            pool.iota(ints[:, :], [[1, P]], base=0, channel_multiplier=0).then_inc(made, 1)
            pool.iota(ints2[:, :], [[P, NT]], base=1, channel_multiplier=1).then_inc(made, 1)
            pool.iota(ints3[:, :], [[-1, E]], base=E, channel_multiplier=0).then_inc(made, 1)
            pool.memset(before[:, :], 1.0).then_inc(made, 1)
            pool.memset(ones[:, :], 1.0).then_inc(made, 1)
            pool.wait_ge(made, 5)
            pool.tensor_copy(ramp[:, :], ints[:, :]).then_inc(made, 1)
            pool.tensor_copy(number[:, :], ints2[:, :]).then_inc(made, 1)
            pool.tensor_copy(ranks[:, :], ints3[:, :]).then_inc(made, 1)
            pool.affine_select(out=before[:, :], in_=before[:, :], compare_op=ALU.is_gt, fill=0.0, base=0,
                               pattern=[[1, P]], channel_multiplier=-1).then_inc(made, 1)

        @block.scalar
        def _(act):
            act.wait_ge(sm, 1)
            act.activation(ex[:, :], diff[:, :], ACT.Exp).then_inc(expd, 1)

        @block.vector
        def _(dve):
            steps = [0]

            def link(instruction):
                steps[0] += 1
                instruction.then_inc(chain, 1)
                dve.wait_ge(chain, steps[0])

            dve.wait_ge(made, 9)
            shape = [P, NT, E]
            for k in range(2):
                src = logits if k == 0 else rest
                link(dve.tensor_reduce(best[:, k, :], src[:, :, :], X, ALU.max))
                link(dve.tensor_tensor(eq[:, :, :], src[:, :, :], bc(best[:, k, :], 2, shape), ALU.is_equal))
                link(dve.tensor_tensor(eq[:, :, :], eq[:, :, :], bc(ranks[:, :], 1, shape), ALU.mult))
                link(dve.tensor_reduce(first[:, k, :], eq[:, :, :], X, ALU.max))
                link(dve.tensor_tensor(hot[:, k, :, :], bc(first[:, k, :], 2, shape), bc(ranks[:, :], 1, shape),
                                       ALU.is_equal))
                if k == 0:
                    link(dve.scalar_tensor_tensor(rest[:, :, :], hot[:, 0, :, :], HUGE, logits[:, :, :], ALU.mult,
                                                  ALU.add))
            dve.tensor_tensor(diff[:, :], best[:, 1, :], best[:, 0, :], ALU.subtract).then_inc(sm, 1)
            dve.tensor_tensor(both[:, :, :], hot[:, 0, :, :], hot[:, 1, :, :], ALU.add).then_inc(counted, 1)
            dve.wait_ge(expd, 1)
            link(dve.tensor_scalar(den[:, :], ex[:, :], 1.0, None, ALU.add))
            link(dve.reciprocal(share[:, 0, :], den[:, :]))
            link(dve.tensor_tensor(share[:, 1, :], ex[:, :], share[:, 0, :], ALU.mult))
            dve.wait_ge(prefixed, 1)
            link(dve.tensor_copy(seen[:, 0, :, :], pp[:, 1, 0:NT * E].rearrange("p (t e) -> p t e", e=E)))
            src, sh = 0, 1
            while sh < NT:
                dst = 1 - src
                link(dve.tensor_tensor(seen[:, dst, sh:NT, :], seen[:, src, sh:NT, :], seen[:, src, 0:NT - sh, :],
                                       ALU.add))
                link(dve.tensor_copy(seen[:, dst, 0:sh, :], seen[:, src, 0:sh, :]))
                src, sh = dst, 2 * sh
            link(dve.tensor_tensor(place[:, :, :], pp[:, 0, 0:NT * E].rearrange("p (t e) -> p t e", e=E),
                                   seen[:, src, :, :], ALU.add))
            link(dve.tensor_tensor(place[:, :, :], place[:, :, :],
                                   pp[:, 1, 0:NT * E].rearrange("p (t e) -> p t e", e=E), ALU.subtract))
            for k in range(2):
                link(dve.tensor_tensor(eq[:, :, :], hot[:, k, :, :], place[:, :, :], ALU.mult))
                link(dve.tensor_reduce(within[:, k, :], eq[:, :, :], X, ALU.add))
            link(dve.tensor_copy(wi[:, :, :], within[:, :, :]))
            link(dve.tensor_scalar(qi[:, :, :], wi[:, :, :], 7, None, ALU.logical_shift_right))
            link(dve.tensor_scalar(ri[:, :, :], wi[:, :, :], P - 1, None, ALU.bitwise_and))
            link(dve.tensor_copy(blk[:, :, :], qi[:, :, :]))
            link(dve.tensor_copy(row[:, :, :], ri[:, :, :]))
            link(dve.tensor_scalar(over[:, :, :], within[:, :, :], float(CAP), 1000.0, ALU.is_ge, ALU.mult))
            link(dve.tensor_tensor(blk[:, :, :], blk[:, :, :], over[:, :, :], ALU.add))
            link(dve.tensor_scalar(over[:, :, :], first[:, :, :], -float(BPE), float(E * BPE), ALU.mult, ALU.add))
            link(dve.tensor_tensor(blk[:, :, :], blk[:, :, :], over[:, :, :], ALU.add))
            for k in range(2):
                with dve.Fori(0, NT // 4) as c:
                    for j in range(4):
                        col = bass.ds(c * 4 + j, 1)
                        dve.wait_ge(tabled, c * 4 + (NT * k + j + 1))
                        dve.tensor_scalar(hot_row[:, j, :], ramp[:, :], row[:, k, col], None, ALU.is_equal)
                        dve.tensor_scalar(hot_blk[:, j, 0, :], ramp[:, 0:NBLK], blk[:, k, col], number[:, col],
                                          ALU.is_equal, ALU.mult)
                        dve.tensor_scalar(hot_blk[:, j, 1, :], ramp[:, 0:NBLK], blk[:, k, col],
                                          share[:, k, col], ALU.is_equal, ALU.mult).then_inc(hots, 1)
            dve.wait_ge(tabled, 2 * NT + 4)
            dve.tensor_copy(tables["shares"][:, :], pt[:, NBLK:2 * NBLK])
            link(dve.tensor_scalar(ids[:, :], pt[:, 0:NBLK], 0.0, 2.0 * N, ALU.is_equal, ALU.mult))
            link(dve.scalar_tensor_tensor(idc[:, :], pt[:, 0:NBLK], -1.0, ids[:, :], ALU.add, ALU.add))
            dve.tensor_copy(tables["rows"][:, :], idc[:, :])

        @block.tensor
        def _(pe):
            pe.sem_inc(tabled, 4)
            pe.wait_ge(made, 9)
            pe.wait_ge(counted, 1)
            flat = both[:, :, :].rearrange("p t e -> p (t e)")
            pe.matmul(pp[:, 0, 0:NT * E], before[:, :], flat, start=True, stop=True)
            pe.matmul(pp[:, 1, 0:NT * E], ones[:, :], flat, start=True, stop=True).then_inc(prefixed, 1)
            for n in range(2 * NT):
                pe.wait_ge(hots, n + 1)
                pe.matmul(pt[:, :], hot_row[:, n % 4, :], hot_blk[:, n % 4, :, :].rearrange("p a b -> p (a b)"),
                          start=n == 0, stop=n == 2 * NT - 1).then_inc(tabled, 1)



def build_experts(nc, a, out2d, z2d, ident, ln2w, ln2b, tables, sb, sem):
    w1 = [[sb(f"w1_{p}{h}", [P, KT, F], F32R) for h in range(2)] for p in range(2)]
    w2 = [[sb(f"w2_{p}{h}", [P, FT, D], F32R) for h in range(2)] for p in range(2)]
    raw = sb("raw", [P, 2, F])
    xg = sb("xg", [P, GB, D])
    yk = sb("yk", [P, 2, GB * P])
    xT = [sb("gT_hi", [P, KT, GB * P], F32R), sb("gT_lo", [P, KT, GB * P], F32R)]
    gl = sb("gl", [P, 2, 2 * GB * P])
    hT = [[sb(f"hT_{p}{h}", [P, FT, GB * P], F32R) for h in range(2)] for p in range(2)]
    og = sb("og", [P, GB, D])
    idx = sb("idx", [P, GPE, GB], I32)
    W = GB * P
    CH = 8
    PER = 2 * GPE

    with ExitStack() as st:
        pT = st.enter_context(nc.psum_tensor("gather_ps", [P, GB, 512], F32))
        pH = st.enter_context(nc.psum_tensor("hidden_ps", [P, 4, 512], F32))
        pY = st.enter_context(nc.psum_tensor("expert_ps", [P, GB, 512], F32))
        raw_in = [sem(f"raw_in{i}") for i in range(2)]
        names = ("w_hi w_lo cleared copied gathered fetched scattered xt_mm yk_done xt_hi xt_lo fc1_mm gelu h_hi h_lo "
                 "fc2_mm summed").split()
        s = {n: sem("e_" + n) for n in names}
        block = st.enter_context(nc.Block())

        def pipeline(engine, step):
            for i in range(PER):
                step(0, i)
            with engine.Fori(1, NG // PER) as c:
                for i in range(PER):
                    step(c, i)
            for i in range(PER):
                step(NG // PER, i)

        def col(g, b):
            return bass.ds(g.count(GB, b), 1)

        def weight_piece(p, half, j):
            if j < 4:
                return w1[p][half][:, j, :]
            return w2[p][half][:, 2 * (j - 4):2 * (j - 4) + 2, :].rearrange("p f n -> p (f n)")

        @block.sync
        def _(sp):
            def load(e, c, p, j):
                n = At(c, CH * p + j, 2 * CH)
                need(sp, s["w_lo"], n.count(1, -1))
                if j < 4:
                    sp.dma_start(raw[:, j % 2, :], a["L0_ffn_moe_w1"].rearrange("e (k p) f -> (e k) p f", p=P)
                                 [bass.ds(e * KT + j, 1), :, :].rearrange("a p f -> (a p) f"))\
                      .then_inc(raw_in[j % 2], 16)
                else:
                    src = a["L0_ffn_moe_w2"].rearrange("e (q f p) n -> (e q) p f n", f=2, p=P)
                    sp.dma_start(raw[:, j % 2, :].rearrange("p (f n) -> p f n", f=2),
                                 src[bass.ds(e * 4 + (j - 4), 1), :, :, :].rearrange("a p f n -> (a p) f n"))\
                      .then_inc(raw_in[j % 2], 16)

            for p in range(2):
                for j in range(CH):
                    load(p, 0, p, j)
            with sp.Fori(1, E // 2) as c:
                for p in range(2):
                    for j in range(CH):
                        load(c * 2 + p, c, p, j)

        def weights_free(engine, c, p, j):
            if isinstance(c, int) and c == 0:
                return
            last = At(c, GPE * p - GPE - 1, PER)
            if j < 4:
                engine.wait_ge(s["fc1_mm"], last.count(4, 4))
            else:
                engine.wait_ge(s["fc2_mm"], last.count(GB, GB))

        def split_pieces(c, i):
            if isinstance(c, int) and c == E // 2:
                return []
            p, g = divmod(i, GPE)
            at = (0, 2, 4, 6, 7, 8)
            return [(c, p, j) for j in range(at[g], at[g + 1])]

        @block.gpsimd
        def _(pool):
            def low(c, p, j):
                n = At(c, CH * p + j, 2 * CH)
                pool.wait_ge(s["w_hi"], n.count(1, 1))
                weights_free(pool, c, p, j)
                pool.tensor_tensor(weight_piece(p, 1, j), raw[:, j % 2, :],
                                   weight_piece(p, 0, j).bitcast(F32), ALU.subtract).then_inc(s["w_lo"], 1)

            def rows(g, k):
                return bass.IndirectOffsetOnAxis(ap=idx[:, g.s % GPE, k:k + 1], axis=0)

            def step(c, i):
                g = At(c, i - 5, PER)
                if g.within(NG):
                    pool.tensor_copy(idx[:, g.s % GPE, :], tables["rows"][:, bass.ds(g.count(GB), GB)])\
                        .then_inc(s["copied"], 1)
                    need_apart(pool, (s["copied"], g.count(1, 1)), (s["xt_mm"], g.count(1)))
                    for k in range(GB):
                        pool.indirect_dma_start(out=xg[:, k, :], out_offset=None, in_=z2d[:, :],
                                                in_offset=rows(g, k), bounds_check=N - 1,
                                                oob_is_err=False).then_inc(s["gathered"], 16)
                g = At(c, i - 7, PER)
                if g.within(NG):
                    need_apart(pool, (s["scattered"], g.count(32)))
                    for k in range(GB):
                        pool.indirect_dma_start(out=og[:, k, :], out_offset=None, in_=out2d[:, :],
                                                in_offset=rows(g, k), bounds_check=N - 1,
                                                oob_is_err=False).then_inc(s["fetched"], 16)
                for piece in split_pieces(c, i):
                    low(*piece)
                if g.within(NG):
                    need_apart(pool, (s["summed"], g.count(GB, GB)))
                    for k in range(GB):
                        pool.indirect_dma_start(out=out2d[:, :], out_offset=rows(g, k), in_=og[:, k, :],
                                                in_offset=None, bounds_check=N - 1,
                                                oob_is_err=False).then_inc(s["scattered"], 16)

            pool.memset(xg[:, :, :], 0.0).then_inc(s["cleared"], 1)
            pool.memset(og[:, :, :], 0.0).then_inc(s["cleared"], 1)
            pool.wait_ge(s["cleared"], 2)
            pipeline(pool, step)
            pool.wait_ge(s["scattered"], 32 * NG)

        @block.scalar
        def _(act):
            def high(c, p, j):
                n = At(c, CH * p + j, 2 * CH)
                act.wait_ge(raw_in[j % 2], At(c, (CH * p + j) // 2, CH).count(16, 16))
                weights_free(act, c, p, j)
                act.activation(weight_piece(p, 0, j), raw[:, j % 2, :], ACT.Copy).then_inc(s["w_hi"], 1)

            def step(c, i):
                g = At(c, i - 6, PER)
                if g.within(NG):
                    for q in range(4):
                        act.wait_ge(s["fc1_mm"], g.count(4, q + 1))
                        need(act, s["h_lo"], g.count(4, q - 1))
                        act.activation(gl[:, q % 2, :], pH[:, q, :], ACT.Gelu_apprx_tanh).then_inc(s["gelu"], 1)
                g = At(c, i - 5, PER)
                if g.within(NG):
                    for k in range(KT):
                        act.wait_ge(s["yk_done"], g.count(KT, k + 1))
                        need(act, s["fc1_mm"], g.count(4))
                        act.activation(xT[0][:, k, :], yk[:, k % 2, :], ACT.Copy).then_inc(s["xt_hi"], 1)
                for piece in split_pieces(c, i):
                    high(*piece)

            pipeline(act, step)

        @block.vector
        def _(dve):
            def step(c, i):
                g = At(c, i - 6, PER)
                if g.within(NG):
                    par = g.s % 2
                    for q in range(4):
                        dve.wait_ge(s["gelu"], g.count(4, q + 1))
                        need(dve, s["fc2_mm"], g.count(GB, -GB))
                        o = [hT[par][h][:, 2 * q:2 * q + 2, :].rearrange("p f n -> p (f n)") for h in range(2)]
                        dve.tensor_copy(o[0], gl[:, q % 2, :]).then_inc(s["h_hi"], 1)
                        dve.wait_ge(s["h_hi"], g.count(4, q + 1))
                        dve.tensor_tensor(o[1], gl[:, q % 2, :], o[0].bitcast(F32), ALU.subtract)\
                           .then_inc(s["h_lo"], 1)
                g = At(c, i - 5, PER)
                if g.within(NG):
                    dve.wait_ge(s["xt_mm"], g.count(1, 1))
                    for k in range(KT):
                        need(dve, s["xt_lo"], g.count(KT, k - 1))
                        need(dve, s["xt_hi"], g.count(KT, k - 1))
                        dve.tensor_scalar(yk[:, k % 2, :].rearrange("p (b n) -> p b n", b=GB),
                                          pT[:, :, k * P:(k + 1) * P], ln2w[:, k:k + 1], ln2b[:, k:k + 1], ALU.mult,
                                          ALU.add).then_inc(s["yk_done"], 1)
                        dve.wait_ge(s["xt_hi"], g.count(KT, k + 1))
                        dve.tensor_tensor(xT[1][:, k, :], yk[:, k % 2, :], xT[0][:, k, :].bitcast(F32),
                                          ALU.subtract).then_inc(s["xt_lo"], 1)
                g = At(c, i - 7, PER)
                if g.within(NG):
                    dve.wait_ge(s["fetched"], g.count(32, 32))
                    for k in range(GB):
                        dve.wait_ge(s["fc2_mm"], g.count(GB, k + 1))
                        dve.scalar_tensor_tensor(og[:, k, :], pY[:, k, :], tables["shares"][:, col(g, k)], og[:, k, :],
                                                 ALU.mult, ALU.add).then_inc(s["summed"], 1)

            pipeline(dve, step)

        @block.tensor
        def _(pe):
            passes = ((0, 0), (0, 1), (1, 0))

            def step(c, i):
                g = At(c, i - 6, PER)
                if g.within(NG):
                    p = g.s // GPE
                    if g.s % GPE == 0:
                        pe.wait_ge(s["w_lo"], c * (2 * CH) + (CH * (g.off // GPE) + 4))
                    pe.wait_ge(s["xt_lo"], g.count(KT, KT))
                    for q in range(4):
                        need(pe, s["gelu"], g.count(4, q - 3))
                        for f in range(2):
                            cols = slice((2 * q + f) * P, (2 * q + f + 1) * P)
                            for k in range(KT):
                                for n, (l, r) in enumerate(passes):
                                    last = pe.matmul(pH[:, q, f * W:(f + 1) * W], w1[p][l][:, k, cols],
                                                     xT[r][:, k, :], start=k == 0 and n == 0,
                                                     stop=k == KT - 1 and n == 2)
                        last.then_inc(s["fc1_mm"], 1)
                g = At(c, i - 5, PER)
                if g.within(NG):
                    pe.wait_ge(s["gathered"], g.count(32, 32))
                    need(pe, s["yk_done"], g.count(KT))
                    for k in range(GB):
                        for m in range(KT):
                            last = pe.transpose(pT[:, k, m * P:(m + 1) * P], xg[:, k, m * P:(m + 1) * P],
                                                ident[:, :])
                    last.then_inc(s["xt_mm"], 1)
                g = At(c, i - 7, PER)
                if g.within(NG):
                    p = (g.s // GPE)
                    par = g.s % 2
                    if g.s % GPE == 0:
                        pe.wait_ge(s["w_lo"], c * (2 * CH) + (CH * (g.off // GPE) + CH))
                    pe.wait_ge(s["h_lo"], g.count(4, 4))
                    for k in range(GB):
                        need(pe, s["summed"], g.count(GB, k - 1))
                        for f in range(FT):
                            for n, (l, r) in enumerate(passes):
                                last = pe.matmul(pY[:, k, :], hT[par][l][:, f, k * P:(k + 1) * P], w2[p][r][:, f, :],
                                                 start=f == 0 and n == 0, stop=f == FT - 1 and n == 2)
                        last.then_inc(s["fc2_mm"], 1)

            pipeline(pe, step)


NAMES = ["x", "ctx_1024", "L0_xattn_Wq", "L0_xattn_bq", "L0_xattn_Wk", "L0_xattn_bk", "L0_xattn_Wv",
         "L0_xattn_bv", "L0_xattn_Wo", "L0_xattn_bo", "L0_ffn_ln1_weight", "L0_ffn_ln1_bias",
         "L0_ffn_ln2_weight", "L0_ffn_ln2_bias", "L0_ffn_qkv_weight", "L0_ffn_proj_weight",
         "L0_ffn_router_weight", "L0_ffn_moe_w1", "L0_ffn_moe_w2"]


def kernel(**inputs):
    import numpy as np
    import concourse.bacc as bacc
    from concourse.bass_utils import run_bass_kernel_spmd

    nc = bacc.Bacc("TRN2", target_bir_lowering=False, num_devices=1)
    arrays, aps = {}, {}
    for name in NAMES:
        v = np.ascontiguousarray(inputs[name])
        arrays[name + "_dram"] = v
        aps[name] = nc.dram_tensor(name + "_dram", v.shape, mybir.dt.from_np(v.dtype), kind="ExternalInput").ap()
    out = nc.dram_tensor("out_dram", (S, L, D), F32, kind="ExternalOutput").ap()
    build(nc, aps, out)
    result = run_bass_kernel_spmd(nc, [arrays], core_ids=[0])
    return result.results[0]["out_dram"]
```

```python
from contextlib import ExitStack

import concourse.bass as bass
from concourse import mybir

F32 = mybir.dt.float32
F32R = mybir.dt.float32r
I32 = mybir.dt.int32
ALU = mybir.AluOpType
ACT = mybir.ActivationFunctionType
X = mybir.AxisListType.X

P = 128
S = 8
L = 512
D = 512
KT = D // P
H = 16
DH = D // H
SK = 77
NKV = 4
HQ = H // NKV
QKV = D + 2 * NKV * DH
NC = L // P
NT = S * NC
N = S * L
E = 8
F = 1024
FT = F // P
CAP = 1280
BPE = CAP // P
NBLK = E * BPE
GB = 2
GPE = BPE // GB
NG = E * GPE
EPS = 1e-5
SCALE = float(DH) ** -0.5
MASKED = -1e30
HUGE = -3e38


class At:

    def __init__(self, c, off, period=8):
        self.c, self.off, self.period = c, off, period
        self.s = off % period
        self.chunk = c + off // period

    def count(self, k, i=0):
        if isinstance(self.c, int):
            return k * (self.period * self.c + self.off) + i
        return self.c * (k * self.period) + (k * self.off + i)

    def turns(self, ring, k=16, i=0):
        return (self.c * (k * (self.period // ring))) + (k * (self.off // ring) + i)

    def within(self, n):
        return not isinstance(self.c, int) or 0 <= self.period * self.c + self.off < n


def need(engine, sem, value):
    if not isinstance(value, int) or value > 0:
        engine.wait_ge(sem, value)


def need_apart(engine, *waits):
    waits = [(sem, v if isinstance(v, int) else engine.to_reg(v)) for sem, v in waits]
    if not all(isinstance(v, int) for _, v in waits):
        engine.wait_ge(waits[0][0], 1)
    for sem, v in waits:
        need(engine, sem, v)


def bc(ap, axis, shape):
    return ap.unsqueeze(axis).to_broadcast(shape)


def build(nc, a, out):
    x2d = a["x"].rearrange("b l d -> (b l) d")
    out2d = out.rearrange("b l d -> (b l) d")
    z2d = nc.dram_tensor("normed_tokens", [N, D], F32, kind="Internal").ap()

    whole = ExitStack()
    with whole:
        def sem(name):
            return whole.enter_context(nc.semaphore(name))

        def keeper(stack):
            def sb(name, shape, dt=F32):
                return stack.enter_context(nc.sbuf_tensor(name, shape, dt))
            return sb

        sb = keeper(whole)
        ident = sb("ident", [P, P])
        logits = sb("logits", [P, NT, E])
        ln2w = sb("ln2w", [P, KT])
        ln2b = sb("ln2b", [P, KT])
        main = ExitStack()
        with main:
            build_main(nc, a, x2d, out2d, z2d, ident, logits, ln2w, ln2b, keeper(main), sem)
        tables = {
            "rows": sb("rows", [P, NBLK], I32),
                "shares": sb("shares", [P, NBLK]),
        }
        routing = ExitStack()
        with routing:
            build_routing(nc, logits, tables, keeper(routing), sem)
        experts = ExitStack()
        with experts:
            build_experts(nc, a, out2d, z2d, ident, ln2w, ln2b, tables, keeper(experts), sem)



JOBS = ([("at", 7, 0), ("xt", 1, 0)] + [("pt", 3, i) for i in range(4)]
        + [("q", 2, 0), ("q", 2, 1), ("z2t", 8, 0), ("zt", 4, 0), ("pj", 7, 0), ("pv", 3, 0), ("lg", 8, 0),
           ("qkv", 4, 0), ("qkv", 4, 1), ("wo", 3, 0)])
RING = 4


def job_places():
    places, order = {}, []
    for s in range(8):
        for job in JOBS:
            if job[0] == "q" and s % 2:
                continue
            places[s, job[0], job[2]] = len(order)
            order.append((s, job))
    assert len(order) % RING == 0
    return places, order


def build_main(nc, a, x2d, out2d, z2d, ident, logits, ln2w, ln2b, sb, sem):
    wq = [sb("wq_hi", [P, KT, D], F32R), sb("wq_lo", [P, KT, D], F32R)]
    wo = [sb("wo_hi", [P, KT, D], F32R), sb("wo_lo", [P, KT, D], F32R)]
    wqkv = [sb("wqkv_hi", [P, KT, QKV], F32R), sb("wqkv_lo", [P, KT, QKV], F32R)]
    wpj = [sb("wpj_hi", [P, KT, D], F32R), sb("wpj_lo", [P, KT, D], F32R)]
    wr = sb("wr", [P, KT, E])
    kT = sb("kT", [P, KT, S * SK])
    va = sb("va", [SK, S, H, DH])
    bq = sb("bq", [P, KT])
    bk = sb("bk", [P, KT])
    ln1w = sb("ln1w", [P, KT])
    ln1b = sb("ln1b", [P, KT])
    bo = sb("bo", [P, D])
    mask = sb("mask", [P, NC, SK])
    expo = sb("expo", [P, 1])

    with ExitStack() as st:
        def tmp(name, shape, dt=F32):
            return st.enter_context(nc.sbuf_tensor(name, shape, dt))

        rq = tmp("rq", [P, KT, D])
        ro = tmp("ro", [P, KT, D])
        rqkv = tmp("rqkv", [P, 6, D])
        rpj = tmp("rpj", [P, KT, D])
        rk = tmp("rk", [P, KT, D])
        rv = tmp("rv", [P, KT, D])
        cx = tmp("cx", [SK, S, D])
        cT = tmp("cT", [P, KT, S * SK])
        bv = tmp("bv", [SK, D])
        ps = st.enter_context(nc.psum_tensor("setup_ps", [P, 8, 512], F32))
        ctx_in, wk_in, wv_in, qkv_in, pj_in, wq_in, wo_in, small_in = (
            sem(n) for n in ("ctx_in", "wk_in", "wv_in", "qkv_in", "pj_in", "wq_in", "wo_in", "small_in"))
        made, mm_done, hi_done, evac = (sem(n) for n in ("consts_made", "setup_mm", "setup_hi", "setup_evac"))
        split_hi = sem("setup_split_hi")

        jobs = ([("ctx", b, 0) for b in range(S)] + [("k", m, h) for m in range(KT) for h in range(2)]
                + [("v", b, 0) for b in range(S)] + [("qkv", k, h) for k in range(KT) for h in range(2)]
                + [("pj", k, 0) for k in range(KT)])
        HC = S * SK // 2
        SMALL = 9
        block = st.enter_context(nc.Block())

        @block.sync
        def _(sp):
            sp.dma_start(cx[:, :, :], a["ctx_1024"].rearrange("b s d -> s b d")).then_inc(ctx_in, 16)
            sp.dma_start(rk[:, :, :], a["L0_xattn_Wk"].rearrange("(k p) n -> p k n", p=P)).then_inc(wk_in, 16)
            sp.dma_start(rv[:, :, :], a["L0_xattn_Wv"].rearrange("(k p) n -> p k n", p=P)).then_inc(wv_in, 16)
            by_group = a["L0_ffn_qkv_weight"].rearrange("(g r) h -> r g h", g=NKV)
            sp.dma_start(rqkv[:, 0:4, :], by_group[0:P, :, :]).then_inc(qkv_in, 16)
            for g in range(NKV):
                rows = slice(g * DH, (g + 1) * DH)
                sp.dma_start(rqkv[rows, 4, :], by_group[P:P + DH, g, :]).then_inc(qkv_in, 16)
                sp.dma_start(rqkv[rows, 5, :], by_group[P + DH:P + 2 * DH, g, :]).then_inc(qkv_in, 16)
            sp.dma_start(rpj[:, :, :], a["L0_ffn_proj_weight"].rearrange("(m p) h -> p m h", p=P)).then_inc(pj_in, 16)
            sp.dma_start(rq[:, :, :], a["L0_xattn_Wq"].rearrange("(k p) n -> p k n", p=P)).then_inc(wq_in, 16)
            sp.dma_start(ro[:, :, :], a["L0_xattn_Wo"].rearrange("(k p) n -> p k n", p=P)).then_inc(wo_in, 16)

        @block.gpsimd
        def _(pool):
            pool.memset(ident[:, :], 0.0).then_inc(made, 1)
            pool.memset(mask[:, :, :], 0.0).then_inc(made, 1)
            pool.memset(expo[:, :], -0.5).then_inc(made, 1)
            pool.wait_ge(made, 3)
            pool.affine_select(out=ident[:, :], in_=ident[:, :], compare_op=ALU.not_equal, fill=1.0, base=0,
                               pattern=[[-1, P]], channel_multiplier=1).then_inc(made, 1)
            pool.affine_select(out=mask[:, 0, :], in_=mask[:, 0, :], compare_op=ALU.is_ge, fill=MASKED, base=0,
                               pattern=[[-1, SK]], channel_multiplier=1).then_inc(made, 1)

        @block.scalar
        def _(act):
            with nc.allow_non_contiguous_dma(reason="512 words of a bias as columns"):
                for dst, name in ((bq, "L0_xattn_bq"), (bk, "L0_xattn_bk"), (ln1w, "L0_ffn_ln1_weight"),
                                  (ln1b, "L0_ffn_ln1_bias"), (ln2w, "L0_ffn_ln2_weight"),
                                  (ln2b, "L0_ffn_ln2_bias")):
                    act.dma_start(dst[:, :], a[name].rearrange("(k p) -> p k", p=P)).then_inc(small_in, 16)
            act.dma_start(bv[:, :], a["L0_xattn_bv"].partition_broadcast(SK)).then_inc(small_in, 16)
            act.dma_start(bo[:, :], a["L0_xattn_bo"].partition_broadcast(P)).then_inc(small_in, 16)
            act.dma_start(wr[:, :, :], a["L0_ffn_router_weight"].rearrange("(k p) e -> p k e", p=P))\
               .then_inc(small_in, 16)
            act.wait_ge(wq_in, 16)
            act.activation(wq[0][:, :, :], rq[:, :, :], ACT.Copy).then_inc(split_hi, 1)
            act.wait_ge(wo_in, 16)
            act.activation(wo[0][:, :, :], ro[:, :, :], ACT.Copy).then_inc(split_hi, 1)
            for n, (kind, i, h) in enumerate(jobs):
                if kind in ("qkv", "pj"):
                    act.wait_ge(mm_done, n + 1)
                    w, c0, c1 = (wpj, 0, D) if kind == "pj" else (wqkv, 512 * h, 512 if h == 0 else QKV)
                    act.activation(w[0][:, i, c0:c1], ps[:, n % 8, 0:c1 - c0], ACT.Copy).then_inc(hi_done, 1)

        @block.vector
        def _(dve):
            dve.wait_ge(small_in, 16 * SMALL)
            halves = 0
            for n, (kind, i, h) in enumerate(jobs):
                dve.wait_ge(mm_done, n + 1)
                if kind == "ctx":
                    dve.tensor_copy(cT[:, :, i * SK:(i + 1) * SK],
                                    ps[:, n % 8, 0:KT * SK].rearrange("p (k s) -> p k s", k=KT)).then_inc(evac, 1)
                elif kind == "k":
                    dve.tensor_scalar(kT[:, i, h * HC:(h + 1) * HC], ps[:, n % 8, 0:HC], bk[:, i:i + 1], None,
                                      ALU.add).then_inc(evac, 1)
                elif kind == "v":
                    dve.tensor_tensor(va[:, i, :, :], ps[0:SK, n % 8, :].rearrange("p (h d) -> p h d", h=H),
                                      bv[:, :].rearrange("p (h d) -> p h d", h=H), ALU.add).then_inc(evac, 1)
                else:
                    halves += 1
                    dve.wait_ge(hi_done, halves)
                    w, c0, c1 = (wpj, 0, D) if kind == "pj" else (wqkv, 512 * h, 512 if h == 0 else QKV)
                    dve.tensor_tensor(w[1][:, i, c0:c1], ps[:, n % 8, 0:c1 - c0],
                                      w[0][:, i, c0:c1].bitcast(F32), ALU.subtract).then_inc(evac, 1)
            dve.wait_ge(split_hi, 2)
            dve.tensor_tensor(wq[1][:, :, :], rq[:, :, :], wq[0][:, :, :].bitcast(F32), ALU.subtract)
            dve.tensor_tensor(wo[1][:, :, :], ro[:, :, :], wo[0][:, :, :].bitcast(F32), ALU.subtract)

        @block.tensor
        def _(pe):
            pe.wait_ge(made, 5)
            for n, (kind, i, h) in enumerate(jobs):
                need(pe, evac, n - 7)
                bank = ps[:, n % 8, :]
                if kind == "ctx":
                    if n == 0:
                        pe.wait_ge(ctx_in, 16)
                    for k in range(KT):
                        last = pe.transpose(bank[:, k * SK:(k + 1) * SK], cx[:, i, k * P:(k + 1) * P],
                                            ident[0:SK, 0:SK])
                elif kind == "k":
                    pe.wait_ge(wk_in, 16)
                    pe.wait_ge(evac, S)
                    for k in range(KT):
                        last = pe.matmul(bank[:, 0:HC], rk[:, k, i * P:(i + 1) * P],
                                         cT[:, k, h * HC:(h + 1) * HC], start=k == 0, stop=k == KT - 1)
                elif kind == "v":
                    pe.wait_ge(wv_in, 16)
                    for k in range(KT):
                        last = pe.matmul(bank[0:SK, :], cT[:, k, i * SK:(i + 1) * SK], rv[:, k, :],
                                         start=k == 0, stop=k == KT - 1)
                else:
                    if kind == "qkv":
                        pe.wait_ge(qkv_in, 16 * 9)
                        raw, m0, m1 = rqkv, 4 * h, 4 if h == 0 else 6
                    else:
                        pe.wait_ge(pj_in, 16)
                        raw, m0, m1 = rpj, 0, KT
                    for m in range(m0, m1):
                        last = pe.transpose(bank[:, (m - m0) * P:(m - m0 + 1) * P],
                                            raw[:, m, i * P:(i + 1) * P], ident[:, :])
                last.then_inc(mm_done, 1)

    xa = sb("xa", [P, 2, D])
    xc = sb("xc", [P, 2, D])
    xT = [sb("xT_hi", [P, KT, 2 * P], F32R), sb("xT_lo", [P, KT, 2 * P], F32R)]
    qT = sb("qT", [P, KT, 2 * P])
    pr = sb("pr", [P, 4, 4, SK])
    pT = sb("pT", [SK, 4, 4, P])
    oT = [sb("oT_hi", [P, KT, P], F32R), sb("oT_lo", [P, KT, P], F32R)]
    x2 = sb("x2", [P, 8, D])
    z = sb("z", [P, D])
    y = sb("y", [P, KT, P])
    zT = [sb("zT_hi", [P, KT, P], F32R), sb("zT_lo", [P, KT, P], F32R)]
    qb = sb("qb", [P, 2, D])
    kc = sb("kc", [P, S, NKV * DH])
    vc = sb("vc", [P, S, NKV * DH])
    kvs = sb("kvs", [P, 2, 2 * NKV * DH])
    prod_k = sb("prod_k", [P, 2, S * P])
    prod_v = sb("prod_v", [P, 2, S * P])
    sc = sb("sc", [P, H, S])
    pa = sb("pa", [P, 2, H, S])
    att_small = sb("att_small", [P, 3, H])
    ao = sb("ao", [P, D])
    aT = [sb("aT_hi", [P, KT, P], F32R), sb("aT_lo", [P, KT, P], F32R)]
    h1 = sb("h1", [P, D])
    z2 = sb("z2", [P, D])
    y2 = sb("y2", [P, KT, P])
    bnx, bnc, bnf = sb("bnx", [P, 6]), sb("bnc", [P, 6]), sb("bnf", [P, 6])
    mvx, mvc, mvf = sb("mvx", [P, 2, 2]), sb("mvc", [P, 8, 2]), sb("mvf", [P, 2, 2])
    rx, rc, rcc, rf = sb("rx", [P, 2]), sb("rc", [P, 8]), sb("rcc", [P, 2]), sb("rf", [P, 2])
    wx, wc, wf = sb("wx", [P, 1]), sb("wc", [P, 4]), sb("wf", [P, 1])
    nm = sb("nm", [P, H])
    den, rec = sb("exp_sums", [P, H]), sb("rec", [P, H])

    main_psum = ExitStack()
    with main_psum:
        psS = main_psum.enter_context(nc.psum_tensor("score_ps", [P, 4, 512], F32))
        psR = main_psum.enter_context(nc.psum_tensor("ring_ps", [P, RING, 512], F32))

        xa_in = [sem(f"xa_in{i}") for i in range(2)]
        xc_in = [sem(f"xc_in{i}") for i in range(2)]
        z2_out = sem("z2_out")
        base_out = sem("base_out")
        names = ("stat_x chain_x rstd_x normed_x xt_mm xt_hi xt_lo q_mm q_evac s_mm masked mx_done nm_done exp_done "
                 "rec_done shared pt_mm pt_act pt_dve pv_mm o_hi o_lo wo_mm bias_x x2_done chain_c stat_c "
                 "pool_c rstd_c z_done zt_mm y_done z_hi z_lo qkv_mm qkv_evac k_kept v_kept prods_k sums_k prods_v "
                 "sums_v sm_chain sm_sub sm_exp sm_p at_mm at_hi at_lo pj_mm h0_done h1_done chain_f stat_f pool_f "
                 "rstd_f base_done z2_done z2t_mm y2_done lg_mm lg_evac pool_x").split()
        s = {n: sem(n) for n in names}
        places, order = job_places()

        read_out = {
            ("z2t", 0): ("y2_done", 4, 4), ("xt", 0): ("xt_lo", 1, 1), ("zt", 0): ("y_done", 4, 4),
            ("at", 0): ("at_lo", 1, 1), ("pt", 0): ("pt_act", 2, 1), ("pt", 1): ("pt_act", 2, 2),
            ("pt", 2): ("pt_dve", 2, 1), ("pt", 3): ("pt_dve", 2, 2), ("lg", 0): ("lg_evac", 1, 1),
            ("wo", 0): ("x2_done", 1, 1), ("qkv", 0): ("qkv_evac", 2, 1), ("qkv", 1): ("qkv_evac", 2, 2),
            ("pj", 0): ("h1_done", 1, 1), ("pv", 0): ("o_lo", 1, 1),
        }

        def bank(step, kind, i=0):
            return psR[:, places[step % 8, kind, i] % RING, :]

        def bank_free(pe, c, step, kind, i=0):
            at = places[step, kind, i]
            while True:
                at -= RING
                back = 0 if at >= 0 else -1
                if back and isinstance(c, int) and c == 0:
                    return
                ps_, (k, lag, j) = order[at % len(order)]
                t = At(c, ps_ + 8 * back - lag)
                if t.within(NT):
                    break
            if k == "q":
                need(pe, s["q_evac"], t.count(2, 2 * j + 2))
            else:
                name, per, j = read_out[k, j]
                need(pe, s[name], t.count(per, j))

        def pipeline(engine, step):
            for i in range(8):
                step(0, i)
            with engine.Fori(1, NC) as c:
                for i in range(8):
                    step(c, i)
            for i in range(8):
                step(NC, i)

        def row0(t):
            return t.chunk * P + t.s * L

        def split_matmuls(pe, dst, lhs, rhs):
            for k in range(KT):
                for n, (l, r) in enumerate(((0, 0), (0, 1), (1, 0))):
                    last = pe.matmul(dst, lhs(l, k), rhs(r, k), start=k == 0 and n == 0,
                                     stop=k == KT - 1 and n == 2)
            return last

        block = main_psum.enter_context(nc.Block())

        @block.sync
        def _(sp):
            def step(c, i):
                t = At(c, i)
                if t.within(NT):
                    need(sp, s["xt_mm"], t.count(1, -1))
                    sp.dma_start(xa[:, t.s % 2, :], x2d[bass.ds(row0(t), P), :]).then_inc(xa_in[t.s % 2], 16)
                t = At(c, i - 2)
                if t.within(NT):
                    need(sp, s["x2_done"], t.count(1, -1))
                    sp.dma_start(xc[:, t.s % 2, :], x2d[bass.ds(row0(t), P), :]).then_inc(xc_in[t.s % 2], 16)

            pipeline(sp, step)

        @block.gpsimd
        def _(pool):
            def rstd(dst, var, work, chain, count):
                pool.tensor_scalar(work, var, EPS, None, ALU.add).then_inc(chain, 1)
                need(pool, chain, count)
                return pool.tensor_tensor(dst, work, expo[:, 0:1], ALU.pow)

            def key_products(t, first, last):
                n = t.s + 1
                shape = [P, n, HQ, DH]
                if first == 0:
                    need_apart(pool, (s["qkv_evac"], t.count(2, 2)), (s["prods_k"], t.count(NKV)))
                    pool.tensor_copy(kc[:, t.s, :], kvs[:, t.s % 2, 0:P]).then_inc(s["k_kept"], 1)
                    pool.wait_ge(s["k_kept"], t.count(1, 1))
                for g in range(first, last):
                    need(pool, s["sums_k"], t.count(NKV, g - 1))
                    pool.tensor_tensor(prod_k[:, g % 2, 0:n * P].rearrange("p (t h d) -> p t h d", t=n, h=HQ),
                                       bc(qb[:, t.s % 2, g * P:(g + 1) * P].rearrange("p (h d) -> p h d", h=HQ),
                                          1, shape),
                                       bc(kc[:, 0:n, g * DH:(g + 1) * DH], 2, shape), ALU.mult)\
                        .then_inc(s["prods_k"], 1)

            def value_products(t, first, last):
                n = t.s + 1
                shape = [P, n, HQ, DH]
                if first == 0:
                    need_apart(pool, (s["prods_v"], t.count(NKV)))
                    pool.tensor_copy(vc[:, t.s, :], kvs[:, t.s % 2, P:2 * P]).then_inc(s["v_kept"], 1)
                    pool.wait_ge(s["v_kept"], t.count(1, 1))
                    need(pool, s["sm_p"], t.count(1, 1))
                for g in range(first, last):
                    need(pool, s["sums_v"], t.count(NKV, g - 1))
                    w = pa[:, t.s % 2, g * HQ:(g + 1) * HQ, 0:n].rearrange("p h t -> p t h")
                    pool.tensor_tensor(prod_v[:, g % 2, 0:n * P].rearrange("p (t h d) -> p t h d", t=n, h=HQ),
                                       bc(w, 3, shape), bc(vc[:, 0:n, g * DH:(g + 1) * DH], 2, shape), ALU.mult)\
                        .then_inc(s["prods_v"], 1)

            def step(c, i):
                tq, tv = At(c, i - 5), At(c, i - 6)
                if tq.within(NT):
                    key_products(tq, 0, 1)
                t = At(c, i - 4)
                if t.within(NT):
                    need_apart(pool, (s["stat_c"], t.count(1, 1)))
                    var, r = mvc[:, t.s, 1:2], rc[:, t.s:t.s + 1]
                    rstd(r, var, wc[:, 0:1], s["pool_c"], t.count(6, 1)).then_inc(s["pool_c"], 1)
                    need(pool, s["pool_c"], t.count(6, 2))
                    pool.tensor_tensor(wc[:, 1:2], var, r, ALU.mult).then_inc(s["pool_c"], 1)
                    need(pool, s["pool_c"], t.count(6, 3))
                    pool.tensor_tensor(wc[:, 2:3], wc[:, 1:2], r, ALU.mult).then_inc(s["pool_c"], 1)
                    need_apart(pool, (s["pool_c"], t.count(6, 4)))
                    rstd(wc[:, 3:4], wc[:, 2:3], wc[:, 0:1], s["pool_c"], t.count(6, 5)).then_inc(s["pool_c"], 1)
                    need(pool, s["pool_c"], t.count(6, 6))
                    need(pool, s["z_done"], t.count(1, -1))
                    pool.tensor_tensor(rcc[:, t.s % 2:t.s % 2 + 1], r, wc[:, 3:4], ALU.mult)\
                        .then_inc(s["rstd_c"], 1)
                if tq.within(NT):
                    key_products(tq, 1, 4)
                t = At(c, i - 4)
                if t.within(NT):
                    need(pool, s["z_hi"], t.count(1, 1))
                    need(pool, s["qkv_mm"], t.count(2))
                    pool.tensor_tensor(zT[1][:, :, :], y[:, :, :], zT[0][:, :, :].bitcast(F32), ALU.subtract)\
                        .then_inc(s["z_lo"], 1)
                if tv.within(NT):
                    value_products(tv, 0, 1)
                t = At(c, i - 7)
                if t.within(NT):
                    need_apart(pool, (s["stat_f"], t.count(1, 1)))
                    rstd(rf[:, t.s % 2:t.s % 2 + 1], mvf[:, t.s % 2, 1:2], wf[:, :], s["pool_f"], t.count(1, 1))\
                        .then_inc(s["rstd_f"], 1)
                if tv.within(NT):
                    value_products(tv, 1, 2)
                t = At(c, i - 3)
                if t.within(NT):
                    pool.wait_ge(xc_in[t.s % 2], t.turns(2, 16, 16))
                    pool.tensor_tensor(xc[:, t.s % 2, :], xc[:, t.s % 2, :], bo[:, :], ALU.add)\
                        .then_inc(s["bias_x"], 1)
                t = At(c, i)
                if t.within(NT):
                    need_apart(pool, (s["stat_x"], t.count(1, 1)))
                    rstd(rx[:, i % 2:i % 2 + 1], mvx[:, i % 2, 1:2], wx[:, :], s["pool_x"], t.count(1, 1))\
                        .then_inc(s["rstd_x"], 1)
                if tv.within(NT):
                    value_products(tv, 2, 4)
                t = At(c, i - 7)
                if t.within(NT):
                    pool.tensor_tensor(x2[:, t.s, :], x2[:, t.s, :], h1[:, :], ALU.add)\
                        .then_inc(s["base_done"], 1)

            pipeline(pool, step)

        @block.scalar
        def _(act):
            def step(c, i):
                for kind, lag, dst in (("at", 7, aT), ("xt", 1, xT)):
                    t = At(c, i - lag)
                    if not t.within(NT):
                        continue
                    act.wait_ge(s[kind + "_mm"], t.count(1, 1))
                    if kind == "xt":
                        half = t.s % 2
                        need(act, s["q_mm"], At(c, i - 1 - half).count(1))
                        o = dst[0][:, :, half * P:(half + 1) * P]
                    else:
                        need(act, s["pj_mm"], t.count(1))
                        o = dst[0][:, :, :]
                    act.activation(o, bank(i, kind).rearrange("p (k n) -> p k n", k=KT), ACT.Copy)\
                        .then_inc(s[kind + "_hi"], 1)
                t = At(c, i - 3)
                if t.within(NT):
                    for j in range(2):
                        act.wait_ge(s["pt_mm"], t.count(4, j + 1))
                        need(act, s["pv_mm"], t.count(1))
                        act.activation(pT[:, j, :, :],
                                       bank(i, "pt", j)[0:SK, :].rearrange("p (g n) -> p g n", g=4),
                                       ACT.Copy).then_inc(s["pt_act"], 1)
                if i % 2 == 0 and At(c, i - 2).within(NT):
                    t = At(c, i - 2)
                    for m in range(KT):
                        if m % 2 == 0:
                            act.wait_ge(s["q_mm"], t.count(1, m // 2 + 1))
                        need(act, s["s_mm"], t.count(1))
                        act.activation(qT[:, m, :], bank(i, "q", m // 2)[:, (m % 2) * 256:(m % 2) * 256 + 256],
                                       ACT.Identity, bias=bq[:, m:m + 1]).then_inc(s["q_evac"], 1)
                t = At(c, i - 4)
                if t.within(NT):
                    act.wait_ge(s["zt_mm"], t.count(1, 1))
                    need(act, s["z_lo"], t.count(1))
                    for k in range(KT):
                        act.activation(y[:, k, :], bank(i, "zt")[:, k * P:(k + 1) * P], ACT.Identity,
                                       bias=ln1b[:, k:k + 1], scale=ln1w[:, k:k + 1]).then_inc(s["y_done"], 1)
                    act.wait_ge(s["y_done"], t.count(4, 4))
                    need(act, s["qkv_mm"], t.count(2))
                    act.activation(zT[0][:, :, :], y[:, :, :], ACT.Copy).then_inc(s["z_hi"], 1)
                t = At(c, i - 8)
                if t.within(NT):
                    need(act, s["base_done"], t.count(1, 1))
                    need(act, s["z2_done"], t.count(1, 1))
                    act.dma_start(out2d[bass.ds(row0(t), P), :], x2[:, t.s, :]).then_inc(base_out, 16)
                    act.dma_start(z2d[bass.ds(row0(t), P), :], z2[:, :]).then_inc(z2_out, 16)
                    act.wait_ge(s["z2t_mm"], t.count(1, 1))
                    for k in range(KT):
                        act.activation(y2[:, k, :], bank(i, "z2t")[:, k * P:(k + 1) * P], ACT.Identity,
                                       bias=ln2b[:, k:k + 1], scale=ln2w[:, k:k + 1]).then_inc(s["y2_done"], 1)
                t = At(c, i - 5)
                if t.within(NT):
                    need(act, s["sm_sub"], t.count(1, 1))
                    act.activation(pa[:, t.s % 2, :, 0:t.s + 1], sc[:, :, 0:t.s + 1], ACT.Exp, scale=SCALE)\
                        .then_inc(s["sm_exp"], 1)
                for first in (0, 2):
                    t = At(c, i - 2)
                    if t.within(NT):
                        if first == 0:
                            act.wait_ge(s["nm_done"], t.count(1, 1))
                            need(act, s["pt_mm"], t.count(4))
                            need(act, s["rec_done"], t.count(1))
                        for b in (first, first + 1):
                            for g in range(4):
                                h = 4 * b + g
                                e = act.activation(pr[:, b, g, :], psS[:, b, g * SK:(g + 1) * SK], ACT.Exp,
                                                   bias=nm[:, h:h + 1], scale=SCALE, accum_out=den[:, h:h + 1])
                            e.then_inc(s["exp_done"], 1)
                    t = At(c, i - 3)
                    if first == 0 and t.within(NT):
                        act.wait_ge(s["pv_mm"], t.count(1, 1))
                        need(act, s["wo_mm"], t.count(1))
                        act.activation(oT[0][:, :, :], bank(i, "pv").rearrange("p (k n) -> p k n", k=KT), ACT.Copy)\
                            .then_inc(s["o_hi"], 1)
                t = At(c, i - 8)
                if t.within(NT):
                    act.wait_ge(s["lg_mm"], t.count(1, 1))
                    act.activation(logits[:, bass.ds(t.s * NC + t.chunk, 1), :],
                                   bank(i, "lg")[:, 0:E].unsqueeze(1), ACT.Copy).then_inc(s["lg_evac"], 1)
                t = At(c, i - 4)
                if t.within(NT):
                    act.wait_ge(s["qkv_mm"], t.count(2, 1))
                    need(act, s["prods_k"], t.count(NKV, -NKV))
                    act.activation(qb[:, t.s % 2, :], bank(i, "qkv", 0), ACT.Copy).then_inc(s["qkv_evac"], 1)
                    act.wait_ge(s["qkv_mm"], t.count(2, 2))
                    need(act, s["v_kept"], t.count(1, -1))
                    act.activation(kvs[:, t.s % 2, :], bank(i, "qkv", 1)[:, 0:2 * P], ACT.Copy)\
                        .then_inc(s["qkv_evac"], 1)

            pipeline(act, step)
            act.wait_ge(base_out, 16 * NT)
            act.wait_ge(z2_out, 16 * NT)

        @block.vector
        def _(dve):
            def stats(src, bn, mv, chain, count):
                dve.bn_stats(bn[:, :], src).then_inc(chain, 1)
                need_apart(dve, (chain, count))
                return dve.bn_aggr(mv, bn[:, :])

            def low_half(c, i, lag, kind, parts, hi, lo):
                t = At(c, i - lag)
                if t.within(NT):
                    dve.wait_ge(s[hi], t.count(1, 1))
                    half = slice((t.s % 2) * P, (t.s % 2) * P + P) if kind == "xt" else slice(0, P)
                    dve.tensor_tensor(parts[1][:, :, half], bank(i, kind).rearrange("p (k n) -> p k n", k=KT),
                                      parts[0][:, :, half].bitcast(F32), ALU.subtract).then_inc(s[lo], 1)

            def key_sums(t, groups):
                n = t.s + 1
                for g in groups:
                    need(dve, s["prods_k"], t.count(NKV, g + 1))
                    need(dve, s["sm_exp"], t.count(1))
                    dve.tensor_reduce(sc[:, g * HQ:(g + 1) * HQ, 0:n].rearrange("p h t -> p t h"),
                                      prod_k[:, g % 2, 0:n * P].rearrange("p (t h d) -> p t h d", t=n, h=HQ),
                                      X, ALU.add).then_inc(s["sums_k"], 1)

            def value_sums(t, groups):
                n = t.s + 1
                for g in groups:
                    need(dve, s["prods_v"], t.count(NKV, g + 1))
                    need(dve, s["at_mm"], t.count(1))
                    dve.tensor_reduce(ao[:, g * P:(g + 1) * P],
                                      prod_v[:, g % 2, 0:n * P].rearrange("p (t f) -> p f t", t=n),
                                      X, ALU.add).then_inc(s["sums_v"], 1)

            def step(c, i):
                tq, tv = At(c, i - 5), At(c, i - 6)
                n = tq.s + 1
                t = At(c, i - 4)
                if t.within(NT):
                    dve.wait_ge(s["wo_mm"], t.count(1, 1))
                    dve.wait_ge(s["bias_x"], t.count(1, 1))
                    need(dve, s["base_done"], t.count(1, -3))
                    dve.tensor_tensor(x2[:, t.s, :], bank(i - 1, "wo"), xc[:, t.s % 2, :], ALU.add)\
                       .then_inc(s["x2_done"], 1)
                    dve.wait_ge(s["x2_done"], t.count(1, 1))
                    stats(x2[:, t.s, :], bnc, mvc[:, t.s, :], s["chain_c"], t.count(1, 1)).then_inc(s["stat_c"], 1)
                low_half(c, i, 7, "at", aT, "at_hi", "at_lo")
                low_half(c, i, 1, "xt", xT, "xt_hi", "xt_lo")
                t = At(c, i - 3)
                if t.within(NT):
                    for j in range(2, 4):
                        dve.wait_ge(s["pt_mm"], t.count(4, j + 1))
                        need(dve, s["pv_mm"], t.count(1))
                        dve.tensor_copy(pT[:, j, :, :],
                                        bank(i, "pt", j)[0:SK, :].rearrange("p (g n) -> p g n", g=4))\
                           .then_inc(s["pt_dve"], 1)
                if tq.within(NT):
                    key_sums(tq, (0,))
                t = At(c, i - 4)
                if t.within(NT):
                    dve.wait_ge(s["rstd_c"], t.count(1, 1))
                    need(dve, s["zt_mm"], t.count(1))
                    dve.tensor_scalar(z[:, :], x2[:, t.s, :], mvc[:, t.s, 0:1], rcc[:, t.s % 2:t.s % 2 + 1],
                                      ALU.subtract, ALU.mult).then_inc(s["z_done"], 1)
                if tq.within(NT):
                    key_sums(tq, (1, 2))
                t = At(c, i - 7)
                if t.within(NT):
                    need(dve, s["base_done"], t.count(1))
                    dve.tensor_scalar(h1[:, :], x2[:, t.s, :], mvc[:, t.s, 0:1], rc[:, t.s:t.s + 1], ALU.subtract,
                                      ALU.mult).then_inc(s["h0_done"], 1)
                    dve.wait_ge(s["h0_done"], t.count(1, 1))
                    dve.wait_ge(s["pj_mm"], t.count(1, 1))
                    dve.tensor_tensor(h1[:, :], bank(i, "pj"), h1[:, :], ALU.add).then_inc(s["h1_done"], 1)
                    dve.wait_ge(s["h1_done"], t.count(1, 1))
                    stats(h1[:, :], bnf, mvf[:, t.s % 2, :], s["chain_f"], t.count(1, 1)).then_inc(s["stat_f"], 1)
                if tq.within(NT):
                    key_sums(tq, (3,))
                    need(dve, s["sums_k"], tq.count(NKV, NKV))
                    dve.tensor_reduce(att_small[:, 0, :], sc[:, :, 0:n], X, ALU.max).then_inc(s["sm_chain"], 1)
                    need(dve, s["sm_chain"], tq.count(3, 1))
                    dve.tensor_tensor(sc[:, :, 0:n], sc[:, :, 0:n], bc(att_small[:, 0, :], 2, [P, H, n]),
                                      ALU.subtract).then_inc(s["sm_sub"], 1)
                t = At(c, i - 2)
                if t.within(NT):
                    dve.wait_ge(s["s_mm"], t.count(1, 1))
                    scores = psS[:, :, 0:4 * SK].rearrange("p b (g k) -> p b g k", g=4)
                    if (isinstance(c, int) and c == 0) or t.off < 0:
                        m = mask[:, bass.ds(t.chunk, 1), :].unsqueeze(1).to_broadcast([P, 4, 4, SK])
                        dve.tensor_tensor(scores, scores, m, ALU.add).then_inc(s["masked"], 1)
                        dve.wait_ge(s["masked"], c * 2 + (i - 1 if isinstance(c, int) and c == 0 else 5 + i))
                    need(dve, s["exp_done"], t.count(4))
                    dve.tensor_reduce(nm[:, :].rearrange("p (b g) -> p b g", b=4), scores, X, ALU.max)\
                       .then_inc(s["mx_done"], 1)
                    dve.wait_ge(s["mx_done"], t.count(1, 1))
                    dve.tensor_scalar(nm[:, :], nm[:, :], -SCALE, None, ALU.mult).then_inc(s["nm_done"], 1)
                if tv.within(NT):
                    value_sums(tv, (0,))
                if tq.within(NT):
                    need(dve, s["sm_exp"], tq.count(1, 1))
                    dve.tensor_reduce(att_small[:, 1, :], pa[:, tq.s % 2, :, 0:n], X, ALU.add)\
                       .then_inc(s["sm_chain"], 1)
                    need(dve, s["sm_chain"], tq.count(3, 2))
                    dve.reciprocal(att_small[:, 2, :], att_small[:, 1, :]).then_inc(s["sm_chain"], 1)
                    need(dve, s["sm_chain"], tq.count(3, 3))
                    dve.tensor_tensor(pa[:, tq.s % 2, :, 0:n], pa[:, tq.s % 2, :, 0:n],
                                      bc(att_small[:, 2, :], 2, [P, H, n]), ALU.mult).then_inc(s["sm_p"], 1)
                low_half(c, i, 3, "pv", oT, "o_hi", "o_lo")
                t = At(c, i - 7)
                if t.within(NT):
                    dve.wait_ge(s["rstd_f"], t.count(1, 1))
                    need(dve, z2_out, t.count(16))
                    need(dve, base_out, t.count(16))
                    need(dve, s["z2t_mm"], t.count(1))
                    dve.tensor_scalar(z2[:, :], h1[:, :], mvf[:, t.s % 2, 0:1], rf[:, t.s % 2:t.s % 2 + 1],
                                      ALU.subtract, ALU.mult).then_inc(s["z2_done"], 1)
                t = At(c, i)
                if t.within(NT):
                    dve.wait_ge(xa_in[i % 2], t.turns(2, 16, 16))
                    stats(xa[:, i % 2, :], bnx, mvx[:, i % 2, :], s["chain_x"], t.count(1, 1)).then_inc(s["stat_x"], 1)
                if tv.within(NT):
                    value_sums(tv, (1,))
                t = At(c, i - 2)
                if t.within(NT):
                    dve.wait_ge(s["exp_done"], t.count(4, 4))
                    need(dve, s["shared"], t.count(1))
                    dve.reciprocal(rec[:, :], den[:, :]).then_inc(s["rec_done"], 1)
                    dve.wait_ge(s["rec_done"], t.count(1, 1))
                    shares = pr[:, :, :, :].rearrange("p b g k -> p (b g) k")
                    dve.tensor_tensor(shares, shares, bc(rec[:, :], 2, [P, H, SK]), ALU.mult)\
                       .then_inc(s["shared"], 1)
                t = At(c, i)
                if t.within(NT):
                    dve.wait_ge(s["rstd_x"], t.count(1, 1))
                    dve.tensor_scalar(xa[:, i % 2, :], xa[:, i % 2, :], mvx[:, i % 2, 0:1], rx[:, i % 2:i % 2 + 1],
                                      ALU.subtract, ALU.mult).then_inc(s["normed_x"], 1)
                if tv.within(NT):
                    value_sums(tv, (2, 3))

            pipeline(dve, step)

        @block.tensor
        def _(pe):
            def transposes(c, i, lag, kind, ready, count, src, mm):
                t = At(c, i - lag)
                if t.within(NT):
                    pe.wait_ge(s[ready], t.count(*count))
                    bank_free(pe, c, i, kind)
                    for k in range(KT):
                        last = pe.transpose(bank(i, kind)[:, k * P:(k + 1) * P], src(t)[:, k * P:(k + 1) * P],
                                            ident[:, :])
                    last.then_inc(s[mm], 1)

            def step(c, i):
                transposes(c, i, 7, "at", "sums_v", (NKV, NKV), lambda t: ao[:, :], "at_mm")
                transposes(c, i, 1, "xt", "normed_x", (1, 1), lambda t: xa[:, t.s % 2, :], "xt_mm")
                t = At(c, i - 3)
                if t.within(NT):
                    pe.wait_ge(s["shared"], t.count(1, 1))
                    for b in range(4):
                        bank_free(pe, c, i, "pt", b)
                        for g in range(4):
                            last = pe.transpose(bank(i, "pt", b)[0:SK, g * P:(g + 1) * P], pr[:, b, g, :],
                                                ident[:, :])
                        last.then_inc(s["pt_mm"], 1)
                if i % 2 == 0 and At(c, i - 2).within(NT):
                    t = At(c, i - 2)
                    pe.wait_ge(s["xt_lo"], t.count(1, 2))
                    for j in range(2):
                        bank_free(pe, c, i, "q", j)
                        for m in range(2):
                            cols = slice((2 * j + m) * P, (2 * j + m + 1) * P)
                            last = split_matmuls(pe, bank(i, "q", j)[:, m * 256:(m + 1) * 256],
                                                 lambda h, k: wq[h][:, k, cols], lambda h, k: xT[h][:, k, :])
                        last.then_inc(s["q_mm"], 1)
                transposes(c, i, 8, "z2t", "z2_done", (1, 1), lambda t: z2[:, :], "z2t_mm")
                transposes(c, i, 4, "zt", "z_done", (1, 1), lambda t: z[:, :], "zt_mm")
                t = At(c, i - 7)
                if t.within(NT):
                    pe.wait_ge(s["at_lo"], t.count(1, 1))
                    bank_free(pe, c, i, "pj")
                    split_matmuls(pe, bank(i, "pj"), lambda h, k: aT[h][:, k, :], lambda h, k: wpj[h][:, k, :])\
                        .then_inc(s["pj_mm"], 1)
                t = At(c, i - 2)
                if t.within(NT):
                    pe.wait_ge(s["q_evac"], At(c, i - 2 - t.s % 2).count(2, 4))
                    for g in range(4):
                        for b in range(4):
                            if g == 0:
                                need(pe, s["exp_done"], t.count(4, b - 3))
                            rows = slice(b * DH, (b + 1) * DH)
                            last = pe.matmul(psS[:, b, g * SK:(g + 1) * SK],
                                             qT[rows, g, (t.s % 2) * P:(t.s % 2) * P + P],
                                             kT[rows, g, t.s * SK:(t.s + 1) * SK], start=True, stop=True)
                    last.then_inc(s["s_mm"], 1)
                t = At(c, i - 3)
                if t.within(NT):
                    pe.wait_ge(s["pt_act"], t.count(2, 2))
                    pe.wait_ge(s["pt_dve"], t.count(2, 2))
                    bank_free(pe, c, i, "pv")
                    for g in range(4):
                        for b in range(4):
                            last = pe.matmul(bank(i, "pv")[b * DH:(b + 1) * DH, g * P:(g + 1) * P],
                                             va[:, t.s, 4 * g + b, :], pT[:, b, g, :], start=True, stop=True)
                    last.then_inc(s["pv_mm"], 1)
                t = At(c, i - 8)
                if t.within(NT):
                    pe.wait_ge(s["y2_done"], t.count(4, 4))
                    bank_free(pe, c, i, "lg")
                    for k in range(KT):
                        last = pe.matmul(bank(i, "lg")[:, 0:E], y2[:, k, :], wr[:, k, :], start=k == 0,
                                         stop=k == KT - 1)
                    last.then_inc(s["lg_mm"], 1)
                t = At(c, i - 4)
                if t.within(NT):
                    pe.wait_ge(s["z_lo"], t.count(1, 1))
                    for j, (c0, c1) in enumerate(((0, D), (D, QKV))):
                        bank_free(pe, c, i, "qkv", j)
                        split_matmuls(pe, bank(i, "qkv", j)[:, 0:c1 - c0], lambda h, k: zT[h][:, k, :],
                                      lambda h, k: wqkv[h][:, k, c0:c1]).then_inc(s["qkv_mm"], 1)
                t = At(c, i - 3)
                if t.within(NT):
                    pe.wait_ge(s["o_lo"], t.count(1, 1))
                    bank_free(pe, c, i, "wo")
                    split_matmuls(pe, bank(i, "wo"), lambda h, k: oT[h][:, k, :], lambda h, k: wo[h][:, k, :])\
                        .then_inc(s["wo_mm"], 1)

            pipeline(pe, step)



def build_routing(nc, logits, tables, sb, sem):
    ranks = sb("ranks", [P, E])
    ramp = sb("ramp", [P, P])
    number = sb("number", [P, NT])
    before = sb("before", [P, P])
    ones = sb("ones", [P, P])
    ints = sb("ints", [P, P], I32)
    ints2 = sb("ints2", [P, NT], I32)
    ints3 = sb("ints3", [P, E], I32)
    best = sb("best", [P, 2, NT])
    first = sb("first", [P, 2, NT])
    eq = sb("eq", [P, NT, E])
    hot = sb("hot", [P, 2, NT, E])
    rest = sb("rest", [P, NT, E])
    both = sb("both", [P, NT, E])
    seen = sb("seen", [P, 2, NT, E])
    place = sb("place", [P, NT, E])
    share = sb("share", [P, 2, NT])
    diff = sb("diff", [P, NT])
    ex = sb("ex", [P, NT])
    den = sb("den", [P, NT])
    within = sb("within", [P, 2, NT])
    wi = sb("wi", [P, 2, NT], I32)
    qi = sb("qi", [P, 2, NT], I32)
    ri = sb("ri", [P, 2, NT], I32)
    blk = sb("blk", [P, 2, NT])
    row = sb("row", [P, 2, NT])
    over = sb("over", [P, 2, NT])
    hot_row = sb("hot_row", [P, 4, P])
    hot_blk = sb("hot_blk", [P, 4, 2, NBLK])
    ids = sb("ids", [P, NBLK])
    idc = sb("idc", [P, NBLK])
    with ExitStack() as st:
        pp = st.enter_context(nc.psum_tensor("prefix_ps", [P, 2, 512], F32))
        pt = st.enter_context(nc.psum_tensor("table_ps", [P, 2 * NBLK], F32))
        made, chain, sm, expd, prefixed, hots, tabled = (
            sem(n) for n in ("r_made", "r_chain", "r_diff", "r_exp", "r_prefixed", "r_hots", "r_tabled"))
        counted = sem("r_counted")
        block = st.enter_context(nc.Block())

        @block.gpsimd
        def _(pool):
            pool.iota(ints[:, :], [[1, P]], base=0, channel_multiplier=0).then_inc(made, 1)
            pool.iota(ints2[:, :], [[P, NT]], base=1, channel_multiplier=1).then_inc(made, 1)
            pool.iota(ints3[:, :], [[-1, E]], base=E, channel_multiplier=0).then_inc(made, 1)
            pool.memset(before[:, :], 1.0).then_inc(made, 1)
            pool.memset(ones[:, :], 1.0).then_inc(made, 1)
            pool.wait_ge(made, 5)
            pool.tensor_copy(ramp[:, :], ints[:, :]).then_inc(made, 1)
            pool.tensor_copy(number[:, :], ints2[:, :]).then_inc(made, 1)
            pool.tensor_copy(ranks[:, :], ints3[:, :]).then_inc(made, 1)
            pool.affine_select(out=before[:, :], in_=before[:, :], compare_op=ALU.is_gt, fill=0.0, base=0,
                               pattern=[[1, P]], channel_multiplier=-1).then_inc(made, 1)

        @block.scalar
        def _(act):
            act.wait_ge(sm, 1)
            act.activation(ex[:, :], diff[:, :], ACT.Exp).then_inc(expd, 1)

        @block.vector
        def _(dve):
            steps = [0]

            def link(instruction):
                steps[0] += 1
                instruction.then_inc(chain, 1)
                dve.wait_ge(chain, steps[0])

            dve.wait_ge(made, 9)
            shape = [P, NT, E]
            for k in range(2):
                src = logits if k == 0 else rest
                link(dve.tensor_reduce(best[:, k, :], src[:, :, :], X, ALU.max))
                link(dve.tensor_tensor(eq[:, :, :], src[:, :, :], bc(best[:, k, :], 2, shape), ALU.is_equal))
                link(dve.tensor_tensor(eq[:, :, :], eq[:, :, :], bc(ranks[:, :], 1, shape), ALU.mult))
                link(dve.tensor_reduce(first[:, k, :], eq[:, :, :], X, ALU.max))
                link(dve.tensor_tensor(hot[:, k, :, :], bc(first[:, k, :], 2, shape), bc(ranks[:, :], 1, shape),
                                       ALU.is_equal))
                if k == 0:
                    link(dve.scalar_tensor_tensor(rest[:, :, :], hot[:, 0, :, :], HUGE, logits[:, :, :], ALU.mult,
                                                  ALU.add))
            dve.tensor_tensor(diff[:, :], best[:, 1, :], best[:, 0, :], ALU.subtract).then_inc(sm, 1)
            dve.tensor_tensor(both[:, :, :], hot[:, 0, :, :], hot[:, 1, :, :], ALU.add).then_inc(counted, 1)
            dve.wait_ge(expd, 1)
            link(dve.tensor_scalar(den[:, :], ex[:, :], 1.0, None, ALU.add))
            link(dve.reciprocal(share[:, 0, :], den[:, :]))
            link(dve.tensor_tensor(share[:, 1, :], ex[:, :], share[:, 0, :], ALU.mult))
            dve.wait_ge(prefixed, 1)
            link(dve.tensor_copy(seen[:, 0, :, :], pp[:, 1, 0:NT * E].rearrange("p (t e) -> p t e", e=E)))
            src, sh = 0, 1
            while sh < NT:
                dst = 1 - src
                link(dve.tensor_tensor(seen[:, dst, sh:NT, :], seen[:, src, sh:NT, :], seen[:, src, 0:NT - sh, :],
                                       ALU.add))
                link(dve.tensor_copy(seen[:, dst, 0:sh, :], seen[:, src, 0:sh, :]))
                src, sh = dst, 2 * sh
            link(dve.tensor_tensor(place[:, :, :], pp[:, 0, 0:NT * E].rearrange("p (t e) -> p t e", e=E),
                                   seen[:, src, :, :], ALU.add))
            link(dve.tensor_tensor(place[:, :, :], place[:, :, :],
                                   pp[:, 1, 0:NT * E].rearrange("p (t e) -> p t e", e=E), ALU.subtract))
            for k in range(2):
                link(dve.tensor_tensor(eq[:, :, :], hot[:, k, :, :], place[:, :, :], ALU.mult))
                link(dve.tensor_reduce(within[:, k, :], eq[:, :, :], X, ALU.add))
            link(dve.tensor_copy(wi[:, :, :], within[:, :, :]))
            link(dve.tensor_scalar(qi[:, :, :], wi[:, :, :], 7, None, ALU.logical_shift_right))
            link(dve.tensor_scalar(ri[:, :, :], wi[:, :, :], P - 1, None, ALU.bitwise_and))
            link(dve.tensor_copy(blk[:, :, :], qi[:, :, :]))
            link(dve.tensor_copy(row[:, :, :], ri[:, :, :]))
            link(dve.tensor_scalar(over[:, :, :], within[:, :, :], float(CAP), 1000.0, ALU.is_ge, ALU.mult))
            link(dve.tensor_tensor(blk[:, :, :], blk[:, :, :], over[:, :, :], ALU.add))
            link(dve.tensor_scalar(over[:, :, :], first[:, :, :], -float(BPE), float(E * BPE), ALU.mult, ALU.add))
            link(dve.tensor_tensor(blk[:, :, :], blk[:, :, :], over[:, :, :], ALU.add))
            for k in range(2):
                with dve.Fori(0, NT // 4) as c:
                    for j in range(4):
                        col = bass.ds(c * 4 + j, 1)
                        dve.wait_ge(tabled, c * 4 + (NT * k + j + 1))
                        dve.tensor_scalar(hot_row[:, j, :], ramp[:, :], row[:, k, col], None, ALU.is_equal)
                        dve.tensor_scalar(hot_blk[:, j, 0, :], ramp[:, 0:NBLK], blk[:, k, col], number[:, col],
                                          ALU.is_equal, ALU.mult)
                        dve.tensor_scalar(hot_blk[:, j, 1, :], ramp[:, 0:NBLK], blk[:, k, col],
                                          share[:, k, col], ALU.is_equal, ALU.mult).then_inc(hots, 1)
            dve.wait_ge(tabled, 2 * NT + 4)
            dve.tensor_copy(tables["shares"][:, :], pt[:, NBLK:2 * NBLK])
            link(dve.tensor_scalar(ids[:, :], pt[:, 0:NBLK], 0.0, 2.0 * N, ALU.is_equal, ALU.mult))
            link(dve.scalar_tensor_tensor(idc[:, :], pt[:, 0:NBLK], -1.0, ids[:, :], ALU.add, ALU.add))
            dve.tensor_copy(tables["rows"][:, :], idc[:, :])

        @block.tensor
        def _(pe):
            pe.sem_inc(tabled, 4)
            pe.wait_ge(made, 9)
            pe.wait_ge(counted, 1)
            flat = both[:, :, :].rearrange("p t e -> p (t e)")
            pe.matmul(pp[:, 0, 0:NT * E], before[:, :], flat, start=True, stop=True)
            pe.matmul(pp[:, 1, 0:NT * E], ones[:, :], flat, start=True, stop=True).then_inc(prefixed, 1)
            for n in range(2 * NT):
                pe.wait_ge(hots, n + 1)
                pe.matmul(pt[:, :], hot_row[:, n % 4, :], hot_blk[:, n % 4, :, :].rearrange("p a b -> p (a b)"),
                          start=n == 0, stop=n == 2 * NT - 1).then_inc(tabled, 1)



def build_experts(nc, a, out2d, z2d, ident, ln2w, ln2b, tables, sb, sem):
    w1 = [[sb(f"w1_{p}{h}", [P, KT, F], F32R) for h in range(2)] for p in range(2)]
    w2 = [[sb(f"w2_{p}{h}", [P, FT, D], F32R) for h in range(2)] for p in range(2)]
    raw = sb("raw", [P, 2, F])
    xg = sb("xg", [P, GB, D])
    yk = sb("yk", [P, 2, GB * P])
    xT = [sb("gT_hi", [P, KT, GB * P], F32R), sb("gT_lo", [P, KT, GB * P], F32R)]
    gl = sb("gl", [P, 2, 2 * GB * P])
    hT = [[sb(f"hT_{p}{h}", [P, FT, GB * P], F32R) for h in range(2)] for p in range(2)]
    og = sb("og", [P, GB, D])
    idx = sb("idx", [P, GPE, GB], I32)
    W = GB * P
    CH = 8
    PER = 2 * GPE

    with ExitStack() as st:
        pT = st.enter_context(nc.psum_tensor("gather_ps", [P, GB, 512], F32))
        pH = st.enter_context(nc.psum_tensor("hidden_ps", [P, 4, 512], F32))
        pY = st.enter_context(nc.psum_tensor("expert_ps", [P, GB, 512], F32))
        raw_in = [sem(f"raw_in{i}") for i in range(2)]
        names = ("w_hi w_lo cleared copied gathered fetched scattered xt_mm yk_done xt_hi xt_lo fc1_mm gelu h_hi h_lo "
                 "fc2_mm summed").split()
        s = {n: sem("e_" + n) for n in names}
        block = st.enter_context(nc.Block())

        def pipeline(engine, step):
            for i in range(PER):
                step(0, i)
            with engine.Fori(1, NG // PER) as c:
                for i in range(PER):
                    step(c, i)
            for i in range(PER):
                step(NG // PER, i)

        def col(g, b):
            return bass.ds(g.count(GB, b), 1)

        def weight_piece(p, half, j):
            if j < 4:
                return w1[p][half][:, j, :]
            return w2[p][half][:, 2 * (j - 4):2 * (j - 4) + 2, :].rearrange("p f n -> p (f n)")

        @block.sync
        def _(sp):
            def load(e, c, p, j):
                n = At(c, CH * p + j, 2 * CH)
                need(sp, s["w_lo"], n.count(1, -1))
                if j < 4:
                    sp.dma_start(raw[:, j % 2, :], a["L0_ffn_moe_w1"].rearrange("e (k p) f -> (e k) p f", p=P)
                                 [bass.ds(e * KT + j, 1), :, :].rearrange("a p f -> (a p) f"))\
                      .then_inc(raw_in[j % 2], 16)
                else:
                    src = a["L0_ffn_moe_w2"].rearrange("e (q f p) n -> (e q) p f n", f=2, p=P)
                    sp.dma_start(raw[:, j % 2, :].rearrange("p (f n) -> p f n", f=2),
                                 src[bass.ds(e * 4 + (j - 4), 1), :, :, :].rearrange("a p f n -> (a p) f n"))\
                      .then_inc(raw_in[j % 2], 16)

            for p in range(2):
                for j in range(CH):
                    load(p, 0, p, j)
            with sp.Fori(1, E // 2) as c:
                for p in range(2):
                    for j in range(CH):
                        load(c * 2 + p, c, p, j)

        def weights_free(engine, c, p, j):
            if isinstance(c, int) and c == 0:
                return
            last = At(c, GPE * p - GPE - 1, PER)
            if j < 4:
                engine.wait_ge(s["fc1_mm"], last.count(4, 4))
            else:
                engine.wait_ge(s["fc2_mm"], last.count(GB, GB))

        def split_pieces(c, i):
            if isinstance(c, int) and c == E // 2:
                return []
            p, g = divmod(i, GPE)
            at = (0, 2, 4, 6, 7, 8)
            return [(c, p, j) for j in range(at[g], at[g + 1])]

        @block.gpsimd
        def _(pool):
            def low(c, p, j):
                n = At(c, CH * p + j, 2 * CH)
                pool.wait_ge(s["w_hi"], n.count(1, 1))
                weights_free(pool, c, p, j)
                pool.tensor_tensor(weight_piece(p, 1, j), raw[:, j % 2, :],
                                   weight_piece(p, 0, j).bitcast(F32), ALU.subtract).then_inc(s["w_lo"], 1)

            def rows(g, k):
                return bass.IndirectOffsetOnAxis(ap=idx[:, g.s % GPE, k:k + 1], axis=0)

            def step(c, i):
                g = At(c, i - 5, PER)
                if g.within(NG):
                    pool.tensor_copy(idx[:, g.s % GPE, :], tables["rows"][:, bass.ds(g.count(GB), GB)])\
                        .then_inc(s["copied"], 1)
                    need_apart(pool, (s["copied"], g.count(1, 1)), (s["xt_mm"], g.count(1)))
                    for k in range(GB):
                        pool.indirect_dma_start(out=xg[:, k, :], out_offset=None, in_=z2d[:, :],
                                                in_offset=rows(g, k), bounds_check=N - 1,
                                                oob_is_err=False).then_inc(s["gathered"], 16)
                g = At(c, i - 7, PER)
                if g.within(NG):
                    need_apart(pool, (s["scattered"], g.count(32)))
                    for k in range(GB):
                        pool.indirect_dma_start(out=og[:, k, :], out_offset=None, in_=out2d[:, :],
                                                in_offset=rows(g, k), bounds_check=N - 1,
                                                oob_is_err=False).then_inc(s["fetched"], 16)
                for piece in split_pieces(c, i):
                    low(*piece)
                if g.within(NG):
                    need_apart(pool, (s["summed"], g.count(GB, GB)))
                    for k in range(GB):
                        pool.indirect_dma_start(out=out2d[:, :], out_offset=rows(g, k), in_=og[:, k, :],
                                                in_offset=None, bounds_check=N - 1,
                                                oob_is_err=False).then_inc(s["scattered"], 16)

            pool.memset(xg[:, :, :], 0.0).then_inc(s["cleared"], 1)
            pool.memset(og[:, :, :], 0.0).then_inc(s["cleared"], 1)
            pool.wait_ge(s["cleared"], 2)
            pipeline(pool, step)
            pool.wait_ge(s["scattered"], 32 * NG)

        @block.scalar
        def _(act):
            def high(c, p, j):
                n = At(c, CH * p + j, 2 * CH)
                act.wait_ge(raw_in[j % 2], At(c, (CH * p + j) // 2, CH).count(16, 16))
                weights_free(act, c, p, j)
                act.activation(weight_piece(p, 0, j), raw[:, j % 2, :], ACT.Copy).then_inc(s["w_hi"], 1)

            def step(c, i):
                g = At(c, i - 6, PER)
                if g.within(NG):
                    for q in range(4):
                        act.wait_ge(s["fc1_mm"], g.count(4, q + 1))
                        need(act, s["h_lo"], g.count(4, q - 1))
                        act.activation(gl[:, q % 2, :], pH[:, q, :], ACT.Gelu_apprx_tanh).then_inc(s["gelu"], 1)
                g = At(c, i - 5, PER)
                if g.within(NG):
                    for k in range(KT):
                        act.wait_ge(s["yk_done"], g.count(KT, k + 1))
                        need(act, s["fc1_mm"], g.count(4))
                        act.activation(xT[0][:, k, :], yk[:, k % 2, :], ACT.Copy).then_inc(s["xt_hi"], 1)
                for piece in split_pieces(c, i):
                    high(*piece)

            pipeline(act, step)

        @block.vector
        def _(dve):
            def step(c, i):
                g = At(c, i - 6, PER)
                if g.within(NG):
                    par = g.s % 2
                    for q in range(4):
                        dve.wait_ge(s["gelu"], g.count(4, q + 1))
                        need(dve, s["fc2_mm"], g.count(GB, -GB))
                        o = [hT[par][h][:, 2 * q:2 * q + 2, :].rearrange("p f n -> p (f n)") for h in range(2)]
                        dve.tensor_copy(o[0], gl[:, q % 2, :]).then_inc(s["h_hi"], 1)
                        dve.wait_ge(s["h_hi"], g.count(4, q + 1))
                        dve.tensor_tensor(o[1], gl[:, q % 2, :], o[0].bitcast(F32), ALU.subtract)\
                           .then_inc(s["h_lo"], 1)
                g = At(c, i - 5, PER)
                if g.within(NG):
                    dve.wait_ge(s["xt_mm"], g.count(1, 1))
                    for k in range(KT):
                        need(dve, s["xt_lo"], g.count(KT, k - 1))
                        need(dve, s["xt_hi"], g.count(KT, k - 1))
                        dve.tensor_scalar(yk[:, k % 2, :].rearrange("p (b n) -> p b n", b=GB),
                                          pT[:, :, k * P:(k + 1) * P], ln2w[:, k:k + 1], ln2b[:, k:k + 1], ALU.mult,
                                          ALU.add).then_inc(s["yk_done"], 1)
                        dve.wait_ge(s["xt_hi"], g.count(KT, k + 1))
                        dve.tensor_tensor(xT[1][:, k, :], yk[:, k % 2, :], xT[0][:, k, :].bitcast(F32),
                                          ALU.subtract).then_inc(s["xt_lo"], 1)
                g = At(c, i - 7, PER)
                if g.within(NG):
                    dve.wait_ge(s["fetched"], g.count(32, 32))
                    for k in range(GB):
                        dve.wait_ge(s["fc2_mm"], g.count(GB, k + 1))
                        dve.scalar_tensor_tensor(og[:, k, :], pY[:, k, :], tables["shares"][:, col(g, k)], og[:, k, :],
                                                 ALU.mult, ALU.add).then_inc(s["summed"], 1)

            pipeline(dve, step)

        @block.tensor
        def _(pe):
            passes = ((0, 0), (0, 1), (1, 0))

            def first_row(g):
                return pe.value_load(tables["rows"][0:1, bass.ds(g.count(GB), 1)], min_val=0, max_val=2 * N)

            def step(c, i):
                g = At(c, i - 6, PER)
                if g.within(NG):
                    row = first_row(g)
                    p = g.s // GPE
                    if g.s % GPE == 0:
                        pe.wait_ge(s["w_lo"], c * (2 * CH) + (CH * (g.off // GPE) + 4))
                    pe.wait_ge(s["xt_lo"], g.count(KT, KT))
                    with pe.If(row < N):
                        for q in range(4):
                            need(pe, s["gelu"], g.count(4, q - 3))
                            for f in range(2):
                                cols = slice((2 * q + f) * P, (2 * q + f + 1) * P)
                                for k in range(KT):
                                    for n, (l, r) in enumerate(passes):
                                        last = pe.matmul(pH[:, q, f * W:(f + 1) * W], w1[p][l][:, k, cols],
                                                         xT[r][:, k, :], start=k == 0 and n == 0,
                                                         stop=k == KT - 1 and n == 2)
                            last.then_inc(s["fc1_mm"], 1)
                    with pe.Else():
                        need(pe, s["gelu"], g.count(4))
                        pe.sem_inc(s["fc1_mm"], 4)
                g = At(c, i - 5, PER)
                if g.within(NG):
                    pe.wait_ge(s["gathered"], g.count(32, 32))
                    need(pe, s["yk_done"], g.count(KT))
                    for k in range(GB):
                        for m in range(KT):
                            last = pe.transpose(pT[:, k, m * P:(m + 1) * P], xg[:, k, m * P:(m + 1) * P],
                                                ident[:, :])
                    last.then_inc(s["xt_mm"], 1)
                g = At(c, i - 7, PER)
                if g.within(NG):
                    row = first_row(g)
                    p = g.s // GPE
                    par = g.s % 2
                    if g.s % GPE == 0:
                        pe.wait_ge(s["w_lo"], c * (2 * CH) + (CH * (g.off // GPE) + CH))
                    pe.wait_ge(s["h_lo"], g.count(4, 4))
                    with pe.If(row < N):
                        for k in range(GB):
                            need(pe, s["summed"], g.count(GB, k - 1))
                            for f in range(FT):
                                for n, (l, r) in enumerate(passes):
                                    last = pe.matmul(pY[:, k, :], hT[par][l][:, f, k * P:(k + 1) * P],
                                                     w2[p][r][:, f, :], start=f == 0 and n == 0,
                                                     stop=f == FT - 1 and n == 2)
                            last.then_inc(s["fc2_mm"], 1)
                    with pe.Else():
                        need(pe, s["summed"], g.count(GB))
                        pe.sem_inc(s["fc2_mm"], GB)

            pipeline(pe, step)


NAMES = ["x", "ctx_1024", "L0_xattn_Wq", "L0_xattn_bq", "L0_xattn_Wk", "L0_xattn_bk", "L0_xattn_Wv",
         "L0_xattn_bv", "L0_xattn_Wo", "L0_xattn_bo", "L0_ffn_ln1_weight", "L0_ffn_ln1_bias",
         "L0_ffn_ln2_weight", "L0_ffn_ln2_bias", "L0_ffn_qkv_weight", "L0_ffn_proj_weight",
         "L0_ffn_router_weight", "L0_ffn_moe_w1", "L0_ffn_moe_w2"]


def kernel(**inputs):
    import numpy as np
    import concourse.bacc as bacc
    from concourse.bass_utils import run_bass_kernel_spmd

    nc = bacc.Bacc("TRN2", target_bir_lowering=False, num_devices=1)
    arrays, aps = {}, {}
    for name in NAMES:
        v = np.ascontiguousarray(inputs[name])
        arrays[name + "_dram"] = v
        aps[name] = nc.dram_tensor(name + "_dram", v.shape, mybir.dt.from_np(v.dtype), kind="ExternalInput").ap()
    out = nc.dram_tensor("out_dram", (S, L, D), F32, kind="ExternalOutput").ap()
    build(nc, aps, out)
    result = run_bass_kernel_spmd(nc, [arrays], core_ids=[0])
    return result.results[0]["out_dram"]
```

```python
from contextlib import ExitStack

import concourse.bass as bass
from concourse import mybir

F32 = mybir.dt.float32
F32R = mybir.dt.float32r
I32 = mybir.dt.int32
ALU = mybir.AluOpType
ACT = mybir.ActivationFunctionType
X = mybir.AxisListType.X

P = 128
S = 8
L = 512
D = 512
KT = D // P
H = 16
DH = D // H
SK = 77
NKV = 4
HQ = H // NKV
QKV = D + 2 * NKV * DH
NC = L // P
NT = S * NC
N = S * L
E = 8
F = 1024
FT = F // P
CAP = 1280
BPE = CAP // P
NBLK = E * BPE
GB = 2
GPE = BPE // GB
NG = E * GPE
EPS = 1e-5
SCALE = float(DH) ** -0.5
MASKED = -1e30
HUGE = -3e38


class At:

    def __init__(self, c, off, period=8):
        self.c, self.off, self.period = c, off, period
        self.s = off % period
        self.chunk = c + off // period

    def count(self, k, i=0):
        if isinstance(self.c, int):
            return k * (self.period * self.c + self.off) + i
        return self.c * (k * self.period) + (k * self.off + i)

    def turns(self, ring, k=16, i=0):
        return (self.c * (k * (self.period // ring))) + (k * (self.off // ring) + i)

    def within(self, n):
        return not isinstance(self.c, int) or 0 <= self.period * self.c + self.off < n


def need(engine, sem, value):
    if not isinstance(value, int) or value > 0:
        engine.wait_ge(sem, value)


def need_apart(engine, *waits):
    waits = [(sem, v if isinstance(v, int) else engine.to_reg(v)) for sem, v in waits]
    if not all(isinstance(v, int) for _, v in waits):
        engine.wait_ge(waits[0][0], 1)
    for sem, v in waits:
        need(engine, sem, v)


def bc(ap, axis, shape):
    return ap.unsqueeze(axis).to_broadcast(shape)


def build(nc, a, out):
    x2d = a["x"].rearrange("b l d -> (b l) d")
    out2d = out.rearrange("b l d -> (b l) d")
    z2d = nc.dram_tensor("normed_tokens", [N, D], F32, kind="Internal").ap()
    keys = nc.dram_tensor("context_keys", [P, KT, S * SK], F32, kind="Internal").ap()

    whole = ExitStack()
    with whole:
        def sem(name):
            return whole.enter_context(nc.semaphore(name))

        def keeper(stack):
            def sb(name, shape, dt=F32):
                return stack.enter_context(nc.sbuf_tensor(name, shape, dt))
            return sb

        sb = keeper(whole)
        ident = sb("ident", [P, P])
        logits = sb("logits", [P, NT, E])
        ln2w = sb("ln2w", [P, KT])
        ln2b = sb("ln2b", [P, KT])
        main = ExitStack()
        with main:
            build_main(nc, a, x2d, out2d, z2d, keys, ident, logits, ln2w, ln2b, keeper(main), sem)
        tables = {"rows": sb("rows", [P, NBLK], I32), "shares": sb("shares", [P, NBLK])}
        weights = expert_weights(a, sb, sem)
        routing = ExitStack()
        with routing:
            build_routing(nc, logits, tables, weights, keeper(routing), sem)
        experts = ExitStack()
        with experts:
            build_experts(nc, out2d, z2d, ident, ln2w, ln2b, tables, weights, keeper(experts), sem)



JOBS = [("pt", 3, 0), ("pt", 3, 1), ("xt", 1, 0), ("at", 7, 0), ("pt", 3, 2), ("pt", 3, 3), ("q", 2, 0), ("q", 2, 1),
        ("z2t", 8, 0), ("zt", 4, 0), ("pj", 7, 0), ("pv", 3, 0), ("lg", 8, 0), ("qkv", 4, 0), ("qkv", 4, 1),
        ("wo", 3, 0)]
RING = 4


PASSES = ((0, 0), (0, 1), (1, 0))


def job_places():
    places, order = {}, []
    for s in range(8):
        for job in JOBS:
            if job[0] == "q" and s % 2:
                continue
            places[s, job[0], job[2]] = len(order)
            order.append((s, job))
    assert len(order) % RING == 0
    return places, order


def build_main(nc, a, x2d, out2d, z2d, keys, ident, logits, ln2w, ln2b, sb, sem):
    wq = [sb("wq_hi", [P, KT, D], F32R), sb("wq_lo", [P, KT, D], F32R)]
    wo = [sb("wo_hi", [P, KT, D], F32R), sb("wo_lo", [P, KT, D], F32R)]
    wqkv = [sb("wqkv_hi", [P, KT, QKV], F32R), sb("wqkv_lo", [P, KT, QKV], F32R)]
    wpj = [sb("wpj_hi", [P, KT, D], F32R), sb("wpj_lo", [P, KT, D], F32R)]
    wr = sb("wr", [P, KT, E])
    kb = sb("kb", [P, 2, KT, 4 * SK])
    va = sb("va", [SK, S, H, DH])
    bq = sb("bq", [P, KT])
    bk = sb("bk", [P, KT])
    ln1w = sb("ln1w", [P, KT])
    ln1b = sb("ln1b", [P, KT])
    bo = sb("bo", [P, D])
    mask = sb("mask", [P, NC, SK])
    expo = sb("expo", [P, 1])

    with ExitStack() as st:
        def tmp(name, shape, dt=F32):
            return st.enter_context(nc.sbuf_tensor(name, shape, dt))

        rq = tmp("rq", [P, KT, D])
        ro = tmp("ro", [P, KT, D])
        rqkv = tmp("rqkv", [P, 6, D])
        rpj = tmp("rpj", [P, KT, D])
        rk = tmp("rk", [P, KT, D])
        rv = tmp("rv", [P, KT, D])
        cx = tmp("cx", [SK, S, D])
        cT = tmp("cT", [P, KT, S * SK])
        kT = tmp("kT", [P, KT, S * SK])
        bv = tmp("bv", [SK, D])
        ps = st.enter_context(nc.psum_tensor("setup_ps", [P, 8, 512], F32))
        ctx_in, wk_in, wv_in, qkv_in, pj_in, wq_in, wo_in, small_in = (
            sem(n) for n in ("ctx_in", "wk_in", "wv_in", "qkv_in", "pj_in", "wq_in", "wo_in", "small_in"))
        made, mm_done, hi_done, evac = (sem(n) for n in ("consts_made", "setup_mm", "setup_hi", "setup_evac"))
        split_hi, keys_out = sem("setup_split_hi"), sem("setup_keys_out")
        plain = ((rq, wq, wq_in), (ro, wo, wo_in))

        jobs = ([("ctx", b, 0) for b in range(S)] + [("k", m, h) for m in range(KT) for h in range(2)]
                + [("pj", k, 0) for k in range(KT)] + [("qkv", k, h) for k in range(KT) for h in range(2)]
                + [("v", b, 0) for b in range(S)])
        HC = S * SK // 2
        SMALL = 9
        block = st.enter_context(nc.Block())

        @block.sync
        def _(sp):
            sp.dma_start(cx[:, :, :], a["ctx_1024"].rearrange("b s d -> s b d")).then_inc(ctx_in, 16)
            sp.dma_start(rk[:, :, :], a["L0_xattn_Wk"].rearrange("(k p) n -> p k n", p=P)).then_inc(wk_in, 16)
            sp.dma_start(rv[:, :, :], a["L0_xattn_Wv"].rearrange("(k p) n -> p k n", p=P)).then_inc(wv_in, 16)
            by_group = a["L0_ffn_qkv_weight"].rearrange("(g r) h -> r g h", g=NKV)
            sp.dma_start(rqkv[:, 0:4, :], by_group[0:P, :, :]).then_inc(qkv_in, 16)
            for g in range(NKV):
                rows = slice(g * DH, (g + 1) * DH)
                sp.dma_start(rqkv[rows, 4, :], by_group[P:P + DH, g, :]).then_inc(qkv_in, 16)
                sp.dma_start(rqkv[rows, 5, :], by_group[P + DH:P + 2 * DH, g, :]).then_inc(qkv_in, 16)
            sp.dma_start(rpj[:, :, :], a["L0_ffn_proj_weight"].rearrange("(m p) h -> p m h", p=P)).then_inc(pj_in, 16)
            sp.dma_start(rq[:, :, :], a["L0_xattn_Wq"].rearrange("(k p) n -> p k n", p=P)).then_inc(wq_in, 16)
            sp.dma_start(ro[:, :, :], a["L0_xattn_Wo"].rearrange("(k p) n -> p k n", p=P)).then_inc(wo_in, 16)
            sp.wait_ge(evac, S + 2 * KT)
            sp.dma_start(keys[:, :, :], kT[:, :, :]).then_inc(keys_out, 16)
            sp.wait_ge(keys_out, 16)

        @block.gpsimd
        def _(pool):
            pool.memset(ident[:, :], 0.0).then_inc(made, 1)
            pool.memset(mask[:, :, :], 0.0).then_inc(made, 1)
            pool.memset(expo[:, :], -0.5).then_inc(made, 1)
            pool.wait_ge(made, 3)
            pool.memset(kb[:, :, :, :], 0.0)
            pool.affine_select(out=ident[:, :], in_=ident[:, :], compare_op=ALU.not_equal, fill=1.0, base=0,
                               pattern=[[-1, P]], channel_multiplier=1).then_inc(made, 1)
            pool.affine_select(out=mask[:, 0, :], in_=mask[:, 0, :], compare_op=ALU.is_ge, fill=MASKED, base=0,
                               pattern=[[-1, SK]], channel_multiplier=1).then_inc(made, 1)
            for n, (raw_w, halves, _) in enumerate(plain):
                pool.wait_ge(split_hi, n + 1)
                pool.tensor_tensor(halves[1][:, :, :], raw_w[:, :, :], halves[0][:, :, :].bitcast(F32), ALU.subtract)

        @block.scalar
        def _(act):
            with nc.allow_non_contiguous_dma(reason="512 words of a bias as columns"):
                for dst, name in ((bq, "L0_xattn_bq"), (bk, "L0_xattn_bk"), (ln1w, "L0_ffn_ln1_weight"),
                                  (ln1b, "L0_ffn_ln1_bias"), (ln2w, "L0_ffn_ln2_weight"),
                                  (ln2b, "L0_ffn_ln2_bias")):
                    act.dma_start(dst[:, :], a[name].rearrange("(k p) -> p k", p=P)).then_inc(small_in, 16)
            act.dma_start(bv[:, :], a["L0_xattn_bv"].partition_broadcast(SK)).then_inc(small_in, 16)
            act.dma_start(bo[:, :], a["L0_xattn_bo"].partition_broadcast(P)).then_inc(small_in, 16)
            act.dma_start(wr[:, :, :], a["L0_ffn_router_weight"].rearrange("(k p) e -> p k e", p=P))\
               .then_inc(small_in, 16)
            for raw_w, halves, arrived in plain:
                act.wait_ge(arrived, 16)
                act.activation(halves[0][:, :, :], raw_w[:, :, :], ACT.Copy).then_inc(split_hi, 1)
            for n, (kind, i, h) in enumerate(jobs):
                if kind in ("qkv", "pj"):
                    act.wait_ge(mm_done, n + 1)
                    w, c0, c1 = (wpj, 0, D) if kind == "pj" else (wqkv, 512 * h, 512 if h == 0 else QKV)
                    act.activation(w[0][:, i, c0:c1], ps[:, n % 8, 0:c1 - c0], ACT.Copy).then_inc(hi_done, 1)

        @block.vector
        def _(dve):
            halves = 0
            for n, (kind, i, h) in enumerate(jobs):
                dve.wait_ge(mm_done, n + 1)
                if kind == "ctx":
                    dve.tensor_copy(cT[:, :, i * SK:(i + 1) * SK],
                                    ps[:, n % 8, 0:KT * SK].rearrange("p (k s) -> p k s", k=KT)).then_inc(evac, 1)
                elif kind == "k":
                    dve.wait_ge(small_in, 16 * SMALL)
                    dve.tensor_scalar(kT[:, i, h * HC:(h + 1) * HC], ps[:, n % 8, 0:HC], bk[:, i:i + 1], None,
                                      ALU.add).then_inc(evac, 1)
                elif kind == "v":
                    dve.tensor_tensor(va[:, i, :, :], ps[0:SK, n % 8, :].rearrange("p (h d) -> p h d", h=H),
                                      bv[:, :].rearrange("p (h d) -> p h d", h=H), ALU.add).then_inc(evac, 1)
                else:
                    halves += 1
                    dve.wait_ge(hi_done, halves)
                    w, c0, c1 = (wpj, 0, D) if kind == "pj" else (wqkv, 512 * h, 512 if h == 0 else QKV)
                    dve.tensor_tensor(w[1][:, i, c0:c1], ps[:, n % 8, 0:c1 - c0],
                                      w[0][:, i, c0:c1].bitcast(F32), ALU.subtract).then_inc(evac, 1)

        @block.tensor
        def _(pe):
            pe.wait_ge(made, 5)
            for n, (kind, i, h) in enumerate(jobs):
                need(pe, evac, n - 7)
                bank = ps[:, n % 8, :]
                if kind == "ctx":
                    if n == 0:
                        pe.wait_ge(ctx_in, 16)
                    for k in range(KT):
                        last = pe.transpose(bank[:, k * SK:(k + 1) * SK], cx[:, i, k * P:(k + 1) * P],
                                            ident[0:SK, 0:SK])
                elif kind == "k":
                    pe.wait_ge(wk_in, 16)
                    pe.wait_ge(evac, S)
                    for k in range(KT):
                        last = pe.matmul(bank[:, 0:HC], rk[:, k, i * P:(i + 1) * P],
                                         cT[:, k, h * HC:(h + 1) * HC], start=k == 0, stop=k == KT - 1)
                elif kind == "v":
                    pe.wait_ge(wv_in, 16)
                    for k in range(KT):
                        last = pe.matmul(bank[0:SK, :], cT[:, k, i * SK:(i + 1) * SK], rv[:, k, :],
                                         start=k == 0, stop=k == KT - 1)
                else:
                    if kind == "qkv":
                        pe.wait_ge(qkv_in, 16 * 9)
                        raw, m0, m1 = rqkv, 4 * h, 4 if h == 0 else 6
                    else:
                        pe.wait_ge(pj_in, 16)
                        raw, m0, m1 = rpj, 0, KT
                    for m in range(m0, m1):
                        last = pe.transpose(bank[:, (m - m0) * P:(m - m0 + 1) * P],
                                            raw[:, m, i * P:(i + 1) * P], ident[:, :])
                last.then_inc(mm_done, 1)

    xa = sb("xa", [P, 2, D])
    xc = sb("xc", [P, 2, D])
    xT = [sb("xT_hi", [P, KT, 2 * P], F32R), sb("xT_lo", [P, KT, 2 * P], F32R)]
    qT = sb("qT", [P, KT, 2 * P])
    pr = sb("pr", [P, 4, 4, SK])
    pT = sb("pT", [SK, 4, 4, P])
    oT = [sb("oT_hi", [P, KT, P], F32R), sb("oT_lo", [P, KT, P], F32R)]
    x2 = sb("x2", [P, 8, D])
    z = sb("z", [P, D])
    y = sb("y", [P, KT, P])
    zT = [sb("zT_hi", [P, KT, P], F32R), sb("zT_lo", [P, KT, P], F32R)]
    qb = sb("qb", [P, 2, D])
    kc = sb("kc", [P, S, NKV * DH])
    vc = sb("vc", [P, S, NKV * DH])
    vs = sb("vs", [P, 2, NKV * DH])
    prod_k = sb("prod_k", [P, 2, S * P])
    prod_v = sb("prod_v", [P, 2, S * P])
    sc = sb("sc", [P, H, S])
    pa = sb("pa", [P, 2, H, S])
    att_small = sb("att_small", [P, 3, H])
    ao = sb("ao", [P, D])
    aT = [sb("aT_hi", [P, KT, P], F32R), sb("aT_lo", [P, KT, P], F32R)]
    h1 = sb("h1", [P, D])
    z2 = sb("z2", [P, D])
    y2 = sb("y2", [P, KT, P])
    bnx, bnc, bnf = sb("bnx", [P, 6]), sb("bnc", [P, 6]), sb("bnf", [P, 6])
    mvx, mvc, mvf = sb("mvx", [P, 2, 2]), sb("mvc", [P, 8, 2]), sb("mvf", [P, 2, 2])
    rx, rc, rcc, rf = sb("rx", [P, 2]), sb("rc", [P, 8]), sb("rcc", [P, 2]), sb("rf", [P, 2])
    wx, wc, wf = sb("wx", [P, 1]), sb("wc", [P, 4]), sb("wf", [P, 1])
    shift_c = sb("shift_c", [P, 8])
    nm = sb("nm", [P, H])
    den, rec = sb("exp_sums", [P, H]), sb("rec", [P, H])

    main_psum = ExitStack()
    with main_psum:
        psS = main_psum.enter_context(nc.psum_tensor("score_ps", [P, 4, 512], F32))
        psR = main_psum.enter_context(nc.psum_tensor("ring_ps", [P, RING, 512], F32))

        xa_in = [sem(f"xa_in{i}") for i in range(2)]
        xc_in = [sem(f"xc_in{i}") for i in range(2)]
        keys_in = [sem(f"keys_in{i}") for i in range(2)]
        z2_out = sem("z2_out")
        base_out = sem("base_out")
        names = ("stat_x chain_x rstd_x normed_x xt_mm xt_hi xt_lo q_mm q_evac s_mm masked mx_done nm_done exp_done "
                 "rec_done shared pt_mm pt_evac pv_mm o_hi o_lo wo_mm bias_x x2_done chain_c stat_c "
                 "pool_c rstd_c z_done zt_mm y_done z_hi z_lo qkv_mm qkv_evac v_kept prods_k sums_k prods_v "
                 "sums_v sm_chain sm_sub sm_exp sm_p at_mm at_hi at_lo pj_mm h0_done h1_done chain_f stat_f pool_f "
                 "rstd_f base_done z2_done z2t_mm y2_done lg_mm lg_evac pool_x").split()
        s = {n: sem(n) for n in names}
        places, order = job_places()

        read_out = {
            ("z2t", 0): ("y2_done", 4, 4), ("xt", 0): ("xt_lo", 1, 1), ("zt", 0): ("y_done", 4, 4),
            ("at", 0): ("at_lo", 1, 1), ("pt", 0): ("pt_evac", 4, 1), ("pt", 1): ("pt_evac", 4, 2),
            ("pt", 2): ("pt_evac", 4, 3), ("pt", 3): ("pt_evac", 4, 4), ("lg", 0): ("lg_evac", 1, 1),
            ("wo", 0): ("x2_done", 1, 1), ("qkv", 0): ("qkv_evac", 2, 1), ("qkv", 1): ("qkv_evac", 2, 2),
            ("pj", 0): ("h1_done", 1, 1), ("pv", 0): ("o_lo", 1, 1),
        }

        def bank(step, kind, i=0):
            return psR[:, places[step % 8, kind, i] % RING, :]

        def bank_free(pe, c, step, kind, i=0):
            at = places[step, kind, i]
            while True:
                at -= RING
                back = 0 if at >= 0 else -1
                if back and isinstance(c, int) and c == 0:
                    return
                ps_, (k, lag, j) = order[at % len(order)]
                t = At(c, ps_ + 8 * back - lag)
                if t.within(NT):
                    break
            if k == "q":
                need(pe, s["q_evac"], t.count(2, 2 * j + 2))
            else:
                name, per, j = read_out[k, j]
                need(pe, s[name], t.count(per, j))

        def pipeline(engine, step):
            for i in range(8):
                step(0, i)
            with engine.Fori(1, NC) as c:
                for i in range(8):
                    step(c, i)
            for i in range(8):
                step(NC, i)

        def row0(t):
            return t.chunk * P + t.s * L

        def split_matmuls(pe, dst, lhs, rhs):
            for k in range(KT):
                for n, (l, r) in enumerate(PASSES):
                    last = pe.matmul(dst, lhs(l, k), rhs(r, k), start=k == 0 and n == 0,
                                     stop=k == KT - 1 and n == 2)
            return last

        block = main_psum.enter_context(nc.Block())

        @block.sync
        def _(sp):
            def step(c, i):
                t = At(c, i)
                if t.within(NT):
                    need(sp, s["xt_mm"], t.count(1, -1))
                    sp.dma_start(xa[:, t.s % 2, :], x2d[bass.ds(row0(t), P), :]).then_inc(xa_in[t.s % 2], 16)
                t = At(c, i - 1)
                if t.within(NT):
                    need(sp, s["s_mm"], t.count(1, -1))
                    for b in range(4):
                        rows = slice(b * DH, (b + 1) * DH)
                        sp.dma_start(kb[rows, t.s % 2, :, b * SK:(b + 1) * SK],
                                     keys[rows, :, t.s * SK:(t.s + 1) * SK]).then_inc(keys_in[t.s % 2], 16)
                t = At(c, i - 2)
                if t.within(NT):
                    need(sp, s["x2_done"], t.count(1, -1))
                    sp.dma_start(xc[:, t.s % 2, :], x2d[bass.ds(row0(t), P), :]).then_inc(xc_in[t.s % 2], 16)

            pipeline(sp, step)

        @block.gpsimd
        def _(pool):
            def rstd(dst, var, work, chain, count):
                pool.tensor_scalar(work, var, EPS, None, ALU.add).then_inc(chain, 1)
                need(pool, chain, count)
                return pool.tensor_tensor(dst, work, expo[:, 0:1], ALU.pow)

            def key_products(t, first, last):
                n = t.s + 1
                shape = [P, n, HQ, DH]
                if first == 0:
                    need(pool, s["qkv_evac"], t.count(2, 2))
                for g in range(first, last):
                    need(pool, s["sums_k"], t.count(NKV, g - 1))
                    pool.tensor_tensor(prod_k[:, g % 2, 0:n * P].rearrange("p (t h d) -> p t h d", t=n, h=HQ),
                                       bc(qb[:, t.s % 2, g * P:(g + 1) * P].rearrange("p (h d) -> p h d", h=HQ),
                                          1, shape),
                                       bc(kc[:, 0:n, g * DH:(g + 1) * DH], 2, shape), ALU.mult)\
                        .then_inc(s["prods_k"], 1)

            def value_products(t, first, last):
                n = t.s + 1
                shape = [P, n, HQ, DH]
                if first == 0:
                    pool.wait_ge(s["v_kept"], t.count(1, 1))
                    need(pool, s["sm_p"], t.count(1, 1))
                for g in range(first, last):
                    need(pool, s["sums_v"], t.count(NKV, g - 1))
                    w = pa[:, t.s % 2, g * HQ:(g + 1) * HQ, 0:n].rearrange("p h t -> p t h")
                    pool.tensor_tensor(prod_v[:, g % 2, 0:n * P].rearrange("p (t h d) -> p t h d", t=n, h=HQ),
                                       bc(w, 3, shape), bc(vc[:, 0:n, g * DH:(g + 1) * DH], 2, shape), ALU.mult)\
                        .then_inc(s["prods_v"], 1)

            def step(c, i):
                tq, tv = At(c, i - 5), At(c, i - 6)
                if tq.within(NT):
                    key_products(tq, 0, 1)
                t = At(c, i - 4)
                if t.within(NT):
                    need_apart(pool, (s["stat_c"], t.count(1, 1)))
                    var = mvc[:, t.s, 1:2]
                    pool.tensor_scalar(wc[:, 0:1], var, 1.0 + EPS, EPS * EPS, ALU.mult, ALU.add)\
                        .then_inc(s["pool_c"], 1)
                    need(pool, s["pool_c"], t.count(4, 1))
                    pool.tensor_tensor(rcc[:, t.s % 2:t.s % 2 + 1], wc[:, 0:1], expo[:, 0:1], ALU.pow)\
                        .then_inc(s["rstd_c"], 1)
                    need_apart(pool, (s["rstd_c"], t.count(1, 1)))
                    rstd(rc[:, t.s:t.s + 1], var, wc[:, 1:2], s["pool_c"], t.count(4, 2)).then_inc(s["pool_c"], 1)
                    need_apart(pool, (s["pool_c"], t.count(4, 3)))
                    pool.tensor_scalar(shift_c[:, t.s:t.s + 1], mvc[:, t.s, 0:1], rc[:, t.s:t.s + 1], -1.0, ALU.mult,
                                       ALU.mult).then_inc(s["pool_c"], 1)
                if tq.within(NT):
                    key_products(tq, 1, 2)
                t = At(c, i)
                if t.within(NT):
                    need_apart(pool, (s["stat_x"], t.count(1, 1)))
                    rstd(rx[:, i % 2:i % 2 + 1], mvx[:, i % 2, 1:2], wx[:, :], s["pool_x"], t.count(1, 1))\
                        .then_inc(s["rstd_x"], 1)
                if tq.within(NT):
                    key_products(tq, 2, 3)
                t = At(c, i - 4)
                if t.within(NT):
                    need(pool, s["z_hi"], t.count(1, 1))
                    need(pool, s["qkv_mm"], t.count(2))
                    pool.tensor_tensor(zT[1][:, :, :], y[:, :, :], zT[0][:, :, :].bitcast(F32), ALU.subtract)\
                        .then_inc(s["z_lo"], 1)
                if tq.within(NT):
                    key_products(tq, 3, 4)
                if tv.within(NT):
                    value_products(tv, 0, 1)
                t = At(c, i - 7)
                if t.within(NT):
                    need_apart(pool, (s["stat_f"], t.count(1, 1)))
                    rstd(rf[:, t.s % 2:t.s % 2 + 1], mvf[:, t.s % 2, 1:2], wf[:, :], s["pool_f"], t.count(1, 1))\
                        .then_inc(s["rstd_f"], 1)
                if tv.within(NT):
                    value_products(tv, 1, 2)
                t = At(c, i - 3)
                if t.within(NT):
                    pool.wait_ge(xc_in[t.s % 2], t.turns(2, 16, 16))
                    pool.tensor_tensor(xc[:, t.s % 2, :], xc[:, t.s % 2, :], bo[:, :], ALU.add)\
                        .then_inc(s["bias_x"], 1)
                if tv.within(NT):
                    value_products(tv, 2, 4)
                t = At(c, i - 7)
                if t.within(NT):
                    pool.tensor_tensor(x2[:, t.s, :], x2[:, t.s, :], h1[:, :], ALU.add)\
                        .then_inc(s["base_done"], 1)

            pipeline(pool, step)

        @block.scalar
        def _(act):
            def transposed_shares(t, i, banks):
                for j in banks:
                    act.wait_ge(s["pt_mm"], t.count(4, j + 1))
                    need(act, s["pv_mm"], t.count(1))
                    act.activation(pT[:, j, :, :], bank(i, "pt", j)[0:SK, :].rearrange("p (g n) -> p g n", g=4),
                                   ACT.Copy).then_inc(s["pt_evac"], 1)

            def step(c, i):
                t = At(c, i - 3)
                if t.within(NT):
                    transposed_shares(t, i, (0, 1))
                for kind, lag, dst in (("xt", 1, xT), ("at", 7, aT)):
                    t = At(c, i - lag)
                    if not t.within(NT):
                        continue
                    act.wait_ge(s[kind + "_mm"], t.count(1, 1))
                    if kind == "xt":
                        half = t.s % 2
                        need(act, s["q_mm"], At(c, i - 1 - half).count(1))
                        o = dst[0][:, :, half * P:(half + 1) * P]
                    else:
                        need(act, s["pj_mm"], t.count(1))
                        o = dst[0][:, :, :]
                    act.activation(o, bank(i, kind).rearrange("p (k n) -> p k n", k=KT), ACT.Copy)\
                        .then_inc(s[kind + "_hi"], 1)
                t = At(c, i - 3)
                if t.within(NT):
                    transposed_shares(t, i, (2, 3))
                if i % 2 == 0 and At(c, i - 2).within(NT):
                    t = At(c, i - 2)
                    for m in range(KT):
                        if m % 2 == 0:
                            act.wait_ge(s["q_mm"], t.count(1, m // 2 + 1))
                        need(act, s["s_mm"], t.count(1))
                        act.activation(qT[:, m, :], bank(i, "q", m // 2)[:, (m % 2) * 256:(m % 2) * 256 + 256],
                                       ACT.Identity, bias=bq[:, m:m + 1]).then_inc(s["q_evac"], 1)
                t = At(c, i - 7)
                if t.within(NT):
                    act.wait_ge(s["pool_c"], t.count(4, 4))
                    need(act, s["base_done"], t.count(1))
                    need(act, s["z2_done"], t.count(1))
                    act.activation(h1[:, :], x2[:, t.s, :], ACT.Identity, bias=shift_c[:, t.s:t.s + 1],
                                   scale=rc[:, t.s:t.s + 1]).then_inc(s["h0_done"], 1)
                t = At(c, i - 4)
                if t.within(NT):
                    act.wait_ge(s["zt_mm"], t.count(1, 1))
                    need(act, s["z_lo"], t.count(1))
                    for k in range(KT):
                        act.activation(y[:, k, :], bank(i, "zt")[:, k * P:(k + 1) * P], ACT.Identity,
                                       bias=ln1b[:, k:k + 1], scale=ln1w[:, k:k + 1]).then_inc(s["y_done"], 1)
                    act.wait_ge(s["y_done"], t.count(4, 4))
                    need(act, s["qkv_mm"], t.count(2))
                    act.activation(zT[0][:, :, :], y[:, :, :], ACT.Copy).then_inc(s["z_hi"], 1)
                t = At(c, i - 8)
                if t.within(NT):
                    need(act, s["base_done"], t.count(1, 1))
                    need(act, s["z2_done"], t.count(1, 1))
                    act.dma_start(out2d[bass.ds(row0(t), P), :], x2[:, t.s, :]).then_inc(base_out, 16)
                    act.dma_start(z2d[bass.ds(row0(t), P), :], z2[:, :]).then_inc(z2_out, 16)
                    act.wait_ge(s["z2t_mm"], t.count(1, 1))
                    for k in range(KT):
                        act.activation(y2[:, k, :], bank(i, "z2t")[:, k * P:(k + 1) * P], ACT.Identity,
                                       bias=ln2b[:, k:k + 1], scale=ln2w[:, k:k + 1]).then_inc(s["y2_done"], 1)
                t = At(c, i - 3)
                if t.within(NT):
                    act.wait_ge(s["pv_mm"], t.count(1, 1))
                    need(act, s["wo_mm"], t.count(1))
                    act.activation(oT[0][:, :, :], bank(i, "pv").rearrange("p (k n) -> p k n", k=KT), ACT.Copy)\
                        .then_inc(s["o_hi"], 1)
                t = At(c, i - 2)
                if t.within(NT):
                    act.wait_ge(s["nm_done"], t.count(1, 1))
                    need(act, s["pt_mm"], t.count(4))
                    need(act, s["rec_done"], t.count(2))
                    for b in range(4):
                        for g in range(4):
                            h = 4 * b + g
                            e = act.activation(pr[:, b, g, :], psS[:, b, g * SK:(g + 1) * SK], ACT.Exp,
                                               bias=nm[:, h:h + 1], scale=SCALE, accum_out=den[:, h:h + 1])
                        e.then_inc(s["exp_done"], 1)
                t = At(c, i - 5)
                if t.within(NT):
                    need(act, s["sm_sub"], t.count(1, 1))
                    act.activation(pa[:, t.s % 2, :, 0:t.s + 1], sc[:, :, 0:t.s + 1], ACT.Exp, scale=SCALE)\
                        .then_inc(s["sm_exp"], 1)
                t = At(c, i - 8)
                if t.within(NT):
                    act.wait_ge(s["lg_mm"], t.count(1, 1))
                    act.activation(logits[:, bass.ds(t.s * NC + t.chunk, 1), :],
                                   bank(i, "lg")[:, 0:E].unsqueeze(1), ACT.Copy).then_inc(s["lg_evac"], 1)
                t = At(c, i - 4)
                if t.within(NT):
                    act.wait_ge(s["qkv_mm"], t.count(2, 1))
                    need(act, s["prods_k"], t.count(NKV, -NKV))
                    act.activation(qb[:, t.s % 2, :], bank(i, "qkv", 0), ACT.Copy).then_inc(s["qkv_evac"], 1)
                    act.wait_ge(s["qkv_mm"], t.count(2, 2))
                    need(act, s["prods_k"], t.count(NKV))
                    act.activation(kc[:, t.s, :], bank(i, "qkv", 1)[:, 0:P], ACT.Copy)
                    need(act, s["v_kept"], t.count(1, -1))
                    act.activation(vs[:, t.s % 2, :], bank(i, "qkv", 1)[:, P:2 * P], ACT.Copy)\
                        .then_inc(s["qkv_evac"], 1)
                t = At(c, i - 5)
                if t.within(NT):
                    need(act, s["qkv_evac"], t.count(2, 2))
                    need(act, s["prods_v"], t.count(NKV))
                    act.activation(vc[:, t.s, :], vs[:, t.s % 2, :], ACT.Copy).then_inc(s["v_kept"], 1)

            pipeline(act, step)
            act.wait_ge(base_out, 16 * NT)
            act.wait_ge(z2_out, 16 * NT)

        @block.vector
        def _(dve):
            def stats(src, bn, mv, chain, count):
                dve.bn_stats(bn[:, :], src).then_inc(chain, 1)
                need_apart(dve, (chain, count))
                return dve.bn_aggr(mv, bn[:, :])

            def low_half(c, i, lag, kind, parts, hi, lo):
                t = At(c, i - lag)
                if t.within(NT):
                    dve.wait_ge(s[hi], t.count(1, 1))
                    half = slice((t.s % 2) * P, (t.s % 2) * P + P) if kind == "xt" else slice(0, P)
                    dve.tensor_tensor(parts[1][:, :, half], bank(i, kind).rearrange("p (k n) -> p k n", k=KT),
                                      parts[0][:, :, half].bitcast(F32), ALU.subtract).then_inc(s[lo], 1)

            def share_out(t, half):
                heads = slice(8 * half, 8 * half + 8)
                dve.wait_ge(s["exp_done"], t.count(4, 2 * half + 2))
                need(dve, s["shared"], t.count(2, half))
                dve.reciprocal(rec[:, heads], den[:, heads]).then_inc(s["rec_done"], 1)
                dve.wait_ge(s["rec_done"], t.count(2, half + 1))
                shares = pr[:, 2 * half:2 * half + 2, :, :].rearrange("p b g k -> p (b g) k")
                dve.tensor_tensor(shares, shares, bc(rec[:, heads], 2, [P, 8, SK]), ALU.mult).then_inc(s["shared"], 1)

            def key_sums(t, groups):
                n = t.s + 1
                for g in groups:
                    need(dve, s["prods_k"], t.count(NKV, g + 1))
                    need(dve, s["sm_exp"], t.count(1))
                    dve.tensor_reduce(sc[:, g * HQ:(g + 1) * HQ, 0:n].rearrange("p h t -> p t h"),
                                      prod_k[:, g % 2, 0:n * P].rearrange("p (t h d) -> p t h d", t=n, h=HQ),
                                      X, ALU.add).then_inc(s["sums_k"], 1)

            def value_sums(t, groups):
                n = t.s + 1
                for g in groups:
                    need(dve, s["prods_v"], t.count(NKV, g + 1))
                    need(dve, s["at_mm"], t.count(1))
                    dve.tensor_reduce(ao[:, g * P:(g + 1) * P],
                                      prod_v[:, g % 2, 0:n * P].rearrange("p (t f) -> p f t", t=n),
                                      X, ALU.add).then_inc(s["sums_v"], 1)

            def step(c, i):
                ts, tq, tv = At(c, i - 2), At(c, i - 5), At(c, i - 6)
                n = tq.s + 1
                t = At(c, i - 4)
                if t.within(NT):
                    dve.wait_ge(s["wo_mm"], t.count(1, 1))
                    dve.wait_ge(s["bias_x"], t.count(1, 1))
                    need(dve, s["base_done"], t.count(1, -3))
                    dve.tensor_tensor(x2[:, t.s, :], bank(i - 1, "wo"), xc[:, t.s % 2, :], ALU.add)\
                       .then_inc(s["x2_done"], 1)
                    dve.wait_ge(s["x2_done"], t.count(1, 1))
                    stats(x2[:, t.s, :], bnc, mvc[:, t.s, :], s["chain_c"], t.count(1, 1)).then_inc(s["stat_c"], 1)
                low_half(c, i, 1, "xt", xT, "xt_hi", "xt_lo")
                low_half(c, i, 7, "at", aT, "at_hi", "at_lo")
                t = At(c, i - 4)
                if t.within(NT):
                    dve.wait_ge(s["rstd_c"], t.count(1, 1))
                    need(dve, s["zt_mm"], t.count(1))
                    dve.tensor_scalar(z[:, :], x2[:, t.s, :], mvc[:, t.s, 0:1], rcc[:, t.s % 2:t.s % 2 + 1],
                                      ALU.subtract, ALU.mult).then_inc(s["z_done"], 1)
                if tv.within(NT):
                    need(dve, s["sm_exp"], tv.count(1, 1))
                    dve.tensor_reduce(att_small[:, 1, :], pa[:, tv.s % 2, :, 0:tv.s + 1], X, ALU.add)\
                       .then_inc(s["sm_chain"], 1)
                    need(dve, s["sm_chain"], tv.count(3, 2))
                    dve.reciprocal(att_small[:, 2, :], att_small[:, 1, :]).then_inc(s["sm_chain"], 1)
                    need(dve, s["sm_chain"], tv.count(3, 3))
                    dve.tensor_tensor(pa[:, tv.s % 2, :, 0:tv.s + 1], pa[:, tv.s % 2, :, 0:tv.s + 1],
                                      bc(att_small[:, 2, :], 2, [P, H, tv.s + 1]), ALU.mult).then_inc(s["sm_p"], 1)
                if tq.within(NT):
                    key_sums(tq, (0,))
                t = At(c, i)
                if t.within(NT):
                    dve.wait_ge(xa_in[i % 2], t.turns(2, 16, 16))
                    stats(xa[:, i % 2, :], bnx, mvx[:, i % 2, :], s["chain_x"], t.count(1, 1)).then_inc(s["stat_x"], 1)
                if tq.within(NT):
                    key_sums(tq, (1, 2))
                t = At(c, i - 7)
                if t.within(NT):
                    dve.wait_ge(s["h0_done"], t.count(1, 1))
                    dve.wait_ge(s["pj_mm"], t.count(1, 1))
                    dve.tensor_tensor(h1[:, :], bank(i, "pj"), h1[:, :], ALU.add).then_inc(s["h1_done"], 1)
                    dve.wait_ge(s["h1_done"], t.count(1, 1))
                    stats(h1[:, :], bnf, mvf[:, t.s % 2, :], s["chain_f"], t.count(1, 1)).then_inc(s["stat_f"], 1)
                t = At(c, i - 2)
                if t.within(NT):
                    dve.wait_ge(s["s_mm"], t.count(1, 1))
                    scores = psS[:, :, 0:4 * SK].rearrange("p b (g k) -> p b g k", g=4)
                    if (isinstance(c, int) and c == 0) or t.off < 0:
                        m = mask[:, bass.ds(t.chunk, 1), :].unsqueeze(1).to_broadcast([P, 4, 4, SK])
                        dve.tensor_tensor(scores, scores, m, ALU.add).then_inc(s["masked"], 1)
                        dve.wait_ge(s["masked"], c * 2 + (i - 1 if isinstance(c, int) and c == 0 else 5 + i))
                    need(dve, s["exp_done"], t.count(4))
                    dve.tensor_reduce(nm[:, :].rearrange("p (b g) -> p b g", b=4), scores, X, ALU.max)\
                       .then_inc(s["mx_done"], 1)
                    dve.wait_ge(s["mx_done"], t.count(1, 1))
                    dve.tensor_scalar(nm[:, :], nm[:, :], -SCALE, None, ALU.mult).then_inc(s["nm_done"], 1)
                low_half(c, i, 3, "pv", oT, "o_hi", "o_lo")
                if tq.within(NT):
                    key_sums(tq, (3,))
                    need(dve, s["sums_k"], tq.count(NKV, NKV))
                    dve.tensor_reduce(att_small[:, 0, :], sc[:, :, 0:n], X, ALU.max).then_inc(s["sm_chain"], 1)
                    need(dve, s["sm_chain"], tq.count(3, 1))
                    dve.tensor_tensor(sc[:, :, 0:n], sc[:, :, 0:n], bc(att_small[:, 0, :], 2, [P, H, n]),
                                      ALU.subtract).then_inc(s["sm_sub"], 1)
                if tv.within(NT):
                    value_sums(tv, (0,))
                if tv.within(NT):
                    value_sums(tv, (1,))
                t = At(c, i)
                if t.within(NT):
                    dve.wait_ge(s["rstd_x"], t.count(1, 1))
                    dve.tensor_scalar(xa[:, i % 2, :], xa[:, i % 2, :], mvx[:, i % 2, 0:1], rx[:, i % 2:i % 2 + 1],
                                      ALU.subtract, ALU.mult).then_inc(s["normed_x"], 1)
                if ts.within(NT):
                    share_out(ts, 0)
                if tv.within(NT):
                    value_sums(tv, (2,))
                t = At(c, i - 7)
                if t.within(NT):
                    dve.wait_ge(s["rstd_f"], t.count(1, 1))
                    need(dve, z2_out, t.count(16))
                    need(dve, base_out, t.count(16))
                    need(dve, s["z2t_mm"], t.count(1))
                    dve.tensor_scalar(z2[:, :], h1[:, :], mvf[:, t.s % 2, 0:1], rf[:, t.s % 2:t.s % 2 + 1],
                                      ALU.subtract, ALU.mult).then_inc(s["z2_done"], 1)
                if ts.within(NT):
                    share_out(ts, 1)
                if tv.within(NT):
                    value_sums(tv, (3,))

            pipeline(dve, step)

        @block.tensor
        def _(pe):
            def transposes(c, i, lag, kind, ready, count, src, mm):
                t = At(c, i - lag)
                if t.within(NT):
                    pe.wait_ge(s[ready], t.count(*count))
                    bank_free(pe, c, i, kind)
                    for k in range(KT):
                        last = pe.transpose(bank(i, kind)[:, k * P:(k + 1) * P], src(t)[:, k * P:(k + 1) * P],
                                            ident[:, :])
                    last.then_inc(s[mm], 1)

            def step(c, i):
                t = At(c, i - 3)
                if t.within(NT):
                    pe.wait_ge(s["shared"], t.count(2, 1))
                for b in range(4):
                    if b == 2:
                        transposes(c, i, 1, "xt", "normed_x", (1, 1), lambda t: xa[:, t.s % 2, :], "xt_mm")
                        transposes(c, i, 7, "at", "sums_v", (NKV, NKV), lambda t: ao[:, :], "at_mm")
                    if t.within(NT):
                        if b == 2:
                            pe.wait_ge(s["shared"], t.count(2, 2))
                        bank_free(pe, c, i, "pt", b)
                        for g in range(4):
                            last = pe.transpose(bank(i, "pt", b)[0:SK, g * P:(g + 1) * P], pr[:, b, g, :],
                                                ident[:, :])
                        last.then_inc(s["pt_mm"], 1)
                if i % 2 == 0 and At(c, i - 2).within(NT):
                    t = At(c, i - 2)
                    pe.wait_ge(s["xt_lo"], t.count(1, 2))
                    for j in range(2):
                        bank_free(pe, c, i, "q", j)
                        for m in range(2):
                            cols = slice((2 * j + m) * P, (2 * j + m + 1) * P)
                            last = split_matmuls(pe, bank(i, "q", j)[:, m * 256:(m + 1) * 256],
                                                 lambda h, k: wq[h][:, k, cols], lambda h, k: xT[h][:, k, :])
                        last.then_inc(s["q_mm"], 1)
                transposes(c, i, 8, "z2t", "z2_done", (1, 1), lambda t: z2[:, :], "z2t_mm")
                transposes(c, i, 4, "zt", "z_done", (1, 1), lambda t: z[:, :], "zt_mm")
                t = At(c, i - 7)
                if t.within(NT):
                    pe.wait_ge(s["at_lo"], t.count(1, 1))
                    bank_free(pe, c, i, "pj")
                    split_matmuls(pe, bank(i, "pj"), lambda h, k: aT[h][:, k, :], lambda h, k: wpj[h][:, k, :])\
                        .then_inc(s["pj_mm"], 1)
                t = At(c, i - 2)
                if t.within(NT):
                    pe.wait_ge(s["q_evac"], At(c, i - 2 - t.s % 2).count(2, 4))
                    pe.wait_ge(keys_in[t.s % 2], t.turns(2, 64, 64))
                    for g in range(4):
                        need(pe, s["exp_done"], t.count(4, g - 3))
                        last = pe.matmul(psS[:, g, 0:4 * SK], qT[:, g, (t.s % 2) * P:(t.s % 2) * P + P],
                                         kb[:, t.s % 2, g, :], start=True, stop=True)
                    last.then_inc(s["s_mm"], 1)
                t = At(c, i - 3)
                if t.within(NT):
                    pe.wait_ge(s["pt_evac"], t.count(4, 4))
                    bank_free(pe, c, i, "pv")
                    for g in range(4):
                        for b in range(4):
                            last = pe.matmul(bank(i, "pv")[b * DH:(b + 1) * DH, g * P:(g + 1) * P],
                                             va[:, t.s, 4 * g + b, :], pT[:, g, b, :], start=True, stop=True)
                    last.then_inc(s["pv_mm"], 1)
                t, tr = At(c, i - 4), At(c, i - 8)
                if tr.within(NT):
                    pe.wait_ge(s["y2_done"], tr.count(4, 4))
                    bank_free(pe, c, i, "lg")
                if t.within(NT):
                    pe.wait_ge(s["z_lo"], t.count(1, 1))
                    bank_free(pe, c, i, "qkv", 0)
                for k in range(KT):
                    if t.within(NT):
                        for n, (l, r) in enumerate(PASSES):
                            last = pe.matmul(bank(i, "qkv", 0), zT[l][:, k, :], wqkv[r][:, k, 0:D],
                                             start=k == 0 and n == 0, stop=k == KT - 1 and n == 2)
                        if k == KT - 1:
                            last.then_inc(s["qkv_mm"], 1)
                    if tr.within(NT):
                        last = pe.matmul(bank(i, "lg")[:, 0:E], y2[:, k, :], wr[:, k, :], start=k == 0,
                                         stop=k == KT - 1)
                        if k == KT - 1:
                            last.then_inc(s["lg_mm"], 1)
                if t.within(NT):
                    bank_free(pe, c, i, "qkv", 1)
                    split_matmuls(pe, bank(i, "qkv", 1)[:, 0:QKV - D], lambda h, k: zT[h][:, k, :],
                                  lambda h, k: wqkv[h][:, k, D:QKV]).then_inc(s["qkv_mm"], 1)
                t = At(c, i - 3)
                if t.within(NT):
                    pe.wait_ge(s["o_lo"], t.count(1, 1))
                    bank_free(pe, c, i, "wo")
                    split_matmuls(pe, bank(i, "wo"), lambda h, k: oT[h][:, k, :], lambda h, k: wo[h][:, k, :])\
                        .then_inc(s["wo_mm"], 1)

            pipeline(pe, step)



def build_routing(nc, logits, tables, weights, sb, sem):
    ranks = sb("ranks", [P, E])
    ramp = sb("ramp", [P, P])
    number = sb("number", [P, NT])
    before = sb("before", [P, P])
    ones = sb("ones", [P, P])
    ints = sb("ints", [P, P], I32)
    ints2 = sb("ints2", [P, NT], I32)
    ints3 = sb("ints3", [P, E], I32)
    best = sb("best", [P, 2, NT])
    first = sb("first", [P, 2, NT])
    eq = sb("eq", [P, NT, E])
    hot = sb("hot", [P, 2, NT, E])
    rest = sb("rest", [P, NT, E])
    both = sb("both", [P, NT, E])
    seen = sb("seen", [P, 2, NT, E])
    place = sb("place", [P, NT, E])
    share = sb("share", [P, 2, NT])
    diff = sb("diff", [P, NT])
    ex = sb("ex", [P, NT])
    den = sb("den", [P, NT])
    within = sb("within", [P, 2, NT])
    wi = sb("wi", [P, 2, NT], I32)
    qi = sb("qi", [P, 2, NT], I32)
    ri = sb("ri", [P, 2, NT], I32)
    blk = sb("blk", [P, 2, NT])
    row = sb("row", [P, 2, NT])
    over = sb("over", [P, 2, NT])
    hot_row = sb("hot_row", [P, 2, 4, P])
    hot_blk = sb("hot_blk", [P, 2, 4, 2, NBLK])
    is_blk = sb("is_blk", [P, 2, 4, NBLK])
    ids = sb("ids", [P, NBLK])
    idc = sb("idc", [P, NBLK])
    with ExitStack() as st:
        pp = st.enter_context(nc.psum_tensor("prefix_ps", [P, 2, 512], F32))
        pt = st.enter_context(nc.psum_tensor("table_ps", [P, 2 * NBLK], F32))
        made, chain, sm, expd, prefixed, tabled, matched, hots = (
            sem("r_" + n) for n in ("made", "chain", "diff", "exp", "prefixed", "tabled", "matched", "hots"))
        counted = sem("r_counted")
        block = st.enter_context(nc.Block())

        @block.gpsimd
        def _(pool):
            pool.iota(ints[:, :], [[1, P]], base=0, channel_multiplier=0).then_inc(made, 1)
            pool.iota(ints2[:, :], [[P, NT]], base=1, channel_multiplier=1).then_inc(made, 1)
            pool.iota(ints3[:, :], [[-1, E]], base=E, channel_multiplier=0).then_inc(made, 1)
            pool.memset(before[:, :], 1.0).then_inc(made, 1)
            pool.memset(ones[:, :], 1.0).then_inc(made, 1)
            pool.wait_ge(made, 5)
            pool.tensor_copy(ramp[:, :], ints[:, :]).then_inc(made, 1)
            pool.tensor_copy(number[:, :], ints2[:, :]).then_inc(made, 1)
            pool.tensor_copy(ranks[:, :], ints3[:, :]).then_inc(made, 1)
            pool.affine_select(out=before[:, :], in_=before[:, :], compare_op=ALU.is_gt, fill=0.0, base=0,
                               pattern=[[1, P]], channel_multiplier=-1).then_inc(made, 1)
            for j in range(CH):
                weights["low"](pool, 0, 0, j)

        @block.sync
        def _(sp):
            for j in range(CH):
                weights["load"](sp, 0, 0, 0, j)

        @block.scalar
        def _(act):
            act.wait_ge(sm, 1)
            act.activation(ex[:, :], diff[:, :], ACT.Exp).then_inc(expd, 1)
            for j in range(CH):
                weights["high"](act, 0, 0, j)

        @block.vector
        def _(dve):
            steps = [0]

            def link(instruction):
                steps[0] += 1
                instruction.then_inc(chain, 1)
                dve.wait_ge(chain, steps[0])

            dve.wait_ge(made, 9)
            shape = [P, NT, E]
            for k in range(2):
                src = logits if k == 0 else rest
                link(dve.tensor_reduce(best[:, k, :], src[:, :, :], X, ALU.max))
                link(dve.tensor_tensor(eq[:, :, :], src[:, :, :], bc(best[:, k, :], 2, shape), ALU.is_equal))
                link(dve.tensor_tensor(eq[:, :, :], eq[:, :, :], bc(ranks[:, :], 1, shape), ALU.mult))
                link(dve.tensor_reduce(first[:, k, :], eq[:, :, :], X, ALU.max))
                link(dve.tensor_tensor(hot[:, k, :, :], bc(first[:, k, :], 2, shape), bc(ranks[:, :], 1, shape),
                                       ALU.is_equal))
                if k == 0:
                    link(dve.scalar_tensor_tensor(rest[:, :, :], hot[:, 0, :, :], HUGE, logits[:, :, :], ALU.mult,
                                                  ALU.add))
            dve.tensor_tensor(diff[:, :], best[:, 1, :], best[:, 0, :], ALU.subtract).then_inc(sm, 1)
            dve.tensor_tensor(both[:, :, :], hot[:, 0, :, :], hot[:, 1, :, :], ALU.add).then_inc(counted, 1)
            dve.wait_ge(expd, 1)
            link(dve.tensor_scalar(den[:, :], ex[:, :], 1.0, None, ALU.add))
            link(dve.reciprocal(share[:, 0, :], den[:, :]))
            link(dve.tensor_tensor(share[:, 1, :], ex[:, :], share[:, 0, :], ALU.mult))
            dve.wait_ge(prefixed, 1)
            link(dve.tensor_copy(seen[:, 0, :, :], pp[:, 1, 0:NT * E].rearrange("p (t e) -> p t e", e=E)))
            src, sh = 0, 1
            while sh < NT:
                dst = 1 - src
                link(dve.tensor_tensor(seen[:, dst, sh:NT, :], seen[:, src, sh:NT, :], seen[:, src, 0:NT - sh, :],
                                       ALU.add))
                link(dve.tensor_copy(seen[:, dst, 0:sh, :], seen[:, src, 0:sh, :]))
                src, sh = dst, 2 * sh
            link(dve.tensor_tensor(place[:, :, :], pp[:, 0, 0:NT * E].rearrange("p (t e) -> p t e", e=E),
                                   seen[:, src, :, :], ALU.add))
            link(dve.tensor_tensor(place[:, :, :], place[:, :, :],
                                   pp[:, 1, 0:NT * E].rearrange("p (t e) -> p t e", e=E), ALU.subtract))
            for k in range(2):
                link(dve.tensor_tensor(eq[:, :, :], hot[:, k, :, :], place[:, :, :], ALU.mult))
                link(dve.tensor_reduce(within[:, k, :], eq[:, :, :], X, ALU.add))
            link(dve.tensor_copy(wi[:, :, :], within[:, :, :]))
            link(dve.tensor_scalar(qi[:, :, :], wi[:, :, :], 7, None, ALU.logical_shift_right))
            link(dve.tensor_scalar(ri[:, :, :], wi[:, :, :], P - 1, None, ALU.bitwise_and))
            link(dve.tensor_copy(blk[:, :, :], qi[:, :, :]))
            link(dve.tensor_copy(row[:, :, :], ri[:, :, :]))
            link(dve.tensor_scalar(over[:, :, :], within[:, :, :], float(CAP), 1000.0, ALU.is_ge, ALU.mult))
            link(dve.tensor_tensor(blk[:, :, :], blk[:, :, :], over[:, :, :], ALU.add))
            link(dve.tensor_scalar(over[:, :, :], first[:, :, :], -float(BPE), float(E * BPE), ALU.mult, ALU.add))
            link(dve.tensor_tensor(blk[:, :, :], blk[:, :, :], over[:, :, :], ALU.add))
            def one_hots(k, j, tiles, count):
                shape = [P, 4, NBLK]
                dve.tensor_tensor(is_blk[:, j, :, :], bc(ramp[:, 0:NBLK], 1, shape), bc(blk[:, k, tiles], 2, shape),
                                  ALU.is_equal).then_inc(matched, 1)
                dve.tensor_tensor(hot_row[:, j, :, :], bc(ramp[:, :], 1, [P, 4, P]), bc(row[:, k, tiles], 2, [P, 4, P]),
                                  ALU.is_equal)
                dve.wait_ge(matched, count)
                dve.tensor_tensor(hot_blk[:, j, :, 0, :], is_blk[:, j, :, :], bc(number[:, tiles], 2, shape), ALU.mult)
                dve.tensor_tensor(hot_blk[:, j, :, 1, :], is_blk[:, j, :, :], bc(share[:, k, tiles], 2, shape),
                                  ALU.mult).then_inc(hots, 1)

            for k in range(2):
                with dve.Fori(0, NT // 8) as c:
                    for j in range(2):
                        dve.wait_ge(tabled, c * 8 + (NT * k + 4 * j + 4))
                        one_hots(k, j, bass.ds(c * 8 + 4 * j, 4), c * 2 + (NT // 4 * k + j + 1))
            dve.wait_ge(tabled, 2 * NT + 8)
            dve.tensor_copy(tables["shares"][:, :], pt[:, NBLK:2 * NBLK])
            link(dve.tensor_scalar(ids[:, :], pt[:, 0:NBLK], 0.0, 2.0 * N, ALU.is_equal, ALU.mult))
            link(dve.scalar_tensor_tensor(idc[:, :], pt[:, 0:NBLK], -1.0, ids[:, :], ALU.add, ALU.add))
            dve.tensor_copy(tables["rows"][:, :], idc[:, :])

        @block.tensor
        def _(pe):
            pe.sem_inc(tabled, 8)
            pe.wait_ge(made, 9)
            pe.wait_ge(counted, 1)
            flat = both[:, :, :].rearrange("p t e -> p (t e)")
            pe.matmul(pp[:, 0, 0:NT * E], before[:, :], flat, start=True, stop=True)
            pe.matmul(pp[:, 1, 0:NT * E], ones[:, :], flat, start=True, stop=True).then_inc(prefixed, 1)
            for n in range(2 * NT):
                if n % 4 == 0:
                    pe.wait_ge(hots, n // 4 + 1)
                pe.matmul(pt[:, :], hot_row[:, n // 4 % 2, n % 4, :],
                          hot_blk[:, n // 4 % 2, n % 4, :, :].rearrange("p a b -> p (a b)"),
                          start=n == 0, stop=n == 2 * NT - 1).then_inc(tabled, 1)



CH = 8
PER = 2 * GPE


def expert_weights(a, sb, sem):
    w1 = [[sb(f"w1_{p}{h}", [P, KT, F], F32R) for h in range(2)] for p in range(2)]
    w2 = [[sb(f"w2_{p}{h}", [P, FT, D], F32R) for h in range(2)] for p in range(2)]
    raw = sb("raw", [P, 2, F])
    raw_in = [sem(f"raw_in{i}") for i in range(2)]
    s = {n: sem("e_" + n) for n in ("w_hi", "w_lo", "fc1_mm", "fc2_mm")}

    def weight_piece(p, half, j):
        if j < 4:
            return w1[p][half][:, j, :]
        return w2[p][half][:, 2 * (j - 4):2 * (j - 4) + 2, :].rearrange("p f n -> p (f n)")

    def weights_free(engine, c, p, j):
        if isinstance(c, int) and c == 0:
            return
        last = At(c, GPE * p - GPE - 1, PER)
        if j < 4:
            engine.wait_ge(s["fc1_mm"], last.count(4, 4))
        else:
            engine.wait_ge(s["fc2_mm"], last.count(GB, GB))

    def load(sp, e, c, p, j):
        n = At(c, CH * p + j, 2 * CH)
        need(sp, s["w_lo"], n.count(1, -1))
        if j < 4:
            sp.dma_start(raw[:, j % 2, :], a["L0_ffn_moe_w1"].rearrange("e (k p) f -> (e k) p f", p=P)
                         [bass.ds(e * KT + j, 1), :, :].rearrange("a p f -> (a p) f"))\
              .then_inc(raw_in[j % 2], 16)
        else:
            src = a["L0_ffn_moe_w2"].rearrange("e (q f p) n -> (e q) p f n", f=2, p=P)
            sp.dma_start(raw[:, j % 2, :].rearrange("p (f n) -> p f n", f=2),
                         src[bass.ds(e * 4 + (j - 4), 1), :, :, :].rearrange("a p f n -> (a p) f n"))\
              .then_inc(raw_in[j % 2], 16)

    def high(act, c, p, j):
        n = At(c, CH * p + j, 2 * CH)
        act.wait_ge(raw_in[j % 2], At(c, (CH * p + j) // 2, CH).count(16, 16))
        weights_free(act, c, p, j)
        act.activation(weight_piece(p, 0, j), raw[:, j % 2, :], ACT.Copy).then_inc(s["w_hi"], 1)

    def low(pool, c, p, j):
        n = At(c, CH * p + j, 2 * CH)
        pool.wait_ge(s["w_hi"], n.count(1, 1))
        weights_free(pool, c, p, j)
        pool.tensor_tensor(weight_piece(p, 1, j), raw[:, j % 2, :],
                           weight_piece(p, 0, j).bitcast(F32), ALU.subtract).then_inc(s["w_lo"], 1)

    return {"w1": w1, "w2": w2, "load": load, "high": high, "low": low, "counts": s}


def build_experts(nc, out2d, z2d, ident, ln2w, ln2b, tables, weights, sb, sem):
    w1, w2, load, high, low = (weights[n] for n in ("w1", "w2", "load", "high", "low"))
    xg = sb("xg", [P, 2, GB, D])
    yk = sb("yk", [P, 2, GB * P])
    xT = [sb("gT_hi", [P, KT, GB * P], F32R), sb("gT_lo", [P, KT, GB * P], F32R)]
    gl = sb("gl", [P, 2, 2 * GB * P])
    hT = [[sb(f"hT_{p}{h}", [P, FT, GB * P], F32R) for h in range(2)] for p in range(2)]
    og = sb("og", [P, GB, D])
    idx = sb("idx", [P, GPE, GB], I32)
    W = GB * P

    with ExitStack() as st:
        pT = st.enter_context(nc.psum_tensor("gather_ps", [P, GB, 512], F32))
        pH = st.enter_context(nc.psum_tensor("hidden_ps", [P, 4, 512], F32))
        pY = st.enter_context(nc.psum_tensor("expert_ps", [P, GB, 512], F32))
        names = ("cleared copied scattered xt_mm yk_done xt_hi xt_lo gelu h_hi h_lo "
                 "summed").split()
        s = {**weights["counts"], **{n: sem("e_" + n) for n in names}}
        gathered = [sem(f"e_gathered{i}") for i in range(2)]
        block = st.enter_context(nc.Block())

        def pipeline(engine, step):
            for i in range(PER):
                step(0, i)
            with engine.Fori(1, NG // PER) as c:
                for i in range(PER):
                    step(c, i)
            for i in range(PER):
                step(NG // PER, i)

        def col(g, b):
            return bass.ds(g.count(GB, b), 1)

        @block.sync
        def _(sp):
            for j in range(CH):
                load(sp, 1, 0, 1, j)
            with sp.Fori(1, E // 2) as c:
                for p in range(2):
                    for j in range(CH):
                        load(sp, c * 2 + p, c, p, j)

        def weights_free(engine, c, p, j):
            if isinstance(c, int) and c == 0:
                return
            last = At(c, GPE * p - GPE - 1, PER)
            if j < 4:
                engine.wait_ge(s["fc1_mm"], last.count(4, 4))
            else:
                engine.wait_ge(s["fc2_mm"], last.count(GB, GB))

        def split_pieces(c, i):
            p, g = divmod(i, GPE)
            if isinstance(c, int) and (c == E // 2 or (c == 0 and p == 0)):
                return []
            at = (0, 2, 4, 6, 7, 8)
            return [(c, p, j) for j in range(at[g], at[g + 1])]

        @block.gpsimd
        def _(pool):
            def rows(g, k):
                return bass.IndirectOffsetOnAxis(ap=idx[:, g.s % GPE, k:k + 1], axis=0)

            def step(c, i):
                g = At(c, i - 4, PER)
                if g.within(NG):
                    pool.tensor_copy(idx[:, g.s % GPE, :], tables["rows"][:, bass.ds(g.count(GB), GB)])\
                        .then_inc(s["copied"], 1)
                    need_apart(pool, (s["copied"], g.count(1, 1)), (s["xt_mm"], g.count(1, -1)))
                    for k in range(GB):
                        pool.indirect_dma_start(out=xg[:, g.s % 2, k, :], out_offset=None, in_=z2d[:, :],
                                                in_offset=rows(g, k), bounds_check=N - 1,
                                                oob_is_err=False).then_inc(gathered[g.s % 2], 16)
                for piece in split_pieces(c, i):
                    low(pool, *piece)
                g = At(c, i - 7, PER)
                if g.within(NG):
                    need_apart(pool, (s["summed"], g.count(GB, GB)))
                    for k in range(GB):
                        pool.indirect_dma_start(out=out2d[:, :], out_offset=rows(g, k), in_=og[:, k, :],
                                                in_offset=None, bounds_check=N - 1, oob_is_err=False,
                                                compute_op=ALU.add).then_inc(s["scattered"], 16)

            pool.memset(xg[:, :, :, :], 0.0).then_inc(s["cleared"], 1)
            pool.wait_ge(s["cleared"], 1)
            pipeline(pool, step)
            pool.wait_ge(s["scattered"], 32 * NG)

        @block.scalar
        def _(act):
            def step(c, i):
                g = At(c, i - 6, PER)
                if g.within(NG):
                    for q in range(4):
                        act.wait_ge(s["fc1_mm"], g.count(4, q + 1))
                        need(act, s["h_lo"], g.count(4, q - 1))
                        act.activation(gl[:, q % 2, :], pH[:, q, :], ACT.Gelu_apprx_tanh).then_inc(s["gelu"], 1)
                g = At(c, i - 5, PER)
                if g.within(NG):
                    for k in range(KT):
                        act.wait_ge(s["yk_done"], g.count(KT, k + 1))
                        need(act, s["fc1_mm"], g.count(4))
                        act.activation(xT[0][:, k, :], yk[:, k % 2, :], ACT.Copy).then_inc(s["xt_hi"], 1)
                for piece in split_pieces(c, i):
                    high(act, *piece)

            pipeline(act, step)

        @block.vector
        def _(dve):
            def step(c, i):
                g = At(c, i - 6, PER)
                if g.within(NG):
                    par = g.s % 2
                    for q in range(4):
                        dve.wait_ge(s["gelu"], g.count(4, q + 1))
                        need(dve, s["fc2_mm"], g.count(GB, -GB))
                        o = [hT[par][h][:, 2 * q:2 * q + 2, :].rearrange("p f n -> p (f n)") for h in range(2)]
                        dve.tensor_copy(o[0], gl[:, q % 2, :]).then_inc(s["h_hi"], 1)
                        dve.wait_ge(s["h_hi"], g.count(4, q + 1))
                        dve.tensor_tensor(o[1], gl[:, q % 2, :], o[0].bitcast(F32), ALU.subtract)\
                           .then_inc(s["h_lo"], 1)
                g = At(c, i - 5, PER)
                if g.within(NG):
                    dve.wait_ge(s["xt_mm"], g.count(1, 1))
                    for k in range(KT + 1):
                        if k < KT:
                            need(dve, s["xt_lo"], g.count(KT, k - 1))
                            dve.tensor_scalar(yk[:, k % 2, :].rearrange("p (b n) -> p b n", b=GB),
                                              pT[:, :, k * P:(k + 1) * P], ln2w[:, k:k + 1], ln2b[:, k:k + 1],
                                              ALU.mult, ALU.add).then_inc(s["yk_done"], 1)
                        if k > 0:
                            dve.wait_ge(s["xt_hi"], g.count(KT, k))
                            dve.tensor_tensor(xT[1][:, k - 1, :], yk[:, (k - 1) % 2, :],
                                              xT[0][:, k - 1, :].bitcast(F32), ALU.subtract).then_inc(s["xt_lo"], 1)
                g = At(c, i - 7, PER)
                if g.within(NG):
                    for k in range(GB):
                        dve.wait_ge(s["fc2_mm"], g.count(GB, k + 1))
                        need(dve, s["scattered"], g.count(32))
                        dve.tensor_scalar(og[:, k, :], pY[:, k, :], tables["shares"][:, col(g, k)], None, ALU.mult)\
                           .then_inc(s["summed"], 1)

            dve.memset(pH[:, :, :], 0.0)
            dve.memset(pY[:, :, :], 0.0)
            pipeline(dve, step)

        @block.tensor
        def _(pe):
            def first_row(g):
                return pe.value_load(tables["rows"][0:1, bass.ds(g.count(GB), 1)], min_val=0, max_val=2 * N)

            def step(c, i):
                g = At(c, i - 6, PER)
                if g.within(NG):
                    row = first_row(g)
                    p = g.s // GPE
                    if g.s % GPE == 0:
                        pe.wait_ge(s["w_lo"], c * (2 * CH) + (CH * (g.off // GPE) + 4))
                    pe.wait_ge(s["xt_lo"], g.count(KT, KT))
                    with pe.If(row < N):
                        for q in range(4):
                            need(pe, s["gelu"], g.count(4, q - 3))
                            for f in range(2):
                                cols = slice((2 * q + f) * P, (2 * q + f + 1) * P)
                                for k in range(KT):
                                    for n, (l, r) in enumerate(PASSES):
                                        last = pe.matmul(pH[:, q, f * W:(f + 1) * W], w1[p][l][:, k, cols],
                                                         xT[r][:, k, :], start=k == 0 and n == 0,
                                                         stop=k == KT - 1 and n == 2)
                            last.then_inc(s["fc1_mm"], 1)
                    with pe.Else():
                        need(pe, s["gelu"], g.count(4))
                        pe.sem_inc(s["fc1_mm"], 4)
                g = At(c, i - 5, PER)
                if g.within(NG):
                    pe.wait_ge(gathered[g.s % 2], g.turns(2, 32, 32))
                    need(pe, s["yk_done"], g.count(KT))
                    for k in range(GB):
                        for m in range(KT):
                            last = pe.transpose(pT[:, k, m * P:(m + 1) * P], xg[:, g.s % 2, k, m * P:(m + 1) * P],
                                                ident[:, :])
                    last.then_inc(s["xt_mm"], 1)
                g = At(c, i - 7, PER)
                if g.within(NG):
                    row = first_row(g)
                    p = g.s // GPE
                    par = g.s % 2
                    if g.s % GPE == 0:
                        pe.wait_ge(s["w_lo"], c * (2 * CH) + (CH * (g.off // GPE) + CH))
                    pe.wait_ge(s["h_lo"], g.count(4, 4))
                    with pe.If(row < N):
                        for k in range(GB):
                            need(pe, s["summed"], g.count(GB, k - 1))
                            for f in range(FT):
                                for n, (l, r) in enumerate(PASSES):
                                    last = pe.matmul(pY[:, k, :], hT[par][l][:, f, k * P:(k + 1) * P],
                                                     w2[p][r][:, f, :], start=f == 0 and n == 0,
                                                     stop=f == FT - 1 and n == 2)
                            last.then_inc(s["fc2_mm"], 1)
                    with pe.Else():
                        need(pe, s["summed"], g.count(GB))
                        pe.sem_inc(s["fc2_mm"], GB)

            pipeline(pe, step)


NAMES = ["x", "ctx_1024", "L0_xattn_Wq", "L0_xattn_bq", "L0_xattn_Wk", "L0_xattn_bk", "L0_xattn_Wv",
         "L0_xattn_bv", "L0_xattn_Wo", "L0_xattn_bo", "L0_ffn_ln1_weight", "L0_ffn_ln1_bias",
         "L0_ffn_ln2_weight", "L0_ffn_ln2_bias", "L0_ffn_qkv_weight", "L0_ffn_proj_weight",
         "L0_ffn_router_weight", "L0_ffn_moe_w1", "L0_ffn_moe_w2"]


def kernel(**inputs):
    import numpy as np
    import concourse.bacc as bacc
    from concourse.bass_utils import run_bass_kernel_spmd

    nc = bacc.Bacc("TRN2", target_bir_lowering=False, num_devices=1)
    arrays, aps = {}, {}
    for name in NAMES:
        v = np.ascontiguousarray(inputs[name])
        arrays[name + "_dram"] = v
        aps[name] = nc.dram_tensor(name + "_dram", v.shape, mybir.dt.from_np(v.dtype), kind="ExternalInput").ap()
    out = nc.dram_tensor("out_dram", (S, L, D), F32, kind="ExternalOutput").ap()
    build(nc, aps, out)
    result = run_bass_kernel_spmd(nc, [arrays], core_ids=[0])
    return result.results[0]["out_dram"]
```
